# Optimizing a Trainium2 kernel written in Bass

```python
import numpy as np
import jax
import jax.numpy as jnp

def _softmax(x, axis=-1):
    return jax.nn.softmax(x, axis=axis)

def _gelu(x):
    return jax.nn.gelu(x, approximate=True)

def _silu(x):
    return jax.nn.silu(x)

def _sigmoid(x):
    return jax.nn.sigmoid(x)

def _layernorm(x, axis=-1, eps=1e-05):
    m = jnp.mean(x, axis=axis, keepdims=True)
    v = jnp.var(x, axis=axis, keepdims=True)
    return (x - m) / jnp.sqrt(v + eps)

def _scatter_add(tgt, idx, src, axis=0):
    return tgt.at[idx].add(src)

def _segment_sum(src, seg, n):
    return jax.ops.segment_sum(src, seg, n)
kernel_name = 'mk_gnn_preln_d2_gnn_r64_05f278'

def setup_inputs(seed: int=0):
    np.random.seed(seed)
    _w = jnp.asarray

    def _rec_inputs():
        import jax
        import jax.numpy as jnp
        _gk = jax.random.key(seed)
        x = -0.0005121 + 1.001 * jax.random.normal(jax.random.fold_in(_gk, 1), (100000, 64), jnp.float32)
        src = jax.random.randint(jax.random.fold_in(_gk, 2), (50000,), 0, 100000, jnp.int32)
        dst = jax.random.randint(jax.random.fold_in(_gk, 3), (50000,), 0, 100000, jnp.int32)
        _o = jnp.argsort(dst, stable=True)
        src = src[_o]
        dst = dst[_o]
        edge_type_8 = jax.random.randint(jax.random.fold_in(_gk, 13), (50000,), 0, 8, jnp.int32)
        return (x, src, dst, edge_type_8)
    x, src, dst, edge_type_8 = _rec_inputs()

    def _L0_gnn_setup():
        import jax, jax.numpy as jnp
        import numpy as np
        N = 50000
        E = 25000
        D = 64

        def _gcn_norm(edge_index, num_nodes):
            loop = jnp.arange(num_nodes, dtype=edge_index.dtype)
            src = jnp.concatenate([edge_index[0], loop])
            dst = jnp.concatenate([edge_index[1], loop])
            ones = jnp.ones(src.shape[0], jnp.float32)
            deg = jax.ops.segment_sum(ones, dst, num_segments=num_nodes)
            dis = jax.lax.rsqrt(deg)
            norm = dis[src] * dis[dst]
            return (src, dst, norm)

        def _gcn_layer(x, src, dst, norm, W, b):
            h = x @ W
            msg = h[src] * norm[:, None]
            agg = jax.ops.segment_sum(msg, dst, num_segments=x.shape[0])
            return agg + b
        key = jax.random.key(seed)
        ks = jax.random.split(key, 8)
        x = jax.random.normal(ks[0], (N, D), dtype=jnp.float32)
        edge_index = jax.random.randint(ks[1], (2, E), 0, N, dtype=jnp.int64)
        s = 1.0 / np.sqrt(D)
        W0 = jax.random.normal(ks[2], (D, D), dtype=jnp.float32) * s
        W1 = jax.random.normal(ks[3], (D, D), dtype=jnp.float32) * s
        W2 = jax.random.normal(ks[4], (D, D), dtype=jnp.float32) * s
        b0 = jnp.zeros((D,), jnp.float32)
        b1 = jnp.zeros((D,), jnp.float32)
        b2 = jnp.zeros((D,), jnp.float32)
        return {'x': x, 'edge_index': edge_index, 'W0': W0, 'b0': b0, 'W1': W1, 'b1': b1, 'W2': W2, 'b2': b2}
    _L0_gnn_all = _L0_gnn_setup()
    _L0_gnn_in = {k: v for k, v in _L0_gnn_all.items() if k in ('W0', 'b0', 'W1', 'b1', 'W2', 'b2')}
    del _L0_gnn_all

    def _L1_gnn_setup():
        import jax, jax.numpy as jnp
        import numpy as np
        C = 0.01
        EPS = 1e-06
        MIN_NORM = 1e-10
        N_NODES = 50000
        N_EDGES = 6250
        IN_FEAT = 64
        OUT_FEAT = 64
        NUM_RELS = 8
        NUM_HEADS = 4
        SQRT_C = np.sqrt(C).astype(np.float32)

        def project_to_ball(x, c=C):
            norm = jnp.maximum(jnp.linalg.norm(x, axis=-1, keepdims=True), MIN_NORM)
            maxnorm = (1.0 - 1e-05) / np.sqrt(c)
            return jnp.where(norm > maxnorm, x * (maxnorm / norm), x)

        def log_map_zero(x, c=C):
            norm = jnp.maximum(jnp.linalg.norm(x, axis=-1, keepdims=True), MIN_NORM)
            t = jnp.clip(np.sqrt(c) * norm, MIN_NORM, 1.0 - 1e-05)
            return jnp.arctanh(t) * x / t

        def exp_map_zero(v, c=C):
            norm = jnp.maximum(jnp.linalg.norm(v, axis=-1, keepdims=True), MIN_NORM)
            t = np.sqrt(c) * norm
            return jnp.tanh(t) * v / t

        def mobius_add(x, y, c=C):
            xy = jnp.sum(x * y, axis=-1, keepdims=True)
            x2 = jnp.sum(x * x, axis=-1, keepdims=True)
            y2 = jnp.sum(y * y, axis=-1, keepdims=True)
            num = (1.0 + 2.0 * c * xy + c * y2) * x + (1.0 - c * x2) * y
            den = 1.0 + 2.0 * c * xy + c ** 2 * x2 * y2
            return num / jnp.maximum(den, MIN_NORM)

        def leaky_relu(x, slope=0.2):
            return jnp.where(x > 0, x, slope * x)
        key = jax.random.key(seed)
        k1, k2, k3, k4, k5, k6, k7 = jax.random.split(key, 7)
        h = jax.random.normal(k1, (N_NODES, IN_FEAT), dtype=jnp.float32) * 0.5
        h = project_to_ball(h)
        rel_weight = jax.random.normal(k2, (NUM_RELS, NUM_HEADS, IN_FEAT, OUT_FEAT), dtype=jnp.float32) * 0.125
        attn_vec = jax.random.normal(k3, (NUM_RELS, NUM_HEADS, OUT_FEAT), dtype=jnp.float32) * 0.125
        rel_emb = jax.random.normal(k4, (NUM_RELS, IN_FEAT), dtype=jnp.float32) * 0.1
        src = jax.random.randint(k5, (N_EDGES,), 0, N_NODES, dtype=jnp.int32)
        dst = jax.random.randint(k6, (N_EDGES,), 0, N_NODES, dtype=jnp.int32)
        etype = jax.random.randint(k7, (N_EDGES,), 0, NUM_RELS, dtype=jnp.int32)
        return {'h_hyper': h, 'rel_weight': rel_weight, 'attn_vec': attn_vec, 'rel_emb': rel_emb, 'src': src, 'dst': dst, 'etype': etype}
    _L1_gnn_all = _L1_gnn_setup()
    _L1_gnn_in = {k: v for k, v in _L1_gnn_all.items() if k in ('rel_weight', 'attn_vec', 'rel_emb')}
    del _L1_gnn_all
    return {'x': x, 'src': src, 'dst': dst, 'edge_type_8': edge_type_8, 'L0_gnn_W0': _L0_gnn_in['W0'], 'L0_gnn_b0': _L0_gnn_in['b0'], 'L0_gnn_W1': _L0_gnn_in['W1'], 'L0_gnn_b1': _L0_gnn_in['b1'], 'L0_gnn_W2': _L0_gnn_in['W2'], 'L0_gnn_b2': _L0_gnn_in['b2'], 'L1_gnn_rel_weight': _L1_gnn_in['rel_weight'], 'L1_gnn_attn_vec': _L1_gnn_in['attn_vec'], 'L1_gnn_rel_emb': _L1_gnn_in['rel_emb']}

def reference(x, src, dst, edge_type_8, L0_gnn_W0, L0_gnn_b0, L0_gnn_W1, L0_gnn_b1, L0_gnn_W2, L0_gnn_b2, L1_gnn_rel_weight, L1_gnn_attn_vec, L1_gnn_rel_emb):
    import jax
    import jax.numpy as jnp

    def _L0_gnn_ref(x, edge_index, W0, b0, W1, b1, W2, b2):
        import jax, jax.numpy as jnp
        import numpy as np
        N = 50000
        E = 25000
        D = 64

        def _gcn_norm(edge_index, num_nodes):
            loop = jnp.arange(num_nodes, dtype=edge_index.dtype)
            src = jnp.concatenate([edge_index[0], loop])
            dst = jnp.concatenate([edge_index[1], loop])
            ones = jnp.ones(src.shape[0], jnp.float32)
            deg = jax.ops.segment_sum(ones, dst, num_segments=num_nodes)
            dis = jax.lax.rsqrt(deg)
            norm = dis[src] * dis[dst]
            return (src, dst, norm)

        def _gcn_layer(x, src, dst, norm, W, b):
            h = x @ W
            msg = h[src] * norm[:, None]
            agg = jax.ops.segment_sum(msg, dst, num_segments=x.shape[0])
            return agg + b
        src, dst, norm = _gcn_norm(edge_index, x.shape[0])
        for W, b in ((W0, b0), (W1, b1), (W2, b2)):
            x = jax.nn.relu(_gcn_layer(x, src, dst, norm, W, b))
        return x

    def _L1_gnn_ref(h_hyper, rel_weight, attn_vec, rel_emb, src, dst, etype):
        import jax, jax.numpy as jnp
        import numpy as np
        C = 0.01
        EPS = 1e-06
        MIN_NORM = 1e-10
        N_NODES = 50000
        N_EDGES = 6250
        IN_FEAT = 64
        OUT_FEAT = 64
        NUM_RELS = 8
        NUM_HEADS = 4
        SQRT_C = np.sqrt(C).astype(np.float32)

        def project_to_ball(x, c=C):
            norm = jnp.maximum(jnp.linalg.norm(x, axis=-1, keepdims=True), MIN_NORM)
            maxnorm = (1.0 - 1e-05) / np.sqrt(c)
            return jnp.where(norm > maxnorm, x * (maxnorm / norm), x)

        def log_map_zero(x, c=C):
            norm = jnp.maximum(jnp.linalg.norm(x, axis=-1, keepdims=True), MIN_NORM)
            t = jnp.clip(np.sqrt(c) * norm, MIN_NORM, 1.0 - 1e-05)
            return jnp.arctanh(t) * x / t

        def exp_map_zero(v, c=C):
            norm = jnp.maximum(jnp.linalg.norm(v, axis=-1, keepdims=True), MIN_NORM)
            t = np.sqrt(c) * norm
            return jnp.tanh(t) * v / t

        def mobius_add(x, y, c=C):
            xy = jnp.sum(x * y, axis=-1, keepdims=True)
            x2 = jnp.sum(x * x, axis=-1, keepdims=True)
            y2 = jnp.sum(y * y, axis=-1, keepdims=True)
            num = (1.0 + 2.0 * c * xy + c * y2) * x + (1.0 - c * x2) * y
            den = 1.0 + 2.0 * c * xy + c ** 2 * x2 * y2
            return num / jnp.maximum(den, MIN_NORM)

        def leaky_relu(x, slope=0.2):
            return jnp.where(x > 0, x, slope * x)
        E = src.shape[0]
        N = h_hyper.shape[0]
        R, H, din, dh = rel_weight.shape
        h_t = log_map_zero(h_hyper)
        h_src_t = h_t[src]
        msg_t = jnp.zeros((E, H, dh), dtype=h_hyper.dtype)
        for r in range(R):
            xr = jnp.where((etype == r)[:, None], h_src_t, 0.0)
            msg_t = msg_t + jnp.einsum('ei,hio->eho', xr, rel_weight[r])
        msg_h = exp_map_zero(msg_t)
        diff = mobius_add(h_hyper[src], -h_hyper[dst])
        diff_t = log_map_zero(diff)
        av = attn_vec[etype]
        score = leaky_relu(jnp.einsum('ed,ehd->eh', diff_t, av))
        m = jax.ops.segment_max(score, dst, num_segments=N)
        ex = jnp.exp(score - m[dst])
        denom = jax.ops.segment_sum(ex, dst, num_segments=N)
        alpha = ex / denom[dst]
        nsq = jnp.sum(msg_h * msg_h, axis=-1)
        lam = 2.0 / (1.0 - C * nsq + EPS)
        w = alpha * lam
        num = jax.ops.segment_sum(w[..., None] * msg_h, dst, num_segments=N)
        den = jax.ops.segment_sum(w, dst, num_segments=N) + EPS
        mid = project_to_ball(num / den[..., None])
        agg_t = jnp.mean(log_map_zero(mid), axis=1)
        h_new = exp_map_zero(agg_t)
        return h_new
    edge_index = jnp.stack([src, dst])
    h = jnp.maximum(_layernorm(x, axis=-1), 0.0)
    x = x + _L0_gnn_ref(h, edge_index, L0_gnn_W0, L0_gnn_b0, L0_gnn_W1, L0_gnn_b1, L0_gnn_W2, L0_gnn_b2)
    h = jnp.maximum(_layernorm(x, axis=-1), 0.0)
    x = x + _L1_gnn_ref(h, L1_gnn_rel_weight, L1_gnn_attn_vec, L1_gnn_rel_emb, src, dst, edge_type_8)
    return x

_drawn_inputs = setup_inputs


def setup_inputs(seed=0):
    import zlib

    import numpy as np

    out = dict(_drawn_inputs(seed))
    spreads = {'L0_gnn_b0': (0.0, 0.1), 'L0_gnn_b1': (0.0, 0.1), 'L0_gnn_b2': (0.0, 0.1)}
    factors = {}
    for name, (base, spread) in spreads.items():
        noise = np.random.default_rng([zlib.crc32(name.encode()), seed]).standard_normal(out[name].shape)
        drawn = base * np.exp(spread * noise) if base else spread * noise
        out[name] = jnp.asarray(drawn.astype(out[name].dtype))
    for name, factor in factors.items():
        out[name] = (out[name] * factor).astype(out[name].dtype)
    return out
```

```python
from contextlib import ExitStack

import numpy as np
import concourse.bass as bass
from concourse import mybir

F32 = mybir.dt.float32
BF16 = mybir.dt.bfloat16
I32 = mybir.dt.int32
ALU = mybir.AluOpType
ACT = mybir.ActivationFunctionType
AX = mybir.AxisListType

P = 128
N, E, D, R, H = 100000, 50000, 64, 8, 4
C = 8
EC = -(-E // P)
SC = -(-(EC + 1) // C) * C
assert SC == EC + 1
NCH = SC // C
SLOTS = P * SC
ROWS = SLOTS + N
XW = D + 4
NB = C * P
ND = -(-N // NB)
LASTP = (N - (ND - 1) * NB) // C
LOOPS = (ND - 2) // 4
assert 4 * LOOPS + 2 == ND and LASTP * C == N - (ND - 1) * NB
OUTSIDE = float(1 << 23)
MW = H * D + 2 * H
CURV, MIN_NORM, EPS = 0.01, 1e-10, 1e-6
MAXNORM = (1.0 - 1e-5) / 0.1
SQ_FLOOR = 1e-19
CHAIN = 1


def build(nc, x, src, dst, etype, w, b, rel_weight, attn_vec, out):
    with ExitStack() as ctx:
        def sb(name, shape, dt=F32):
            return ctx.enter_context(nc.sbuf_tensor(name, shape, dt))

        def psum(name, shape, dt=F32):
            return ctx.enter_context(nc.psum_tensor(name, shape, dt))

        def sem(name):
            return ctx.enter_context(nc.semaphore(name))

        def dram(name, shape):
            return nc.dram_tensor(name, shape, F32).ap()

        nodes = dram("nodes", (N, XW))
        xslot = dram("xslot", (SLOTS, XW))
        table = [None, dram("table1", (ROWS, D)), dram("table2", (ROWS, D)), dram("table3", (ROWS, D))]
        x1slot = dram("x1slot", (SLOTS, D))
        hsrc = dram("hsrc", (SLOTS, D))

        ident = sb("ident", [P, P])
        identb = sb("identb", [P, P], BF16)
        below = sb("below", [P, P])
        ones = sb("ones", [P, P])
        diag = sb("diag", [P, P])
        carrym = sb("carrym", [P, P])
        carryt = sb("carryt", [P, P])
        pen = sb("pen", [P, P])
        wblk = sb("wblk", [P, 3, P])
        bcol = sb("bcol", [P, 3])
        relw = sb("relw", [P, 4, H * D])
        avblk = sb("avblk", [P, 2 * R * H])
        epsln = sb("epsln", [P, 1])
        srci = sb("srci", [P, SC], I32)
        dsti = sb("dsti", [P, SC], I32)
        eti = sb("eti", [P, SC], I32)
        dnext = sb("dnext", [P, 1], I32)
        slotno = sb("slotno", [P, SC], I32)
        srcf = sb("srcf", [P, SC])
        dstf = sb("dstf", [P, SC])
        etf = sb("etf", [P, SC])
        dnextf = sb("dnextf", [P, 1])
        onehot = sb("onehot", [P, SC, R], BF16)
        cont = sb("cont", [P, SC])
        ends = sb("ends", [P, SC])
        head = sb("head", [P, SC])
        headend = sb("headend", [P, SC])
        owns = sb("owns", [P, SC])
        goes = sb("goes", [P, SC])
        cnt = sb("cnt", [P, SC])
        dis = sb("dis", [P, SC])
        tmp = sb("tmp", [P, SC])
        tmp2 = sb("tmp2", [P, SC])
        slotdata = sb("slotdata", [P, SC, 4])
        idx_dst = sb("idx_dst", [P, SC], I32)
        idx_map = sb("idx_map", [P, SC], I32)
        idx_out = sb("idx_out", [P, SC], I32)
        row_of_src = sb("row_of_src", [P, SC], I32)
        headsum = sb("headsum", [P, MW])
        hpart = sb("hpart", [P, MW])
        idxr = sb("idxr", [P, 2, C], I32)
        datar = sb("datar", [P, 2, C, 4])
        rows = sb("rows", [P, 2, C, XW])
        rows64 = rows[:].rearrange("p v c f -> p (v c f)")[:, 0:2 * C * D].rearrange("p (v c f) -> p v c f", v=2, f=D)
        xd = sb("xd", [P, 4, C, XW])
        lns = sb("lns", [P, 2, 2 * C, 1])
        lnc = sb("lnc", [P, 2, 2 * C, D])
        lnq = sb("lnq", [P, 2, 2 * C, D])
        lnv = sb("lnv", [P, 2, 2 * C, 1])
        lnd = sb("lnd", [P, 2, 2 * C, 1])
        lnr = sb("lnr", [P, 2, 2 * C, 1])
        h0 = sb("h0", [P, 2 * C, D])
        hT = sb("hT", [P, 4, P * 4])
        outs = sb("outs", [P, 4, 2, C, D])
        o1, o2, ox, o3 = (outs[:, n, :, :, :] for n in range(4))
        selfr = sb("selfr", [P, 2, C, XW])
        agg = sb("agg", [P, C, D])
        last = sb("last", [P, D])
        prod = sb("prod", [P, C, MW])
        dsrc = sb("dsrc", [P, C])
        small = sb("small", [P, 12, SC])

        zbuf = sb("zbuf", [P, C, D])
        hdb = sb("hdb", [P, C, D])
        hnext = sb("hnext", [P, D])
        hclose = sb("hclose", [P, D])
        score = sb("score", [P, SC, H])
        dots = sb("dots", [P, 2, SC, H])
        smax = sb("smax", [P, SC, H])
        ex4 = sb("ex4", [P, SC, H])
        edge = sb("edge", [P, H])
        masks = sb("masks", [P, 4, C * P], BF16)
        pairsel = sb("pairsel", [R, 4, P], BF16)
        xm = sb("xm", [P, C, 4 * P])
        twice = dots[:].rearrange("p a c h -> p (a c h)")[:, 0:4 * C * D].rearrange("p (v c f) -> p v c f", v=2, f=2 * D)
        ohT = smax[0:R, :, :].rearrange("p c h -> p (c h)")[:, 0:C * P // 2].bitcast(BF16)
        ohc = smax[:, :, :].rearrange("p c h -> p (c h)")[:, C * P // 2:C * P // 2 + C * R // 2].bitcast(BF16)
        rawsb = hT[:].rearrange("p a b -> p (a b)").rearrange("p (c f) -> p c f", f=H * D)
        sqb = outs[:, 2:4, :, :, :].rearrange("p n v c f -> p (n v c f)").rearrange("p (c f) -> p c f", f=H * D)
        aggm = xd[:].rearrange("p v c f -> p (v c f)")[:, 0:C * MW].rearrange("p (c f) -> p c f", f=MW)
        lastm = lnq[:, 1, :, :].rearrange("p c f -> p (c f)")[:, 0:MW]
        k4 = lnc[:, 1, :, :].rearrange("p c f -> p (c f)")[:, 0:12 * C * H].rearrange("p (n c h) -> p n c h", c=C, h=H)
        k1 = sb("k1", [P, 6, C])

        bank = [psum(f"bank{i}", [P, 512]) for i in range(8)]

        s_const = sem("constants_made")
        s_in = sem("inputs_loaded")
        s_pad = sem("pads_set")
        s_padv = sem("attention_pad_set")
        s_nodes = sem("nodes_copied")
        s_prep = sem("prep_step")
        s_prepdiag = sem("prep_operand_ready")
        s_prepact = sem("prep_sqrt")
        s_preppe = sem("prep_product")
        s_idx = sem("index_arrays_ready")
        s_turn, s_turn_sp, s_turn_dve = sem("pool_turn"), sem("sp_turn"), sem("dve_turn")
        s_idxr = sem("indices_staged")
        s_rows = [sem(f"rows_gathered{s}") for s in range(2)]
        s_xst = [sem(f"xslot_stored{s}") for s in range(2)]
        s_map = [sem(f"map_scattered{s}") for s in range(2)]

        sems_dense = {}
        for name in ("xc1", "sq1", "var1", "std1", "h0", "h0t_ps", "h0t", "z1", "h1t", "z2", "h2t", "z3",
                     "h3t", "b1", "b2", "b3", "o1", "o2", "x1", "xc2", "sq2", "var2", "std2", "o3", "step"):
            sems_dense[name] = sem("dense_" + name)
        s_xd = [sem(f"dense_x_loaded{u}") for u in range(4)]
        s_dst = [sem(f"dense_stored{v}") for v in range(2)]
        sems_layer = {}
        for name in ("xc1", "sq1", "var1", "std1", "used", "z", "t_ps", "t", "mm", "relu", "back", "u", "xc2", "sq2",
                     "var2", "std2", "o3", "step", "chain_end", "carry"):
            sems_layer[name] = sem("layer_" + name)
        s_self = [sem(f"self_rows_loaded{s}") for s in range(2)]
        s_ust = [sem(f"slots_stored{s}") for s in range(2)]
        s_map_used = sem("row_numbers_made")

        s_loc = [sem(f"attention_rows_loaded{s}") for s in range(2)]
        s_hst = [sem(f"hsrc_stored{s}") for s in range(2)]
        s_out = [sem(f"out_scattered{s}") for s in range(2)]
        sa = {}
        for name in ("step", "bulk", "chain", "hd", "sq", "ps_t", "t", "dots", "used", "seed", "seed_ps", "bulk_pe",
                     "bulk_op", "bulk_act", "bulk_ln"):
            sa[name] = sem("score_" + name)
        sm = {}
        for name in ("step", "ohc", "oh_ps", "oh", "mask_ps", "mask", "hst", "xm", "raw", "rawsb", "n2", "norm", "tanh", "agg", "aggsq", "N2",
                     "Nn", "lnt", "n2sum", "N2sum", "tanh_in", "ln", "upd", "updsq", "u2", "un", "ut", "uth", "o", "chain_end", "carry"):
            sm[name] = sem("msg_" + name)

        def slots_view(t, width=None):
            v = t[0:SLOTS, :].rearrange("(p j) f -> p j f", j=SC)
            return v if width is None else v[:, :, 0:width]

        def dense_view(t, first):
            return t[first:first + (ND - 1) * NB, :].rearrange("(k p r) f -> k p r f", p=P, r=C)

        def dense_last(t, first):
            return t[first + (ND - 1) * NB:first + N, :].rearrange("(p r) f -> p r f", r=C)

        def dense_at(t, first, k):
            if isinstance(k, int) and k == ND - 1:
                return dense_last(t, first)
            return dense_view(t, first)[bass.ds(k, 1)].rearrange("k p r f -> (k p) r f")

        class Steps:

            def __init__(self, eng, semaphore):
                self.eng, self.semaphore, self.base, self.n = eng, semaphore, 0, 0

            def __call__(self, ins):
                self.n += 1
                ins.then_inc(self.semaphore, 1)
                self.eng.wait_ge(self.semaphore, self.base + self.n)

            def restart(self, base):
                self.base, self.n = base, 0

        def bc(ap, shape):
            return ap.broadcast_to(shape)

        block = ctx.enter_context(nc.Block())
        full_rows, rest = P - 1, E - (P - 1) * EC

        def edges_view(a):
            return (a[0:full_rows * EC].rearrange("(p j) -> p j", j=EC),
                    a[full_rows * EC:E].rearrange("(p j) -> p j", p=1))

        N_IN = 0

        def used(q, i, s):
            return q * (NCH // 2 + 1 - s) + i

        def dmas(L, i, s):
            return 16 * used(L, i, s) if L < 2 else 16 * used(2, 0, s) + 32 * i

        def at_turn(L, t):
            return L * NCH + t

        def load_self(sp, L, i, s):
            t = 2 * i + s
            if L > 0 or not (isinstance(t, int) and t < 2):
                sp.wait_ge(sems_layer["u"], at_turn(L, t) - 1)
            if L == 0:
                sp.dma_start(selfr[:, s, :, :], slots_view(xslot)[:, bass.ds(t * C, C), :]).then_inc(s_self[s], 16)
            else:
                sp.dma_start(selfr[:, s, :, 0:D], slots_view(table[L])[:, bass.ds(t * C, C), :]).then_inc(s_self[s], 16)
                if L == 2:
                    sp.dma_start(xd[:, s, :, :], slots_view(xslot)[:, bass.ds(t * C, C), :]).then_inc(s_self[s], 16)

        def store_slots(sp, L, i, s):
            t = 2 * i + s
            where = slots_view(table[L + 1])[:, bass.ds(t * C, C), :]
            if L < 2:
                sp.wait_ge(sems_layer["u"], at_turn(L, t) + 1)
                sp.dma_start(where, o1[:, s, :, :]).then_inc(s_ust[s], 16)
            else:
                sp.wait_ge(sems_layer["u"], at_turn(L, t) + 1)
                sp.dma_start(slots_view(x1slot)[:, bass.ds(t * C, C), :], ox[:, s, :, :]).then_inc(s_ust[s], 16)
                sp.wait_ge(sems_layer["o3"], t + 1)
                sp.dma_start(where, o3[:, s, :, :]).then_inc(s_ust[s], 16)

        def layer_sp(sp, L):
            if L > 0:
                for s in range(2):
                    sp.wait_ge(s_ust[s], dmas(L, 0, s))
            else:
                sp.wait_ge(sems_dense["x1"], ND)
            load_self(sp, L, 0, 0)
            load_self(sp, L, 0, 1)
            with sp.Fori(0, NCH // 2 - 1) as i:
                store_slots(sp, L, i, 0)
                load_self(sp, L, i + 1, 0)
                store_slots(sp, L, i, 1)
                load_self(sp, L, i + 1, 1)
            i = NCH // 2 - 1
            store_slots(sp, L, i, 0)
            load_self(sp, L, i + 1, 0)
            store_slots(sp, L, i, 1)
            store_slots(sp, L, i + 1, 0)
            if L == 2:
                for s in range(2):
                    sp.wait_ge(s_ust[s], dmas(2, NCH // 2 + 1 - s, s))

        def attention_sp(sp):
            def load(i, s):
                k = 2 * i + s
                t = (NCH - 1) - k
                if not (isinstance(k, int) and k < 2):
                    sp.wait_ge(sa["chain"], k - 1)
                    sp.sem_inc(s_turn_sp, 1)
                sp.dma_start(selfr[:, s, :, 0:D], slots_view(table[3])[:, bass.ds(t * C, C), :]).then_inc(s_loc[s], 16)

            def store(i, s):
                t = (NCH - 1) - (2 * i + s)
                sp.wait_ge(s_rows[s], (used(4, i, s) + 1) * (16 * C))
                sp.sem_inc(s_turn_sp, 1)
                sp.dma_start(slots_view(hsrc)[:, bass.ds(t * C, C), :], rows64[:, s, :, :]).then_inc(s_hst[s], 16)

            load(0, 0)
            load(0, 1)
            with sp.Fori(0, NCH // 2 - 1) as i:
                for s in range(2):
                    store(i, s)
                    load(i + 1, s)
            i = NCH // 2 - 1
            store(i, 0)
            load(i + 1, 0)
            store(i, 1)
            store(i + 1, 0)
            for s in range(2):
                sp.wait_ge(s_hst[s], 16 * (NCH // 2 + 1 - s))
            sp.wait_ge(sa["bulk_act"], 5)

            def load_message(i, s):
                t = 2 * i + s
                if not (isinstance(t, int) and t < 2):
                    sp.wait_ge(sm["o"], t - 1)
                for half in range(2):
                    sp.dma_start(twice[:, s, :, D * half:D * half + D], slots_view(hsrc)[:, bass.ds(t * C, C), :]) \
                        .then_inc(s_loc[s], 16)
                sp.dma_start(selfr[:, s, :, 0:D], slots_view(x1slot)[:, bass.ds(t * C, C), :]).then_inc(s_loc[s], 16)

            load_message(0, 0)
            load_message(0, 1)
            with sp.Fori(1, NCH // 2) as i:
                load_message(i, 0)
                load_message(i, 1)
            load_message(NCH // 2, 0)

        def rows_loaded(i, s):
            return 16 * (NCH // 2 + 1 - s) + 48 * (i + 1)

        def attention_pool(pool, gather_pass, stage):
            for s in range(2):
                pool.wait_ge(s_ust[s], dmas(2, NCH // 2 + 1 - s, s))

            def free(i, s):
                if isinstance(i, int) and i == 0:
                    return [(sems_layer["used"], 3 * NCH)]
                return [(sa["used"], 2 * i + s - 1), (s_hst[s], 16 * i)]

            gather_pass(4, row_of_src, table[3], D, ROWS - 1, free, reverse=True, ring=rows64)
            for s in range(2):
                pool.wait_ge(s_rows[s], used(5, 0, s) * (16 * C))

            def scatter(i, s):
                k = 2 * i + s
                if not (isinstance(i, int) and i == 0):
                    pool.wait_ge(s_out[s], i * (16 * C))
                stage(idx_out, k, s)
                pool.wait_ge(sm["o"], k + 1)
                pool.wait_ge(s_idxr, 7 * NCH + k + 1)
                pool.sem_inc(s_turn, 1)
                for c in range(C):
                    pool.indirect_dma_start(out=out[:, :],
                                            out_offset=bass.IndirectOffsetOnAxis(ap=idxr[:, s, c:c + 1], axis=0),
                                            in_=o1[:, s, c, :], in_offset=None, bounds_check=N - 1,
                                            oob_is_err=False).then_inc(s_out[s], 16)

            scatter(0, 0)
            scatter(0, 1)
            with pool.Fori(1, NCH // 2) as i:
                scatter(i, 0)
                scatter(i, 1)
            scatter(NCH // 2, 0)
            for s in range(2):
                pool.wait_ge(s_out[s], (NCH // 2 + 1 - s) * 16 * C)

        def score_dve(dve):
            link = Steps(dve, sa["step"])
            PER = C + 5

            def turn(i, s, k):
                t = (NCH - 1) - k
                cols = bass.ds(t * C, C)
                first = isinstance(k, int) and k == 0
                g = rows64[:, s, :, :]
                own = selfr[:, s, :, 0:D]
                dve.wait_ge(s_loc[s], 16 * (i + 1))
                dve.sem_inc(s_turn_dve, 1)
                if first:
                    nc.vector.tensor_scalar(last[:], own[:, C - 1, :], owns[:, EC:SC], None, ALU.mult).then_inc(sa["seed"], 1)
                    dve.wait_ge(sa["seed_ps"], 1)
                    link(nc.vector.tensor_copy(hnext[:], bank[5][:, 0:D]))
                    link(nc.vector.tensor_scalar(edge[:, 0:1], owns[:, EC:SC], -1.0, 1.0, ALU.mult, ALU.add))
                    link(nc.vector.scalar_tensor_tensor(hclose[:], hnext[:], edge[:, 0:1], last[:], ALU.mult, ALU.add))
                ob = owns[:, cols].rearrange("p (c k) -> p c k", k=1)
                link(nc.vector.tensor_tensor(prod[:, :, 0:D], own, bc(ob, [P, C, D]), ALU.mult))
                for c in range(C):
                    ins = nc.vector.scalar_tensor_tensor(prod[:, c, 0:D], hclose[:], head[:, bass.ds(t * C + c, 1)],
                                                         prod[:, c, 0:D], ALU.mult, ALU.add)
                link(ins)
                if not first:
                    dve.wait_ge(sa["ps_t"], k)
                    dve.wait_ge(sa["sq"], k)
                columns = range(C - 2, -1, -1) if first else range(C - 1, -1, -1)
                for c in columns:
                    behind = hnext[:] if c == columns[0] else hdb[:, c + 1, :]
                    ins = nc.vector.scalar_tensor_tensor(hdb[:, c, :], behind, goes[:, bass.ds(t * C + c, 1)],
                                                         prod[:, c, 0:D], ALU.mult, ALU.add)
                    if c > 0:
                        link(ins)
                ins.then_inc(sa["chain"], 1)
                dve.wait_ge(sa["chain"], k + 1)
                dve.wait_ge(s_rows[s], (used(4, i, s) + 1) * (16 * C))
                nc.vector.tensor_copy(hnext[:], hdb[:, 0, :])
                link(nc.vector.tensor_tensor(prod[:, :, 0:D], g, hdb[:], ALU.mult))
                nc.vector.tensor_reduce(small[:, 2, cols], prod[:, :, 0:D], AX.X, ALU.add)
                dve.wait_ge(sa["sq"], k + 1)
                nc.vector.tensor_reduce(small[:, 0:2, cols], lnq[:, 0, :, :].rearrange("p (a c) f -> p a c f", a=2), AX.X,
                                        ALU.add)
                dve.wait_ge(sa["dots"], k + 1)
                oh = onehot[:, cols, :].rearrange("p c (r k) -> p (c r) k", k=1)
                for a in range(2):
                    ins = nc.vector.tensor_tensor(prod[:, :, 64 + 32 * a:96 + 32 * a].rearrange("p c (r h) -> p c r h", h=H),
                                                  bank[2][:, 256 * a:256 * a + 256].rearrange("p (c r h) -> p c r h", r=R, h=H),
                                                  bc(onehot[:, cols, :].rearrange("p c (r k) -> p c r k", k=1), [P, C, R, H]),
                                                  ALU.mult)
                link(ins)
                for a in range(2):
                    ins = nc.vector.tensor_reduce(dots[:, a, cols, :],
                                                  prod[:, :, 64 + 32 * a:96 + 32 * a].rearrange("p c (r h) -> p c h r", h=H),
                                                  AX.X, ALU.add)
                ins.then_inc(sa["used"], 1)
                dve.wait_ge(sa["used"], k + 1)

            link.restart(0)
            dve.wait_ge(sems_layer["o3"], NCH)
            turn(0, 0, 0)
            start = link.n
            link.restart(start)
            turn(0, 1, 1)
            per = link.n
            with dve.Fori(1, NCH // 2) as i:
                for s in range(2):
                    link.restart(start + (2 * i + s - 1) * per)
                    turn(i, s, 2 * i + s)
                    assert link.n == per
            link.restart(start + (NCH - 2) * per)
            turn(NCH // 2, 0, NCH - 1)
            assert link.n == per

            link = Steps(dve, sa["bulk"])
            acts = [0]
            ops = [0]

            def ready(ins):
                ops[0] += 1
                ins.then_inc(sa["bulk_op"], 1)

            def after_act():
                acts[0] += 1
                dve.wait_ge(sa["bulk_act"], acts[0])

            a2, b2, ab = small[:, 0, :], small[:, 1, :], small[:, 2, :]
            v = [small[:, n, :] for n in range(12)]

            def log_factor(norm2, into):
                ready(nc.vector.tensor_scalar(v[9], norm2, SQ_FLOOR, None, ALU.max))
                after_act()
                link(nc.vector.tensor_scalar(v[9], v[10], CURV ** 0.5, MIN_NORM, ALU.mult, ALU.max))
                ready(nc.vector.tensor_scalar(v[9], v[9], 1.0 - 1e-5, None, ALU.min))
                after_act()
                link(nc.vector.tensor_tensor(v[10], v[10], v[11], ALU.subtract))
                link(nc.vector.reciprocal(v[11], v[9]))
                link(nc.vector.scalar_tensor_tensor(into, v[10], 0.5, v[11], ALU.mult, ALU.mult))

            log_factor(a2, small[:, 3, :])
            link(nc.vector.tensor_scalar(v[4], ab, -2.0 * CURV, 1.0, ALU.mult, ALU.add))
            link(nc.vector.tensor_tensor(v[5], a2, b2, ALU.mult))
            link(nc.vector.scalar_tensor_tensor(v[5], v[5], CURV ** 2, v[4], ALU.mult, ALU.add))
            link(nc.vector.tensor_scalar(v[5], v[5], MIN_NORM, None, ALU.max))
            link(nc.vector.reciprocal(v[6], v[5]))
            link(nc.vector.scalar_tensor_tensor(v[4], b2, CURV, v[4], ALU.mult, ALU.add))
            link(nc.vector.tensor_tensor(v[4], v[4], v[6], ALU.mult))
            link(nc.vector.tensor_scalar(v[5], a2, -CURV, 1.0, ALU.mult, ALU.add))
            link(nc.vector.tensor_tensor(v[5], v[5], v[6], ALU.mult))
            link(nc.vector.tensor_tensor(v[6], v[4], a2, ALU.mult))
            link(nc.vector.tensor_tensor(v[7], v[5], ab, ALU.mult))
            link(nc.vector.scalar_tensor_tensor(v[6], v[7], -2.0, v[6], ALU.mult, ALU.add))
            link(nc.vector.tensor_tensor(v[6], v[6], v[4], ALU.mult))
            link(nc.vector.tensor_tensor(v[7], v[5], v[5], ALU.mult))
            link(nc.vector.tensor_tensor(v[7], v[7], b2, ALU.mult))
            link(nc.vector.tensor_tensor(v[6], v[6], v[7], ALU.add))
            log_factor(v[6], v[8])
            link(nc.vector.tensor_tensor(v[4], v[4], v[8], ALU.mult))
            link(nc.vector.tensor_tensor(v[5], v[5], v[8], ALU.mult))
            f4 = bc(v[4].rearrange("p (c k) -> p c k", k=1), [P, SC, H])
            f5 = bc(v[5].rearrange("p (c k) -> p c k", k=1), [P, SC, H])
            link(nc.vector.tensor_tensor(dots[:, 0, :, :], dots[:, 0, :, :], f4, ALU.mult))
            link(nc.vector.tensor_tensor(dots[:, 1, :, :], dots[:, 1, :, :], f5, ALU.mult))
            link(nc.vector.tensor_tensor(score[:], dots[:, 0, :, :], dots[:, 1, :, :], ALU.subtract))
            link(nc.vector.scalar_tensor_tensor(score[:], score[:], 0.2, score[:], ALU.mult, ALU.max))
            BIG = 1e30
            link(nc.vector.tensor_scalar(tmp[:], cont[:], BIG, -BIG, ALU.mult, ALU.add))
            link(nc.vector.tensor_scalar(tmp2[:, 0:EC], ends[:, 0:EC], -BIG, None, ALU.mult))
            for h in range(H):
                link(nc.vector.tensor_tensor_scan(smax[:, 0:EC, h], tmp[:, 0:EC], score[:, 0:EC, h], -BIG, ALU.add,
                                                  ALU.max))
            link(nc.vector.tensor_copy(edge[:], smax[:, EC - 1, :]))
            for h in range(H):
                nc.vector.tensor_tensor_scan(dots[:, 0, 0:EC, h][:, ::-1],
                                             tmp2[:, 0:EC][:, ::-1], smax[:, 0:EC, h][:, ::-1], -BIG, ALU.add, ALU.max)
            link(nc.vector.tensor_scalar(v[9], head[:], BIG, -BIG, ALU.mult, ALU.add))
            link(nc.vector.tensor_scalar(v[10], dstf[:], dstf[:, EC - 1:EC], None, ALU.is_equal))
            link(nc.vector.tensor_scalar(v[10], v[10], BIG, -BIG, ALU.mult, ALU.add))
            for h in range(H):
                for part, value, m, mask in ((0, edge[:, h:h + 1], carryt, v[9]), (1, dots[:, 0, 0, h:h + 1], carrym, v[10])):
                    ready(nc.vector.tensor_scalar(diag[:], ident[:], value, None, ALU.mult))
                    link(nc.vector.tensor_scalar(pen[:], m[:], BIG, -BIG, ALU.mult, ALU.add))
                    acts[0] += 0
                    dve.wait_ge(sa["bulk_pe"], 2 * h + part + 1)
                    link(nc.vector.tensor_tensor(pen[:], pen[:], bank[5][:, 0:P], ALU.add))
                    link(nc.vector.tensor_reduce(hpart[:, part:part + 1], pen[:], AX.X, ALU.max))
                for part, mask in ((0, v[9]), (1, v[10])):
                    link(nc.vector.scalar_tensor_tensor(dots[:, 0, :, h], mask, hpart[:, part:part + 1], dots[:, 0, :, h],
                                                        ALU.add, ALU.max))
            ready(nc.vector.tensor_tensor(score[:, 0:EC, :], score[:, 0:EC, :], dots[:, 0, 0:EC, :], ALU.subtract))
            after_act()

        def score_act(act):
            def turn(i, s, k):
                act.wait_ge(s_rows[s], (used(4, i, s) + 1) * (16 * C))
                nc.scalar.activation(lnq[:, 0, 0:C, :], rows64[:, s, :, :], ACT.Square)
                act.wait_ge(sa["chain"], k + 1)
                nc.scalar.activation(lnq[:, 0, C:2 * C, :], hdb[:], ACT.Square).then_inc(sa["sq"], 1)
                act.wait_ge(sa["ps_t"], k + 1)
                nc.scalar.copy(hT[:, 0, :], bank[0][:])
                nc.scalar.copy(hT[:, 1, :], bank[1][:]).then_inc(sa["t"], 1)

            def turn_at(i, s):
                k = 2 * i + s
                if not (isinstance(k, int) and k == 0):
                    act.wait_ge(sa["used"], k)
                turn(i, s, k)

            turn_at(0, 0)
            turn_at(0, 1)
            with act.Fori(1, NCH // 2) as i:
                turn_at(i, 0)
                turn_at(i, 1)
            turn_at(NCH // 2, 0)
            for n in range(2):
                act.wait_ge(sa["bulk_op"], 2 * n + 1)
                nc.scalar.activation(small[:, 10, :], small[:, 9, :], ACT.Sqrt).then_inc(sa["bulk_act"], 1)
                act.wait_ge(sa["bulk_op"], 2 * n + 2)
                nc.scalar.activation(small[:, 10, :], small[:, 9, :], ACT.Ln, bias=1.0, scale=1.0).then_inc(sa["bulk_ln"], 1)
                act.wait_ge(sa["bulk_ln"], n + 1)
                nc.scalar.activation(small[:, 11, :], small[:, 9, :], ACT.Ln, bias=1.0, scale=-1.0).then_inc(sa["bulk_act"], 1)
            act.wait_ge(sa["bulk_op"], 4 + 2 * H + 1)
            nc.scalar.activation(ex4[:, 0:EC, :], score[:, 0:EC, :], ACT.Exp).then_inc(sa["bulk_act"], 1)

        def score_pe(pe):
            def turn(i, s, k):
                pe.wait_ge(s_rows[s], (used(4, i, s) + 1) * (16 * C))
                if not (isinstance(k, int) and k == 0):
                    pe.wait_ge(sa["t"], k)
                for q in range(4):
                    nc.tensor.transpose(bank[0][:, q * P:(q + 1) * P], rows64[:, s, 2 * q:2 * q + 2, :].rearrange("p c f -> p (c f)"), ident[:])
                pe.wait_ge(sa["chain"], k + 1)
                for q in range(4):
                    ins = nc.tensor.transpose(bank[1][:, q * P:(q + 1) * P],
                                              hdb[:, 2 * q:2 * q + 2, :].rearrange("p c f -> p (c f)"), ident[:])
                ins.then_inc(sa["ps_t"], 1)
                pe.wait_ge(sa["t"], k + 1)
                if not (isinstance(k, int) and k == 0):
                    pe.wait_ge(sa["used"], k)
                for a in range(2):
                    for q in range(4):
                        ins = nc.tensor.matmul(bank[2][:, 256 * a + 64 * q:256 * a + 64 * q + 64],
                                               hT[:, a, q * P:(q + 1) * P], avblk[:], start=True, stop=True)
                ins.then_inc(sa["dots"], 1)

            pe.wait_ge(sa["seed"], 1)
            nc.tensor.matmul(bank[5][:, 0:D], carryt[:], last[:], start=True, stop=True).then_inc(sa["seed_ps"], 1)
            turn(0, 0, 0)
            turn(0, 1, 1)
            with pe.Fori(1, NCH // 2) as i:
                turn(i, 0, 2 * i)
                turn(i, 1, 2 * i + 1)
            turn(NCH // 2, 0, NCH - 1)
            for n in range(2 * H):
                pe.wait_ge(sa["bulk_op"], 4 + n + 1)
                nc.tensor.matmul(bank[5][:, 0:P], ones[:], diag[:], start=True, stop=True).then_inc(sa["bulk_pe"], 1)

        def message_pe(pe):
            def mask(t):
                first = isinstance(t, int) and t == 0
                if not first:
                    pe.wait_ge(sm["mask"], 8 * t)
                pe.wait_ge(sm["ohc"], t + 1)
                bk = bank[2][:].bitcast(BF16)
                for c in range(C):
                    ins = nc.tensor.transpose(bk[0:R, c * P:(c + 1) * P],
                                              ohc[:, c * R:(c + 1) * R], identb[:])
                ins.then_inc(sm["oh_ps"], 1)
                pe.wait_ge(sm["oh"], t + 1)
                for n in range(8):
                    q, half = n // 2, n % 2
                    if n >= 2:
                        pe.wait_ge(sm["mask"], 8 * t + n - 1)
                    nc.tensor.matmul(bank[2 + half][:], pairsel[:, q, :], ohT[:, 512 * half:512 * half + 512],
                                     start=True, stop=True).then_inc(sm["mask_ps"], 1)

            def sources(i, s):
                t = 2 * i + s
                pe.wait_ge(s_loc[s], rows_loaded(i, s))
                for c in range(C):
                    n = t * C + c
                    if not (isinstance(n, int) and n < 2):
                        pe.wait_ge(sm["xm"], n - 1)
                    two = twice[:, s, c, :]
                    nc.tensor.transpose(bank[c % 2][:, 0:P], two, ident[:]).then_inc(sm["hst"], 1)

            def products(t):
                for c in range(C):
                    pe.wait_ge(sm["xm"], t * C + c + 1)
                    if c % 2 == 0 and not (isinstance(t, int) and t == 0):
                        pe.wait_ge(sm["rawsb"], (t - 1) * 4 + c // 2 + 1)
                    for q in range(4):
                        ins = nc.tensor.matmul(bank[4 + c // 2][:, 256 * (c % 2):256 * (c % 2) + 256],
                                               xm[:, c, q * P:(q + 1) * P], relw[:, q, :], start=(q == 0), stop=(q == 3))
                    if c % 2 == 1:
                        ins.then_inc(sm["raw"], 1)

            pe.wait_ge(sa["bulk_act"], 5)
            pe.wait_ge(sa["used"], NCH)
            mask(0)
            sources(0, 0)
            mask(1)
            products(0)

            def step(i, s):
                t = 2 * i + s
                sources(i + s, 1 - s)
                products(t + 1)
                if not (isinstance(t, int) and t + 2 >= NCH):
                    mask(t + 2)

            step(0, 0)
            step(0, 1)
            with pe.Fori(1, NCH // 2 - 1) as i:
                step(i, 0)
                step(i, 1)
            step(NCH // 2 - 1, 0)
            step(NCH // 2 - 1, 1)
            pe.wait_ge(sm["chain_end"], 1)
            nc.tensor.matmul(bank[0][:, 0:MW], carrym[:], lastm[:], start=True, stop=True).then_inc(sm["carry"], 1)

        def message_act(act):
            def masks_out(t):
                nc.scalar.copy(ohc.rearrange("p (c r) -> p c r", r=R), onehot[:, bass.ds(t * C, C), :]).then_inc(sm["ohc"], 1)
                act.wait_ge(sm["oh_ps"], t + 1)
                nc.scalar.copy(ohT, bank[2][:].bitcast(BF16)[0:R, :]).then_inc(sm["oh"], 1)
                if not (isinstance(t, int) and t == 0):
                    act.wait_ge(sm["xm"], t * C)
                for n in range(8):
                    q, half = n // 2, n % 2
                    act.wait_ge(sm["mask_ps"], 8 * t + n + 1)
                    nc.scalar.copy(masks[:, q, 512 * half:512 * half + 512], bank[2 + half][:]).then_inc(sm["mask"], 1)

            def raw_out(t):
                for m in range(4):
                    act.wait_ge(sm["raw"], t * 4 + m + 1)
                    if m == 0 and not (isinstance(t, int) and t == 0):
                        act.wait_ge(sm["agg"], t)
                        act.wait_ge(sm["N2"], t)
                    bk = bank[4 + m][:].rearrange("p (c f) -> p c f", f=H * D)
                    nc.scalar.activation(sqb[:, 2 * m:2 * m + 2, :], bk, ACT.Square)
                    nc.scalar.copy(rawsb[:, 2 * m:2 * m + 2, :], bk).then_inc(sm["rawsb"], 1)

            def root(wait, done, src_, dst_, t):
                act.wait_ge(sm[wait], t + 1)
                nc.scalar.activation(dst_, src_, ACT.Ln).then_inc(sm[done], 1)
                act.wait_ge(sm[done], 2 * t + 1)
                nc.scalar.activation(dst_, dst_, ACT.Exp, scale=0.5).then_inc(sm[done], 1)

            def post(t):
                root("n2", "norm", k4[:, 0, :, :], k4[:, 1, :, :], t)
                act.wait_ge(sm["tanh_in"], t + 1)
                nc.scalar.activation(k4[:, 2, :, :], k4[:, 3, :, :], ACT.Tanh).then_inc(sm["tanh"], 1)
                act.wait_ge(sm["agg"], t + 1)
                nc.scalar.activation(sqb[:], aggm[:, :, 0:H * D], ACT.Square).then_inc(sm["aggsq"], 1)
                root("N2", "Nn", k4[:, 0, :, :], k4[:, 1, :, :], t)
                act.wait_ge(sm["lnt"], t + 1)
                nc.scalar.activation(k4[:, 4, :, :], k4[:, 3, :, :], ACT.Ln, bias=1.0, scale=1.0)
                nc.scalar.activation(k4[:, 5, :, :], k4[:, 3, :, :], ACT.Ln, bias=1.0, scale=-1.0).then_inc(sm["ln"], 1)
                act.wait_ge(sm["upd"], t + 1)
                nc.scalar.activation(lnq[:, 0, 0:C, :], lnc[:, 0, 0:C, :], ACT.Square).then_inc(sm["updsq"], 1)
                root("u2", "un", k1[:, 0, :], k1[:, 1, :], t)
                act.wait_ge(sm["ut"], t + 1)
                nc.scalar.activation(k1[:, 3, :], k1[:, 2, :], ACT.Tanh).then_inc(sm["uth"], 1)

            masks_out(0)
            masks_out(1)
            raw_out(0)

            def step(t):
                post(t)
                if not (isinstance(t, int) and t + 2 >= NCH):
                    masks_out(t + 2)
                if not (isinstance(t, int) and t + 1 >= NCH):
                    raw_out(t + 1)

            with act.Fori(0, NCH - 2) as t:
                step(t)
            step(NCH - 2)
            step(NCH - 1)

        def message_dve(dve):
            link = Steps(dve, sm["step"])

            def masked(t):
                for c in range(C):
                    n = t * C + c
                    dve.wait_ge(sm["hst"], n + 1)
                    dve.wait_ge(sm["mask"], 8 * t + 8)
                    if c == 0 and not (isinstance(t, int) and t == 0):
                        dve.wait_ge(sm["raw"], t * 4)
                    nc.vector.tensor_tensor(xm[:, c, :].rearrange("p (q e) -> p q e", q=4),
                                            bc(bank[c % 2][:, 0:P].rearrange("p (k e) -> p k e", k=1), [P, 4, P]),
                                            masks[:, :, c * P:(c + 1) * P], ALU.mult).then_inc(sm["xm"], 1)

            def q4(n):
                return k4[:, n, :, :]

            def factor(t):
                return bc(small[:, 3, bass.ds(t * C, C)].rearrange("p (c k) -> p c k", k=1), [P, C, H])

            def post(i, s, t, first=False, last_chunk=False):
                ext = ex4[:, bass.ds(t * C, C), :]
                dve.wait_ge(sm["rawsb"], t * 4 + 4)
                nc.vector.tensor_reduce(q4(6).rearrange("p c h -> p (c h)"), sqb[:].rearrange("p c (h o) -> p (c h) o", o=D),
                                        AX.X, ALU.add).then_inc(sm["n2sum"], 1)
                dve.wait_ge(sm["n2sum"], t + 1)
                nc.vector.tensor_scalar(q4(0), q4(6), SQ_FLOOR, None, ALU.max).then_inc(sm["n2"], 1)
                dve.wait_ge(sm["norm"], 2 * t + 2)
                link(nc.vector.tensor_tensor(q4(3), q4(1), factor(t), ALU.mult))
                nc.vector.tensor_scalar(q4(3), q4(3), MIN_NORM, CURV ** 0.5, ALU.max, ALU.mult).then_inc(sm["tanh_in"], 1)
                dve.wait_ge(sm["tanh"], t + 1)
                link(nc.vector.tensor_tensor(q4(4), q4(2), q4(2), ALU.mult))
                link(nc.vector.tensor_scalar(q4(4), q4(4), -1.0, 1.0, ALU.mult, ALU.add))
                link(nc.vector.tensor_scalar(q4(4), q4(4), EPS, None, ALU.add))
                link(nc.vector.tensor_tensor(q4(4), q4(4), q4(3), ALU.mult))
                link(nc.vector.reciprocal(q4(5), q4(4)))
                link(nc.vector.scalar_tensor_tensor(q4(5), q4(5), 2.0, ext, ALU.mult, ALU.mult))
                nc.vector.tensor_tensor(prod[:, :, H * D:H * D + H], q4(5), q4(3), ALU.mult)
                nc.vector.tensor_copy(prod[:, :, H * D + H:MW], ext)
                link(nc.vector.tensor_tensor(q4(6), q4(5), q4(2), ALU.mult))
                link(nc.vector.tensor_tensor(q4(6), q4(6), factor(t), ALU.mult))
                link(nc.vector.tensor_tensor(prod[:, :, 0:H * D].rearrange("p c (h o) -> p c h o", o=D),
                                             rawsb[:].rearrange("p c (h o) -> p c h o", o=D),
                                             bc(q4(6).rearrange("p c (h k) -> p c h k", k=1), [P, C, H, D]), ALU.mult))
                m = C - 1 if last_chunk else C
                for c in range(m):
                    if c == 0 and first:
                        link(nc.vector.tensor_copy(aggm[:, 0, :], prod[:, 0, :]))
                        continue
                    before = lastm[:] if c == 0 else aggm[:, c - 1, :]
                    link(nc.vector.scalar_tensor_tensor(aggm[:, c, :], before, cont[:, bass.ds(t * C + c, 1)], prod[:, c, :],
                                                        ALU.mult, ALU.add))
                hb = headend[:, bass.ds(t * C, m)].rearrange("p (c k) -> p c k", k=1)
                link(nc.vector.tensor_tensor(prod[:, 0:m, :], aggm[:, 0:m, :], bc(hb, [P, m, MW]), ALU.mult))
                target = headsum if first else hpart
                link(nc.vector.tensor_reduce(target[:], prod[:, 0:m, :].rearrange("p c f -> p f c"), AX.X, ALU.add))
                if not first:
                    link(nc.vector.tensor_tensor(headsum[:], headsum[:], hpart[:], ALU.add))
                if last_chunk:
                    nc.vector.tensor_copy(lastm[:], aggm[:, C - 2, :]).then_inc(sm["chain_end"], 1)
                    dve.wait_ge(sm["carry"], 1)
                    nc.vector.tensor_tensor(aggm[:, C - 1, :], headsum[:], bank[0][:, 0:MW], ALU.add).then_inc(sm["agg"], 1)
                else:
                    nc.vector.tensor_copy(lastm[:], aggm[:, C - 1, :]).then_inc(sm["agg"], 1)
                dve.wait_ge(sm["aggsq"], t + 1)
                nc.vector.tensor_reduce(q4(6).rearrange("p c h -> p (c h)"), sqb[:].rearrange("p c (h o) -> p (c h) o", o=D),
                                        AX.X, ALU.add).then_inc(sm["N2sum"], 1)
                dve.wait_ge(sm["N2sum"], t + 1)
                nc.vector.tensor_scalar(q4(0), q4(6), SQ_FLOOR, None, ALU.max).then_inc(sm["N2"], 1)
                wsum, esum = aggm[:, :, H * D:H * D + H], aggm[:, :, H * D + H:MW]
                link(nc.vector.scalar_tensor_tensor(q4(7), esum, EPS, wsum, ALU.mult, ALU.add))
                link(nc.vector.tensor_scalar(q4(7), q4(7), 1e-30, None, ALU.max))
                link(nc.vector.reciprocal(q4(8), q4(7)))
                dve.wait_ge(sm["Nn"], 2 * t + 2)
                link(nc.vector.tensor_tensor(q4(9), q4(1), q4(8), ALU.mult))
                link(nc.vector.tensor_scalar(q4(9), q4(9), MIN_NORM, None, ALU.max))
                link(nc.vector.reciprocal(q4(10), q4(9)))
                link(nc.vector.tensor_scalar(q4(10), q4(10), MAXNORM, 1.0, ALU.mult, ALU.min))
                link(nc.vector.tensor_tensor(q4(9), q4(9), q4(10), ALU.mult))
                link(nc.vector.tensor_scalar(q4(9), q4(9), CURV ** 0.5, MIN_NORM, ALU.mult, ALU.max))
                nc.vector.tensor_scalar(q4(3), q4(9), 1.0 - 1e-5, None, ALU.min).then_inc(sm["lnt"], 1)
                dve.wait_ge(sm["ln"], t + 1)
                link(nc.vector.tensor_tensor(q4(4), q4(4), q4(5), ALU.subtract))
                link(nc.vector.reciprocal(q4(5), q4(3)))
                link(nc.vector.scalar_tensor_tensor(q4(4), q4(4), 0.5 / H, q4(5), ALU.mult, ALU.mult))
                link(nc.vector.tensor_tensor(q4(4), q4(4), q4(8), ALU.mult))
                link(nc.vector.tensor_tensor(q4(4), q4(4), q4(10), ALU.mult))
                link(nc.vector.tensor_tensor(prod[:, :, 0:H * D].rearrange("p c (h o) -> p c h o", o=D),
                                             aggm[:, :, 0:H * D].rearrange("p c (h o) -> p c h o", o=D),
                                             bc(q4(4).rearrange("p c (h k) -> p c h k", k=1), [P, C, H, D]), ALU.mult))
                nc.vector.tensor_reduce(lnc[:, 0, 0:C, :], prod[:, :, 0:H * D].rearrange("p c (h o) -> p c o h", o=D), AX.X,
                                        ALU.add).then_inc(sm["upd"], 1)
                dve.wait_ge(sm["updsq"], t + 1)
                link(nc.vector.tensor_reduce(k1[:, 4, :], lnq[:, 0, 0:C, :], AX.X, ALU.add))
                nc.vector.tensor_scalar(k1[:, 0, :], k1[:, 4, :], SQ_FLOOR, None, ALU.max).then_inc(sm["u2"], 1)
                dve.wait_ge(sm["un"], 2 * t + 2)
                nc.vector.tensor_scalar(k1[:, 2, :], k1[:, 1, :], MIN_NORM, CURV ** 0.5, ALU.max, ALU.mult).then_inc(sm["ut"], 1)
                dve.wait_ge(sm["uth"], t + 1)
                link(nc.vector.reciprocal(k1[:, 4, :], k1[:, 2, :]))
                link(nc.vector.tensor_tensor(k1[:, 5, :], k1[:, 4, :], k1[:, 3, :], ALU.mult))
                fb = bc(k1[:, 5, :].rearrange("p (c k) -> p c k", k=1), [P, C, D])
                link(nc.vector.tensor_tensor(lnc[:, 0, 0:C, :], lnc[:, 0, 0:C, :], fb, ALU.mult))
                dve.wait_ge(s_loc[s], rows_loaded(i, s))
                if not (isinstance(i, int) and i == 0):
                    dve.wait_ge(s_out[s], i * (16 * C))
                nc.vector.tensor_tensor(o1[:, s, :, :], lnc[:, 0, 0:C, :], selfr[:, s, :, 0:D], ALU.add).then_inc(sm["o"], 1)

            masked(0)
            masked(1)
            link.restart(0)
            post(0, 0, 0, first=True)
            start = link.n
            link.restart(start)
            masked(2)
            post(0, 1, 1)
            per = link.n
            with dve.Fori(1, NCH // 2) as i:
                for s in range(2):
                    t = 2 * i + s
                    link.restart(start + (t - 1) * per)
                    masked(t + 1)
                    post(i, s, t)
                    assert link.n == per
            link.restart(start + (NCH - 2) * per)
            post(NCH // 2, 0, NCH - 1, last_chunk=True)

        @block.sync
        def _(sp):
            sp.dma_start(nodes.rearrange("(a n) f -> a (n f)", a=16), x.rearrange("(a n) f -> a (n f)", a=16)) \
                .then_inc(s_nodes, 16)
            sp.wait_ge(s_pad, 5)
            for a, t in ((src, srci), (dst, dsti), (etype, eti)):
                body, tail = edges_view(a)
                sp.dma_start(t[0:full_rows, 0:EC], body).then_inc(s_in, 16)
                sp.dma_start(t[full_rows:P, 0:rest], tail).then_inc(s_in, 16)
            sp.dma_start(dnext[0:full_rows, :], dst[EC:EC + (full_rows - 1) * EC + 1:EC].rearrange("(p k) -> p k", k=1),
                         allow_slow_non_contiguous=True).then_inc(s_in, 16)
            sp.wait_ge(s_padv, 1)
            for half in range(2):
                sp.dma_start(avblk[D * half:D * half + D, R * H * half:R * H * half + R * H],
                             attn_vec.rearrange("r h d -> d (r h)"), allow_slow_non_contiguous=True).then_inc(s_in, 16)
            for r in range(R):
                sp.dma_start(relw[D * (r % 2):D * (r % 2) + D, r // 2, :].rearrange("p (h o) -> p h o", o=D),
                             rel_weight[r].rearrange("h i o -> i h o")).then_inc(s_in, 16)
            for l in range(3):
                for half in range(2):
                    q = slice(D * half, D * half + D)
                    sp.dma_start(wblk[q, l, D * half:D * half + D], w[l][:, :]).then_inc(s_in, 16)
                    sp.dma_start(bcol[q, l:l + 1], b[l].rearrange("(f k) -> f k", k=1)).then_inc(s_in, 16)

            def store_c(i, s):
                sp.wait_ge(s_rows[s], (i + 1) * (16 * C))
                sp.dma_start(slots_view(xslot)[:, bass.ds((2 * i + s) * C, C), :], rows[:, s, :, :]).then_inc(s_xst[s], 16)

            with sp.Fori(0, NCH // 2) as i:
                store_c(i, 0)
                store_c(i, 1)
            store_c(NCH // 2, 0)
            for s in range(2):
                sp.wait_ge(s_xst[s], 16 * (NCH // 2 + 1 - s))

            for L in range(3):
                layer_sp(sp, L)
            attention_sp(sp)

        @block.gpsimd
        def _(pool):
            nc.gpsimd.memset(srci[:], 0).then_inc(s_pad, 1)
            nc.gpsimd.memset(eti[:], 0).then_inc(s_pad, 1)
            nc.gpsimd.memset(dsti[:], N).then_inc(s_pad, 1)
            nc.gpsimd.memset(dnext[:], 2 * N).then_inc(s_pad, 1)
            nc.gpsimd.memset(ident[:], 0.0)
            nc.gpsimd.memset(below[:], 0.0)
            nc.gpsimd.memset(pairsel[:], 0.0)
            nc.gpsimd.iota(slotno[:], pattern=[[1, SC]], base=1, channel_multiplier=SC).then_inc(s_const, 1)
            pool.wait_ge(s_const, 1)
            nc.gpsimd.affine_select(out=ident[:], in_=ident[:], compare_op=ALU.not_equal, fill=1.0, base=0,
                                    pattern=[[-1, P]], channel_multiplier=1).then_inc(s_const, 1)
            nc.gpsimd.affine_select(out=below[:], in_=below[:], compare_op=ALU.is_ge, fill=1.0, base=0,
                                    pattern=[[-1, P]], channel_multiplier=1).then_inc(s_const, 1)
            nc.gpsimd.affine_select(out=pairsel[:].rearrange("r q (a f) -> r (q a) f", a=2),
                                    in_=pairsel[:].rearrange("r q (a f) -> r (q a) f", a=2), compare_op=ALU.not_equal,
                                    fill=1.0, base=0, pattern=[[-1, R], [0, D]], channel_multiplier=1).then_inc(s_const, 1)


            def stage(array, t, s):
                nc.gpsimd.tensor_copy(idxr[:, s, :], array[:, bass.ds(t * C, C)]).then_inc(s_idxr, 1)

            def gather(q, i, s, array, table_, width, bound, free, reverse, ring):
                k = 2 * i + s
                t = (NCH - 1) - k if reverse else k
                if q > 0 or not isinstance(i, int) or i > 0:
                    pool.wait_ge(s_rows[s], used(q, i, s) * (16 * C))
                stage(array, t, s)
                for semaphore, value in free(i, s):
                    pool.wait_ge(semaphore, value)
                pool.wait_ge(s_idxr, (q if q == 0 else q + 2) * NCH + k + 1)
                pool.sem_inc(s_turn, 1)
                for c in range(C):
                    pool.indirect_dma_start(out=ring[:, s, c, 0:width], out_offset=None, in_=table_[:, :],
                                            in_offset=bass.IndirectOffsetOnAxis(ap=idxr[:, s, c:c + 1], axis=0),
                                            bounds_check=bound, oob_is_err=False).then_inc(s_rows[s], 16)

            def gather_pass(q, array, table_, width, bound, free, reverse=False, ring=rows):
                gather(q, 0, 0, array, table_, width, bound, free, reverse, ring)
                gather(q, 0, 1, array, table_, width, bound, free, reverse, ring)
                with pool.Fori(1, NCH // 2) as i:
                    for s in range(2):
                        gather(q, i, s, array, table_, width, bound, free, reverse, ring)
                gather(q, NCH // 2, 0, array, table_, width, bound, free, reverse, ring)

            pool.wait_ge(s_idx, 1)
            gather_pass(0, idx_dst, x, XW, N - 1, lambda i, s: [] if isinstance(i, int) and i == 0 else [(s_xst[s], i * 16)])

            pool.wait_ge(s_idx, 2)
            pool.wait_ge(s_nodes, 16)
            for s in range(2):
                pool.wait_ge(s_rows[s], used(1, 0, s) * (16 * C))

            def scatter_map(i, s):
                k = 2 * i + s
                if not (isinstance(i, int) and i == 0):
                    pool.wait_ge(s_map[s], i * (16 * C))
                stage(idx_map, k, s)
                nc.gpsimd.tensor_copy(datar[:, s, :, :], slotdata[:, bass.ds(k * C, C), :]).then_inc(s_idxr, 1)
                pool.wait_ge(s_idxr, NCH + 2 * k + 2)
                pool.sem_inc(s_turn, 1)
                for c in range(C):
                    pool.indirect_dma_start(out=nodes.rearrange("n (a b) -> (n a) b", b=4),
                                            out_offset=bass.IndirectOffsetOnAxis(ap=idxr[:, s, c:c + 1], axis=0),
                                            in_=datar[:, s, c, :], in_offset=None,
                                            bounds_check=N * (XW // 4) - 1, oob_is_err=False).then_inc(s_map[s], 16)

            scatter_map(0, 0)
            scatter_map(0, 1)
            with pool.Fori(1, NCH // 2) as i:
                scatter_map(i, 0)
                scatter_map(i, 1)
            scatter_map(NCH // 2, 0)
            for s in range(2):
                pool.wait_ge(s_map[s], (NCH // 2 + 1 - s) * 16 * C)

            for L in range(3):
                if L == 0:
                    for s in range(2):
                        pool.wait_ge(s_xst[s], 16 * (NCH // 2 + 1 - s))
                else:
                    if L == 1:
                        pool.wait_ge(s_map_used, NCH)
                        for v in range(2):
                            pool.wait_ge(s_dst[v], 64 * (ND // 2))
                    for s in range(2):
                        pool.wait_ge(s_ust[s], dmas(L, 0, s))

                def free(i, s, L=L):
                    k = 2 * i + s
                    if L == 0 and isinstance(i, int) and i == 0:
                        return []
                    return [(sems_layer["used"], at_turn(L, k) - 1)]

                if L == 0:
                    gather_pass(1, srci, nodes, XW, N - 1, free)
                else:
                    gather_pass(1 + L, row_of_src, table[L], D, ROWS - 1, free)
            attention_pool(pool, gather_pass, stage)

        layer_base = [0, 0, 0, 0]
        def layer_dve(dve, L):
            sl = sems_layer
            link = Steps(dve, sl["step"])
            LX = (C + 1 + 4 if L > 0 else C + 1 + 4 + 2 + 6)
            LY = (0, 0, 2)[L]

            def x_part(i, s, first_chunk=False, last_chunk=False):
                t = 2 * i + s
                n = at_turn(L, t)
                g = rows[:, s, :, 0:D]
                own = selfr[:, s, :, 0:D]
                cols = bass.ds(t * C, C)
                dve.wait_ge(s_rows[s], (used(1 + L, i, s) + 1) * (16 * C))
                dve.wait_ge(s_self[s], dmas(L, i + 1, s))
                if L == 0:
                    link(nc.vector.tensor_reduce(lns[:, 0, 0:C, 0], g, AX.X, ALU.add))
                    link(nc.vector.tensor_reduce(lns[:, 0, C:2 * C, 0], own, AX.X, ALU.add))
                    link(nc.vector.scalar_tensor_tensor(lnc[:, 0, 0:C, :], bc(lns[:, 0, 0:C, :], [P, C, D]), -1.0 / D, g,
                                                        ALU.mult, ALU.add))
                    nc.vector.scalar_tensor_tensor(lnc[:, 0, C:2 * C, :], bc(lns[:, 0, C:2 * C, :], [P, C, D]), -1.0 / D,
                                                   own, ALU.mult, ALU.add).then_inc(sl["xc1"], 1)
                    v = rows[:, s, :, D]
                    link(nc.vector.scalar_tensor_tensor(tmp[:, 0:C], v, 0.0, srcf[:, cols], ALU.is_equal, ALU.mult))
                    link(nc.vector.scalar_tensor_tensor(tmp[:, 0:C], tmp[:, 0:C], -1.0, v, ALU.add, ALU.add))
                    nc.vector.tensor_copy(row_of_src[:, cols], tmp[:, 0:C]).then_inc(s_map_used, 1)
                    dve.wait_ge(sl["sq1"], t + 1)
                    nc.vector.tensor_reduce(lnv[:, 0, :, 0], lnq[:, 0, :, :], AX.X, ALU.add).then_inc(sl["var1"], 1)
                    dve.wait_ge(sl["std1"], t + 1)
                    link(nc.vector.reciprocal(lnr[:, 0, :, 0], lnd[:, 0, :, 0]))
                    link(nc.vector.scalar_tensor_tensor(lnr[:, 0, 0:C, 0], rows[:, s, :, D + 1], 1.0, lnr[:, 0, 0:C, 0],
                                                        ALU.add, ALU.mult))
                    link(nc.vector.tensor_tensor(lnr[:, 0, C:2 * C, 0], dis[:, cols], lnr[:, 0, C:2 * C, 0], ALU.mult))
                    link(nc.vector.scalar_tensor_tensor(h0[:, :, :], lnc[:, 0, :, :], 0.0,
                                                        bc(lnr[:, 0, :, :], [P, 2 * C, D]), ALU.max, ALU.mult))
                    g, own = h0[:, 0:C, :], h0[:, C:2 * C, :]
                for c in range(C - 1 if last_chunk else C):
                    before = last[:] if c == 0 else agg[:, c - 1, :]
                    if c == 0 and first_chunk:
                        link(nc.vector.tensor_copy(agg[:, 0, :], g[:, 0, :]))
                        continue
                    link(nc.vector.scalar_tensor_tensor(agg[:, c, :], before, cont[:, bass.ds(t * C + c, 1)], g[:, c, :],
                                                        ALU.mult, ALU.add))
                m = C - 1 if last_chunk else C
                hb = headend[:, bass.ds(t * C, m)].rearrange("p (c k) -> p c k", k=1)
                link(nc.vector.tensor_tensor(prod[:, 0:m, 0:D], agg[:, 0:m, :], bc(hb, [P, m, D]), ALU.mult))
                if first_chunk:
                    link(nc.vector.tensor_reduce(headsum[:, 0:D], prod[:, 0:m, 0:D].rearrange("p c f -> p f c"), AX.X,
                                                 ALU.add))
                else:
                    link(nc.vector.tensor_reduce(hpart[:, 0:D], prod[:, 0:m, 0:D].rearrange("p c f -> p f c"), AX.X,
                                                 ALU.add))
                    link(nc.vector.tensor_tensor(headsum[:, 0:D], headsum[:, 0:D], hpart[:, 0:D], ALU.add))
                if last_chunk:
                    nc.vector.tensor_copy(last[:], agg[:, C - 2, :]).then_inc(sl["chain_end"], 1)
                    dve.wait_ge(sl["carry"], L + 1)
                    link(nc.vector.tensor_tensor(agg[:, C - 1, :], headsum[:, 0:D], bank[5][:, 0:D], ALU.add))
                else:
                    link(nc.vector.tensor_copy(last[:], agg[:, C - 1, :]))
                nc.vector.tensor_tensor(agg[:], agg[:], own, ALU.add).then_inc(sl["used"], 1)
                dve.wait_ge(sl["used"], n + 1)
                if L > 0 or not (isinstance(t, int) and t == 0):
                    dve.wait_ge(sl["t_ps"], n)
                db = dis[:, cols].rearrange("p (c k) -> p c k", k=1)
                nc.vector.tensor_tensor(zbuf[:], agg[:], bc(db, [P, C, D]), ALU.mult).then_inc(sl["z"], 1)
                dve.wait_ge(sl["z"], n + 1)

            def y_part(i, s):
                t = 2 * i + s
                n = at_turn(L, t)
                cols = bass.ds(t * C, C)
                back = bank[4][:].rearrange("p (c f) -> p c f", f=D)
                dve.wait_ge(sl["back"], n + 1)
                if L > 0:
                    dve.wait_ge(s_ust[s], dmas(L, i, s))
                elif not (isinstance(i, int) and i == 0):
                    dve.wait_ge(s_ust[s], dmas(L, i, s))
                if L < 2:
                    db = dis[:, cols].rearrange("p (c k) -> p c k", k=1)
                    nc.vector.tensor_tensor(o1[:, s, :, :], back, bc(db, [P, C, D]), ALU.mult).then_inc(sl["u"], 1)
                    return
                nc.vector.tensor_tensor(ox[:, s, :, :], back, xd[:, s, :, 0:D], ALU.add).then_inc(sl["u"], 1)
                dve.wait_ge(sl["u"], n + 1)
                link(nc.vector.tensor_reduce(lns[:, 1, 0:C, 0], ox[:, s, :, :], AX.X, ALU.add))
                nc.vector.scalar_tensor_tensor(lnc[:, 1, 0:C, :], bc(lns[:, 1, 0:C, :], [P, C, D]), -1.0 / D,
                                               ox[:, s, :, :], ALU.mult, ALU.add).then_inc(sl["xc2"], 1)
                dve.wait_ge(sl["sq2"], t + 1)
                nc.vector.tensor_reduce(lnv[:, 1, 0:C, 0], lnq[:, 1, 0:C, :], AX.X, ALU.add).then_inc(sl["var2"], 1)
                dve.wait_ge(sl["std2"], t + 1)
                link(nc.vector.reciprocal(lnr[:, 1, 0:C, 0], lnd[:, 1, 0:C, 0]))
                nc.vector.scalar_tensor_tensor(o3[:, s, :, :], lnc[:, 1, 0:C, :], 0.0, bc(lnr[:, 1, 0:C, :], [P, C, D]),
                                               ALU.max, ALU.mult).then_inc(sl["o3"], 1)

            ln0 = 9 if L == 0 else 0
            xs = ln0 + C + 4
            first, lastn = ln0 + C + 3, ln0 + C + 3
            per = xs + LY
            base = layer_base[L]

            def step(i, s, last_chunk=False):
                t = 2 * i + s
                link.restart(base + first + t * per)
                if s == 0:
                    x_part(i, 1, last_chunk=last_chunk)
                else:
                    x_part(i + 1, 0, last_chunk=last_chunk)
                assert link.n == (lastn if last_chunk else xs), (L, link.n, xs, lastn)
                y_part(i, s)

            link.restart(base)
            x_part(0, 0, first_chunk=True)
            assert link.n == first, (link.n, first)
            step(0, 0)
            step(0, 1)
            with dve.Fori(1, NCH // 2 - 1) as i:
                step(i, 0)
                step(i, 1)
            i = NCH // 2 - 1
            step(i, 0)
            step(i, 1, last_chunk=True)
            link.restart(base + first + (NCH - 2) * per + lastn + LY)
            y_part(NCH // 2, 0)
            layer_base[L + 1] = base + first + (NCH - 2) * per + lastn + LY + LY

        prep_counts = {}

        def link_small(dve):
            return Steps(dve, s_prep)

        def prep_dve(dve):
            link = link_small(dve)
            nc.vector.memset(wblk[:], 0.0).then_inc(s_pad, 1)
            nc.vector.memset(avblk[:], 0.0).then_inc(s_padv, 1)
            nc.vector.memset(ones[:], 1.0)
            nc.vector.memset(ex4[:], 0.0)
            nc.vector.memset(hdb[:], 0.0)
            nc.vector.memset(score[:], 0.0)
            nc.vector.memset(epsln[:], 1e-5)
            nc.vector.memset(head[:], 0.0)
            nc.vector.memset(slotdata[:], 0.0)
            link(nc.vector.memset(cont[:], 0.0))
            dve.wait_ge(s_in, 16 * (6 + 1 + 2 + R + 12))
            dve.wait_ge(s_const, 4)
            nc.vector.tensor_copy(dstf[:], dsti[:])
            nc.vector.tensor_copy(srcf[:], srci[:])
            nc.vector.tensor_copy(etf[:], eti[:])
            nc.vector.tensor_copy(identb[:], ident[:])
            link(nc.vector.tensor_copy(dnextf[:], dnext[:]))
            link(nc.vector.tensor_copy(dstf[:, EC:SC], dstf[:, 0:1]))
            link(nc.vector.tensor_scalar(tmp[:], dstf[:], float(N - 1), None, ALU.min))
            nc.vector.tensor_copy(idx_dst[:], tmp[:]).then_inc(s_idx, 1)
            dve.wait_ge(s_idx, 1)
            nc.vector.tensor_tensor(cont[:, 1:EC], dstf[:, 1:EC], dstf[:, 0:EC - 1], ALU.is_equal)
            nc.vector.tensor_tensor(ends[:, 0:EC - 1], dstf[:, 1:EC], dstf[:, 0:EC - 1], ALU.not_equal)
            link(nc.vector.tensor_tensor(ends[:, EC - 1:EC], dstf[:, EC - 1:EC], dnextf[:], ALU.not_equal))
            link(nc.vector.tensor_scalar(head[:, 0:EC], dstf[:, 0:EC], dstf[:, 0:1], None, ALU.is_equal))
            link(nc.vector.tensor_tensor(headend[:, 0:EC], head[:, 0:EC], ends[:, 0:EC], ALU.mult))
            link(nc.vector.tensor_tensor(owns[:, 0:EC], ends[:, 0:EC], headend[:, 0:EC], ALU.subtract))
            link(nc.vector.tensor_reduce(owns[:, EC:SC], headend[:, 0:EC], AX.X, ALU.max))
            nc.vector.memset(headend[:, EC:SC], 0.0)
            link(nc.vector.tensor_scalar(tmp[:, 0:EC], ends[:, 0:EC], -1.0, 1.0, ALU.mult, ALU.add))
            link(nc.vector.tensor_scalar(tmp2[:, 0:EC], head[:, 0:EC], -1.0, 1.0, ALU.mult, ALU.add))
            link(nc.vector.memset(goes[:], 0.0))
            link(nc.vector.tensor_tensor(goes[:, 0:EC], tmp[:, 0:EC], tmp2[:, 0:EC], ALU.mult))
            link(nc.vector.tensor_scalar(diag[:], ident[:], dstf[:, 0:1], None, ALU.mult))
            nc.vector.tensor_scalar(tmp2[:, 0:1], dstf[:, EC - 1:EC], 1.0, None, ALU.mult).then_inc(s_prepdiag, 1)
            dve.wait_ge(s_prepdiag, 1)
            dve.wait_ge(s_preppe, 1)
            link(nc.vector.tensor_scalar(carrym[:], bank[0][:, 0:P], dstf[:, EC - 1:EC], None, ALU.is_equal))
            link(nc.vector.tensor_tensor(carrym[:], carrym[:], below[:], ALU.mult))
            nc.vector.memset(tmp[:], 1.0).then_inc(s_prepdiag, 1)
            dve.wait_ge(s_prepdiag, 2)
            dve.wait_ge(s_preppe, 2)
            link(nc.vector.tensor_copy(carryt[:], bank[1][:, 0:P]))
            link(nc.vector.tensor_tensor_scan(cnt[:, 0:EC], cont[:, 0:EC], tmp[:, 0:EC], 0.0, ALU.mult, ALU.add))
            link(nc.vector.tensor_tensor(tmp2[:, 0:EC], headend[:, 0:EC], cnt[:, 0:EC], ALU.mult))
            link(nc.vector.tensor_reduce(cnt[:, EC:SC], tmp2[:, 0:EC], AX.X, ALU.add))
            nc.vector.tensor_scalar(tmp2[:, 0:1], cnt[:, EC - 1:EC], 1.0, None, ALU.mult).then_inc(s_prepdiag, 1)
            dve.wait_ge(s_prepdiag, 3)
            dve.wait_ge(s_preppe, 3)
            link(nc.vector.tensor_tensor(cnt[:, EC:SC], cnt[:, EC:SC], bank[0][:, P:P + 1], ALU.add))
            nc.vector.tensor_scalar(tmp[:], cnt[:], 1.0, None, ALU.add).then_inc(s_prepdiag, 1)
            dve.wait_ge(s_prepact, 1)
            link(nc.vector.reciprocal(dis[:], tmp2[:]))
            nc.vector.tensor_copy(slotdata[:, :, 0], slotno[:])
            link(nc.vector.tensor_scalar(slotdata[:, :, 1], dis[:], -1.0, None, ALU.add))
            link(nc.vector.tensor_scalar(tmp[:], dstf[:], float(XW // 4), float(D // 4) - OUTSIDE, ALU.mult, ALU.add))
            link(nc.vector.tensor_tensor(tmp[:], tmp[:], owns[:], ALU.mult))
            link(nc.vector.tensor_scalar(idx_map[:], tmp[:], OUTSIDE, None, ALU.add))
            link(nc.vector.scalar_tensor_tensor(tmp[:], dstf[:], -OUTSIDE, owns[:], ALU.add, ALU.mult))
            nc.vector.tensor_scalar(idx_out[:], tmp[:], OUTSIDE, None, ALU.add).then_inc(s_idx, 1)
            for r in range(R):
                nc.vector.tensor_scalar(onehot[:, :, r], etf[:], float(r), None, ALU.is_equal)
            link(nc.vector.tensor_scalar(srcf[:], srcf[:], float(SLOTS + 1), None, ALU.add))

        @block.vector
        def _(dve):
            prep_dve(dve)
            link = Steps(dve, sems_dense["step"])
            sd = sems_dense

            def dense_c(k, u, i):
                v = u % 2
                if not (isinstance(k, int) and k < 2):
                    dve.wait_ge(s_dst[v], (2 * i + u // 2) * 64)
                dve.wait_ge(sd["b1"], k + 1)
                nc.vector.tensor_copy(o1[:, v, :, :], bank[2][:].rearrange("p (c f) -> p c f", f=D)).then_inc(sd["o1"], 1)
                dve.wait_ge(sd["b3"], k + 1)
                nc.vector.tensor_tensor(ox[:, v, :, :], bank[4][:].rearrange("p (c f) -> p c f", f=D),
                                        xd[:, u, :, 0:D], ALU.add).then_inc(sd["x1"], 1)
                dve.wait_ge(sd["x1"], k + 1)
                link(nc.vector.tensor_reduce(lns[:, 1, 0:C, 0], ox[:, v, :, :], AX.X, ALU.add))
                nc.vector.scalar_tensor_tensor(lnc[:, 1, 0:C, :], bc(lns[:, 1, 0:C, :], [P, C, D]), -1.0 / D,
                                               ox[:, v, :, :], ALU.mult, ALU.add).then_inc(sd["xc2"], 1)
                dve.wait_ge(sd["sq2"], k + 1)
                nc.vector.tensor_reduce(lnv[:, 1, 0:C, 0], lnq[:, 1, 0:C, :], AX.X, ALU.add).then_inc(sd["var2"], 1)
                dve.wait_ge(sd["std2"], k + 1)
                link(nc.vector.reciprocal(lnr[:, 1, 0:C, 0], lnd[:, 1, 0:C, 0]))
                nc.vector.scalar_tensor_tensor(o3[:, v, :, :], lnc[:, 1, 0:C, :], 0.0, bc(lnr[:, 1, 0:C, :], [P, C, D]),
                                               ALU.max, ALU.mult).then_inc(sd["o3"], 1)

            PER = 4

            def dense_step(i, u):
                k = 4 * i + u
                link.restart(2 + k * PER)
                if not (isinstance(k, int) and k == ND - 1):
                    dense_a(i + (u + 1) // 4, (u + 1) % 4)
                dense_c(k, u, i)
                assert link.n == (PER if not (isinstance(k, int) and k == ND - 1) else 2)

            def dense_a(i, u):
                k = 4 * i + u
                xk = xd[:, u, :, 0:D]
                dve.wait_ge(s_xd[u], (i + 1) * 16)
                link(nc.vector.tensor_reduce(lns[:, 0, 0:C, 0], xk, AX.X, ALU.add))
                nc.vector.scalar_tensor_tensor(lnc[:, 0, 0:C, :], bc(lns[:, 0, 0:C, :], [P, C, D]), -1.0 / D, xk,
                                               ALU.mult, ALU.add).then_inc(sd["xc1"], 1)
                dve.wait_ge(sd["sq1"], k + 1)
                nc.vector.tensor_reduce(lnv[:, 0, 0:C, 0], lnq[:, 0, 0:C, :], AX.X, ALU.add).then_inc(sd["var1"], 1)
                dve.wait_ge(sd["std1"], k + 1)
                link(nc.vector.reciprocal(lnr[:, 0, 0:C, 0], lnd[:, 0, 0:C, 0]))
                if not (isinstance(k, int) and k == 0):
                    dve.wait_ge(sd["h0t_ps"], k)
                nc.vector.scalar_tensor_tensor(h0[:, 0:C, :], lnc[:, 0, 0:C, :], 0.0, bc(lnr[:, 0, 0:C, :], [P, C, D]),
                                               ALU.max, ALU.mult).then_inc(sd["h0"], 1)

            link.restart(0)
            dense_a(0, 0)
            for u in range(4):
                dense_step(0, u)
            with dve.Fori(1, LOOPS) as i:
                for u in range(4):
                    dense_step(i, u)
            dense_step(LOOPS, 0)
            dense_step(LOOPS, 1)
            for v in range(2):
                dve.wait_ge(s_dst[v], 64 * (ND // 2))
            for L in range(3):
                layer_dve(dve, L)
            score_dve(dve)
            message_dve(dve)

        @block.scalar
        def _(act):
            act.wait_ge(s_prepdiag, 4)
            nc.scalar.activation(tmp2[:], tmp[:], ACT.Sqrt).then_inc(s_prepact, 1)
            sd = sems_dense

            def load(i, u):
                act.dma_start(xd[0:(LASTP if isinstance(i, int) and 4 * i + u == ND - 1 else P), u, :, :],
                              dense_at(x, 0, 4 * i + u)).then_inc(s_xd[u], 16)

            def acts_a(k):
                act.wait_ge(sd["xc1"], k + 1)
                nc.scalar.activation(lnq[:, 0, 0:C, :], lnc[:, 0, 0:C, :], ACT.Square).then_inc(sd["sq1"], 1)
                act.wait_ge(sd["var1"], k + 1)
                nc.scalar.activation(lnd[:, 0, 0:C, 0], lnv[:, 0, 0:C, 0], ACT.Sqrt, bias=epsln[:], scale=1.0 / D) \
                    .then_inc(sd["std1"], 1)

            def acts_b(k):
                act.wait_ge(sd["h0t_ps"], k + 1)
                nc.scalar.copy(hT[:, 0, :], bank[0][:]).then_inc(sd["h0t"], 1)
                for l, (z, h) in enumerate((("z1", "h1t"), ("z2", "h2t"), ("z3", "h3t"))):
                    act.wait_ge(sd[z], k + 1)
                    nc.scalar.activation(hT[:, l + 1, :], bank[1][:], ACT.Relu, bias=bcol[:, l:l + 1]).then_inc(sd[h], 1)

            def acts_c(k, u, i):
                v = u % 2
                act.wait_ge(sd["b2"], k + 1)
                if not (isinstance(k, int) and k < 2):
                    act.wait_ge(s_dst[v], (2 * i + u // 2) * 64)
                nc.scalar.copy(o2[:, v, :, :], bank[3][:].rearrange("p (c f) -> p c f", f=D)).then_inc(sd["o2"], 1)
                act.wait_ge(sd["xc2"], k + 1)
                nc.scalar.activation(lnq[:, 1, 0:C, :], lnc[:, 1, 0:C, :], ACT.Square).then_inc(sd["sq2"], 1)
                act.wait_ge(sd["var2"], k + 1)
                nc.scalar.activation(lnd[:, 1, 0:C, 0], lnv[:, 1, 0:C, 0], ACT.Sqrt, bias=epsln[:], scale=1.0 / D) \
                    .then_inc(sd["std2"], 1)

            def store(k, u):
                v = u % 2
                pp = LASTP if isinstance(k, int) and k == ND - 1 else P
                act.wait_ge(sd["o1"], k + 1)
                act.wait_ge(sd["o2"], k + 1)
                act.wait_ge(sd["o3"], k + 1)
                for tgt, base, o in ((table[1], SLOTS, o1), (table[2], SLOTS, o2), (table[3], SLOTS, o3), (out, 0, ox)):
                    act.dma_start(dense_at(tgt, base, k), o[0:pp, v, :, :]).then_inc(s_dst[v], 16)

            def step(i, u):
                k = 4 * i + u
                not_last = not (isinstance(k, int) and k == ND - 1)
                if not_last:
                    acts_a(k + 1)
                acts_c(k, u, i)
                if not_last:
                    acts_b(k + 1)
                store(k, u)
                if not (isinstance(k, int) and k + 4 >= ND):
                    load(i + 1, u)

            for u in range(4):
                load(0, u)
            acts_a(0)
            acts_b(0)
            for u in range(4):
                step(0, u)
            with act.Fori(1, LOOPS - 1) as i:
                for u in range(4):
                    step(i, u)
            for k in range(4 * (LOOPS - 1), ND):
                step(k // 4, k % 4)

            sl = sems_layer
            for L in range(3):
                def layer_acts_x(t):
                    if L == 0:
                        act.wait_ge(sl["xc1"], t + 1)
                        nc.scalar.activation(lnq[:, 0, :, :], lnc[:, 0, :, :], ACT.Square).then_inc(sl["sq1"], 1)
                        act.wait_ge(sl["var1"], t + 1)
                        nc.scalar.activation(lnd[:, 0, :, 0], lnv[:, 0, :, 0], ACT.Sqrt, bias=epsln[:], scale=1.0 / D) \
                            .then_inc(sl["std1"], 1)

                def layer_acts_b(t):
                    n = at_turn(L, t)
                    act.wait_ge(sl["t_ps"], n + 1)
                    nc.scalar.copy(hT[:, 0, :], bank[0][:]).then_inc(sl["t"], 1)
                    act.wait_ge(sl["mm"], n + 1)
                    nc.scalar.activation(hT[:, 1, :], bank[1][:], ACT.Relu, bias=bcol[:, L:L + 1]).then_inc(sl["relu"], 1)

                def layer_acts_y(t):
                    if L == 2:
                        act.wait_ge(sl["xc2"], t + 1)
                        nc.scalar.activation(lnq[:, 1, 0:C, :], lnc[:, 1, 0:C, :], ACT.Square).then_inc(sl["sq2"], 1)
                        act.wait_ge(sl["var2"], t + 1)
                        nc.scalar.activation(lnd[:, 1, 0:C, 0], lnv[:, 1, 0:C, 0], ACT.Sqrt, bias=epsln[:],
                                             scale=1.0 / D).then_inc(sl["std2"], 1)

                def layer_step(t):
                    layer_acts_x(t + 1)
                    layer_acts_y(t)
                    layer_acts_b(t + 1)

                layer_acts_x(0)
                layer_acts_b(0)
                with act.Fori(0, NCH - 1) as t:
                    layer_step(t)
                layer_acts_y(NCH - 1)

            score_act(act)
            message_act(act)

        @block.tensor
        def _(pe):
            pe.wait_ge(s_prepdiag, 1)
            nc.tensor.matmul(bank[0][:, 0:P], ones[:], diag[:], start=True, stop=True).then_inc(s_preppe, 1)
            pe.wait_ge(s_prepdiag, 2)
            nc.tensor.transpose(bank[1][:, 0:P], carrym[:], ident[:]).then_inc(s_preppe, 1)
            pe.wait_ge(s_prepdiag, 3)
            nc.tensor.matmul(bank[0][:, P:P + 1], carrym[:], tmp2[:, 0:1], start=True, stop=True).then_inc(s_preppe, 1)
            sd = sems_dense

            def transposes(bank_, source):
                for q in range(4):
                    ins = nc.tensor.transpose(bank_[:, q * P:(q + 1) * P], source(q), ident[:])
                return ins

            def dense_b(k):
                first = isinstance(k, int) and k == 0
                pe.wait_ge(sd["h0"], k + 1)
                if first:
                    pe.wait_ge(s_prepdiag, 4)
                    pe.wait_ge(s_prepact, 1)
                if not first:
                    pe.wait_ge(sd["h0t"], k)
                transposes(bank[0], lambda q: h0[:, 2 * q:2 * q + 2, :].rearrange("p c f -> p (c f)")) \
                    .then_inc(sd["h0t_ps"], 1)
                rings = (("h0t", "z1"), ("h1t", "z2"), ("h2t", "z3"))
                backs = (("h1t", "b1", "o1", 2), ("h2t", "b2", "o2", 3), ("h3t", "b3", "x1", 4))
                for l in range(4):
                    if l < 3:
                        pe.wait_ge(sd[rings[l][0]], k + 1)
                        nc.tensor.matmul(bank[1][:], wblk[:, l, :], hT[:, l, :], start=True, stop=True) \
                            .then_inc(sd[rings[l][1]], 1)
                    if l > 0:
                        ready, done, free, bk = backs[l - 1]
                        pe.wait_ge(sd[ready], k + 1)
                        if not first:
                            pe.wait_ge(sd[free], k)
                        transposes(bank[bk], lambda q: hT[:, l, q * P:(q + 1) * P]).then_inc(sd[done], 1)

            dense_b(0)
            with pe.Fori(1, ND) as k:
                dense_b(k)

            sl = sems_layer
            for L in range(3):
                def layer_b(t, last_chunk=False):
                    n = at_turn(L, t)
                    if last_chunk:
                        pe.wait_ge(sl["chain_end"], L + 1)
                        nc.tensor.matmul(bank[5][:, 0:D], carrym[:], last[:], start=True, stop=True) \
                            .then_inc(sl["carry"], 1)
                    pe.wait_ge(sl["z"], n + 1)
                    transposes(bank[0], lambda q: zbuf[:, 2 * q:2 * q + 2, :].rearrange("p c f -> p (c f)")) \
                        .then_inc(sl["t_ps"], 1)
                    pe.wait_ge(sl["t"], n + 1)
                    nc.tensor.matmul(bank[1][:], wblk[:, L, :], hT[:, 0, :], start=True, stop=True).then_inc(sl["mm"], 1)
                    pe.wait_ge(sl["relu"], n + 1)
                    if not (isinstance(n, int) and n == 0):
                        pe.wait_ge(sl["u"], n)
                    transposes(bank[4], lambda q: hT[:, 1, q * P:(q + 1) * P]).then_inc(sl["back"], 1)

                layer_b(0)
                with pe.Fori(1, NCH - 1) as t:
                    layer_b(t)
                layer_b(NCH - 1, last_chunk=True)
            score_pe(pe)
            message_pe(pe)


def kernel(x, src, dst, edge_type_8, L0_gnn_W0, L0_gnn_b0, L0_gnn_W1, L0_gnn_b1, L0_gnn_W2, L0_gnn_b2,
           L1_gnn_rel_weight, L1_gnn_attn_vec, L1_gnn_rel_emb):
    import concourse.bacc as bacc
    from concourse.bass_utils import run_bass_kernel_spmd

    nc = bacc.Bacc("TRN2", target_bir_lowering=False, num_devices=1)
    arrays, aps = {}, {}

    def given(name, a):
        a = np.ascontiguousarray(a)
        arrays[name] = a
        aps[name] = nc.dram_tensor(name, a.shape, mybir.dt.from_np(a.dtype), kind="ExternalInput").ap()
        return aps[name]

    padded = np.zeros((N, XW), np.float32)
    padded[:, :D] = x
    args = [given("x_in", padded), given("src_in", src), given("dst_in", dst), given("etype_in", edge_type_8),
            [given("w0", L0_gnn_W0), given("w1", L0_gnn_W1), given("w2", L0_gnn_W2)],
            [given("b0", L0_gnn_b0), given("b1", L0_gnn_b1), given("b2", L0_gnn_b2)],
            given("rel_weight", L1_gnn_rel_weight), given("attn_vec", L1_gnn_attn_vec)]
    out = nc.dram_tensor("out", (N, D), F32, kind="ExternalOutput").ap()
    build(nc, *args, out)
    got = run_bass_kernel_spmd(nc, [arrays], core_ids=[0])
    return got.results[0]["out"]
```

```python
from contextlib import ExitStack

import numpy as np
import concourse.bass as bass
from concourse import mybir

F32 = mybir.dt.float32
BF16 = mybir.dt.bfloat16
I32 = mybir.dt.int32
ALU = mybir.AluOpType
ACT = mybir.ActivationFunctionType
AX = mybir.AxisListType

P = 128
N, E, D, R, H = 100000, 50000, 64, 8, 4
C = 8
EC = -(-E // P)
SC = -(-(EC + 1) // C) * C
assert SC == EC + 1
NCH = SC // C
SLOTS = P * SC
ROWS = SLOTS + N
XW = D + 4
DC = 2 * C
NB = DC * P
ND = -(-N // NB)
LASTP = (N - (ND - 1) * NB) // DC
assert (ND - 4) % 3 == 0 and LASTP * DC == N - (ND - 1) * NB
OUTSIDE = float(1 << 23)
MW = H * D + 2 * H
CURV, MIN_NORM, EPS = 0.01, 1e-10, 1e-6
MAXNORM = (1.0 - 1e-5) / 0.1
SQ_FLOOR = 1e-19
HEADSTEPS = 8


def build(nc, x, src, dst, etype, w, b, rel_weight, attn_vec, out):
    with ExitStack() as ctx:
        def sb(name, shape, dt=F32):
            return ctx.enter_context(nc.sbuf_tensor(name, shape, dt))

        def psum(name, shape, dt=F32):
            return ctx.enter_context(nc.psum_tensor(name, shape, dt))

        def sem(name):
            return ctx.enter_context(nc.semaphore(name))

        def dram(name, shape):
            return nc.dram_tensor(name, shape, F32).ap()

        nodes = dram("nodes", (N, XW))
        xslot = dram("xslot", (SLOTS, XW))
        table = [None, dram("table1", (ROWS, D)), dram("table2", (ROWS, D)), dram("table3", (ROWS, D))]
        x1slot = dram("x1slot", (SLOTS, D))
        hsrc = dram("hsrc", (SLOTS, D))

        ident = sb("ident", [P, P])
        identb = sb("identb", [P, P], BF16)
        below = sb("below", [P, P])
        ones = sb("ones", [P, P])
        diag = sb("diag", [P, P])
        carrym = sb("carrym", [P, P])
        carryt = sb("carryt", [P, P])
        pen = sb("pen", [P, P])
        wblk = sb("wblk", [P, 3, P])
        bcol = sb("bcol", [P, 3])
        relw = sb("relw", [P, 4, H * D])
        avblk = sb("avblk", [P, 2 * R * H])
        epsln = sb("epsln", [P, 1])
        srci = sb("srci", [P, SC], I32)
        dsti = sb("dsti", [P, SC], I32)
        eti = sb("eti", [P, SC], I32)
        dnext = sb("dnext", [P, 1], I32)
        slotno = sb("slotno", [P, SC], I32)
        srcf = sb("srcf", [P, SC])
        dstf = sb("dstf", [P, SC])
        etf = sb("etf", [P, SC])
        dnextf = sb("dnextf", [P, 1])
        onehot = sb("onehot", [P, SC, R], BF16)
        cont = sb("cont", [P, SC])
        ends = sb("ends", [P, SC])
        head = sb("head", [P, SC])
        headend = sb("headend", [P, SC])
        owns = sb("owns", [P, SC])
        goes = sb("goes", [P, SC])
        cnt = sb("cnt", [P, SC])
        dis = sb("dis", [P, SC])
        tmp = sb("tmp", [P, SC])
        tmp2 = sb("tmp2", [P, SC])
        slotdata = sb("slotdata", [P, SC, 4])
        idx_dst = sb("idx_dst", [P, SC], I32)
        idx_map = sb("idx_map", [P, SC], I32)
        idx_out = sb("idx_out", [P, SC], I32)
        row_of_src = sb("row_of_src", [P, SC], I32)
        headsum = sb("headsum", [P, MW])
        hpart = sb("hpart", [P, MW])
        idxr = sb("idxr", [P, 2, C], I32)
        datar = sb("datar", [P, 2, C, 4])
        rows = sb("rows", [P, 2, C, XW])
        rows64 = rows[:].rearrange("p v c f -> p (v c f)")[:, 0:2 * C * D].rearrange("p (v c f) -> p v c f", v=2, f=D)
        xd = sb("xd", [P, 4, C, XW])
        lns = sb("lns", [P, 2, 2 * C, 1])
        lnc = sb("lnc", [P, 2, 2 * C, D])
        lnq = sb("lnq", [P, 2, 2 * C, D])
        lnv = sb("lnv", [P, 2, 2 * C, 1])
        lnd = sb("lnd", [P, 2, 2 * C, 1])
        lnr = sb("lnr", [P, 2, 2 * C, 1])
        h0 = sb("h0", [P, 2 * C, D])
        hT = sb("hT", [P, 4, P * 4])
        outs = sb("outs", [P, 4, 2, C, D])
        o1, o2, ox, o3 = (outs[:, n, :, :, :] for n in range(4))
        selfr = sb("selfr", [P, 2, C, XW])
        agghead = sb("agghead", [P, C, D])
        last = sb("last", [P, D])
        prod = sb("prod", [P, C, MW])
        dsrc = sb("dsrc", [P, C])
        small = sb("small", [P, 12, SC])

        dense_x = [xd[:].rearrange("p v c f -> p (v c) f")[:, DC * u:DC * u + DC, :] for u in range(2)]
        dense_x.append(prod[:].rearrange("p c f -> p (c f)")[:, 0:DC * XW].rearrange("p (c f) -> p c f", f=XW))
        d1, d2, dx, d3 = (outs[:, n, :, :, :].rearrange("p v c f -> p (v c) f") for n in range(4))
        zbuf = sb("zbuf", [P, C, D])
        scan_g, scan_cont, scan_sum = (prod[:].rearrange("p c f -> p (c f)")[:, n * D * (C + 1):(n + 1) * D * (C + 1)]
                                       for n in range(3))
        by_feature = [a.rearrange("p (f c) -> p f c", c=C + 1) for a in (scan_g, scan_cont, scan_sum)]
        g_in, cont_in, sums = by_feature
        hdb = sb("hdb", [P, C, D])
        hnext = sb("hnext", [P, D])
        hclose = sb("hclose", [P, D])
        score = sb("score", [P, SC, H])
        dots = sb("dots", [P, 2, SC, H])
        smax = sb("smax", [P, SC, H])
        ex4 = sb("ex4", [P, SC, H])
        edge = sb("edge", [P, H])
        masks = sb("masks", [P, 4, C * P], BF16)
        pairsel = sb("pairsel", [R, 4, P], BF16)
        xm = sb("xm", [P, C, 4 * P])
        twice = dots[:].rearrange("p a c h -> p (a c h)")[:, 0:4 * C * D].rearrange("p (v c f) -> p v c f", v=2, f=2 * D)
        ohT = smax[0:R, :, :].rearrange("p c h -> p (c h)")[:, 0:C * P // 2].bitcast(BF16)
        ohc = smax[:, :, :].rearrange("p c h -> p (c h)")[:, C * P // 2:C * P // 2 + C * R // 2].bitcast(BF16)
        rawsb = hT[:].rearrange("p a b -> p (a b)").rearrange("p (c f) -> p c f", f=H * D)
        sqb = outs[:, 2:4, :, :, :].rearrange("p n v c f -> p (n v c f)").rearrange("p (c f) -> p c f", f=H * D)
        sqa = lnq[:].rearrange("p v c f -> p (v c f)").rearrange("p (c f) -> p c f", f=H * D)
        aggs = [xd[:].rearrange("p v c f -> p (v c f)")[:, 0:C * MW].rearrange("p (c f) -> p c f", f=MW),
                small[:].rearrange("p n c -> p (n c)")[:, 4 * SC:4 * SC + C * MW].rearrange("p (c f) -> p c f", f=MW)]
        headpart = rows[:].rearrange("p v c f -> p (v c f)")[:, 0:C // 2 * MW].rearrange("p (c f) -> p c f", f=MW)
        upd, updsq = lnc[:, 0, 0:C, :], lnc[:, 1, 0:C, :]
        scratch = score[:].rearrange("p c h -> p (c h)")
        CH = C * H

        def part(first, n):
            return scratch[:, first:first + n]

        squares, norms = part(0, 2 * CH + C), part(2 * CH + C, 2 * CH + C)
        tanh_in, tanh_out = part(4 * CH + 2 * C, CH + C), part(5 * CH + 3 * C, CH + C)
        logs = part(6 * CH + 4 * C, 3 * CH)
        ka = [part((9 + n) * CH + 4 * C, CH) for n in range(6)]
        kb = [part((15 + n) * CH + 4 * C, CH) for n in range(8)]
        kc = [part((23 + n) * CH + 4 * C, C) for n in range(4)]

        bank = [psum(f"bank{i}", [P, 512]) for i in range(8)]

        s_const = sem("constants_made")
        s_in = sem("inputs_loaded")
        s_pad = sem("pads_set")
        s_padv = sem("attention_pad_set")
        s_nodes = sem("nodes_copied")
        s_prep = sem("prep_step")
        s_prepdiag = sem("prep_operand_ready")
        s_prepact = sem("prep_sqrt")
        s_preppe = sem("prep_product")
        s_idx = sem("index_arrays_ready")
        s_turn, s_turn_sp, s_turn_dve = sem("pool_turn"), sem("sp_turn"), sem("dve_turn")
        s_idxr = sem("indices_staged")
        s_rows = [sem(f"rows_gathered{s}") for s in range(2)]
        s_xst = [sem(f"xslot_stored{s}") for s in range(2)]
        s_map = [sem(f"map_scattered{s}") for s in range(2)]

        sems_dense = {}
        for name in ("xc1", "sq1", "var1", "std1", "h0", "z", "hT", "b1", "b2", "b3", "o1", "o2", "x1", "xc2", "sq2",
                     "var2", "std2", "o3", "step"):
            sems_dense[name] = sem("dense_" + name)
        s_xd = [sem(f"dense_x_loaded{u}") for u in range(3)]
        s_dst1, s_dst2, s_dst3 = sem("dense_rows1_stored"), sem("dense_rows2_stored"), sem("dense_x1_rows3_stored")
        sems_layer = {}
        for name in ("xc1", "sq1", "var1", "std1", "used", "z", "t_ps", "t", "mm", "relu", "back", "u", "xc2", "sq2",
                     "var2", "std2", "o3", "step", "ready", "tiled", "chain", "head", "head_added", "last", "carry"):
            sems_layer[name] = sem("layer_" + name)
        s_self = [sem(f"self_rows_loaded{s}") for s in range(2)]
        s_ust = [sem(f"slots_stored{s}") for s in range(2)]
        s_map_used = sem("row_numbers_made")

        s_loc = [sem(f"attention_rows_loaded{s}") for s in range(2)]
        s_hst = [sem(f"hsrc_stored{s}") for s in range(2)]
        s_out = [sem(f"out_scattered{s}") for s in range(2)]
        sa = {}
        for name in ("step", "bulk", "chain", "hd", "sq", "ps_t", "t", "dots", "used", "seed", "seed_ps", "bulk_pe",
                     "bulk_op", "bulk_act", "bulk_ln"):
            sa[name] = sem("score_" + name)
        s_src = [sem(f"message_sources_loaded{s}") for s in range(2)]
        s_x1 = [sem(f"message_x1_loaded{s}") for s in range(2)]
        sm = {}
        for name in ("step", "ohc", "oh_ps", "oh", "mask_ps", "mask", "sources", "xm", "raw", "rawsb", "squares", "log",
                     "norms", "tanh_in", "tanh", "ln", "scaled", "agg", "aggsq", "upd", "updsq", "head", "headstep",
                     "o", "chain_end", "carry"):
            sm[name] = sem("msg_" + name)

        def slots_view(t, width=None):
            v = t[0:SLOTS, :].rearrange("(p j) f -> p j f", j=SC)
            return v if width is None else v[:, :, 0:width]

        def dense_view(t, first):
            return t[first:first + (ND - 1) * NB, :].rearrange("(k p r) f -> k p r f", p=P, r=DC)

        def dense_last(t, first):
            return t[first + (ND - 1) * NB:first + N, :].rearrange("(p r) f -> p r f", r=DC)

        def dense_at(t, first, k):
            if isinstance(k, int) and k == ND - 1:
                return dense_last(t, first)
            return dense_view(t, first)[bass.ds(k, 1)].rearrange("k p r f -> (k p) r f")

        def dense_stored(eng):
            eng.wait_ge(s_dst1, 16 * ND)
            eng.wait_ge(s_dst2, 16 * ND)
            eng.wait_ge(s_dst3, 32 * ND)

        class Marks:

            def __init__(self, eng, semaphore):
                self.eng, self.semaphore, self.base, self.n = eng, semaphore, 0, 0

            def __call__(self, ins):
                self.n += 1
                ins.then_inc(self.semaphore, 1)
                return self.n

            def wait(self, mark):
                self.eng.wait_ge(self.semaphore, self.base + mark)

            def restart(self, base):
                self.base, self.n = base, 0

        class Steps:

            def __init__(self, eng, semaphore):
                self.eng, self.semaphore, self.base, self.n = eng, semaphore, 0, 0

            def __call__(self, ins):
                self.n += 1
                ins.then_inc(self.semaphore, 1)
                self.eng.wait_ge(self.semaphore, self.base + self.n)

            def restart(self, base):
                self.base, self.n = base, 0

        def bc(ap, shape):
            return ap.broadcast_to(shape)

        block = ctx.enter_context(nc.Block())
        full_rows, rest = P - 1, E - (P - 1) * EC

        def edges_view(a):
            return (a[0:full_rows * EC].rearrange("(p j) -> p j", j=EC),
                    a[full_rows * EC:E].rearrange("(p j) -> p j", p=1))

        N_IN = 0

        def used(q, i, s):
            return q * (NCH // 2 + 1 - s) + i

        def dmas(L, i, s):
            return 16 * used(L, i, s) if L < 2 else 16 * used(2, 0, s) + 32 * i

        def at_turn(L, t):
            return L * NCH + t

        def load_self(sp, L, i, s):
            t = 2 * i + s
            if L > 0 or not (isinstance(t, int) and t < 2):
                sp.wait_ge(sems_layer["used"], at_turn(L, t) - 1)
                if L == 2:
                    sp.wait_ge(sems_layer["u"], at_turn(L, t) - 1)
            if L == 0:
                sp.dma_start(selfr[:, s, :, :], slots_view(xslot)[:, bass.ds(t * C, C), :]).then_inc(s_self[s], 16)
            else:
                sp.dma_start(selfr[:, s, :, 0:D], slots_view(table[L])[:, bass.ds(t * C, C), :]).then_inc(s_self[s], 16)
                if L == 2:
                    sp.dma_start(xd[:, s, :, :], slots_view(xslot)[:, bass.ds(t * C, C), :]).then_inc(s_self[s], 16)

        def store_slots(sp, L, i, s):
            t = 2 * i + s
            where = slots_view(table[L + 1])[:, bass.ds(t * C, C), :]
            if L < 2:
                sp.wait_ge(sems_layer["u"], at_turn(L, t) + 1)
                sp.dma_start(where, o1[:, s, :, :]).then_inc(s_ust[s], 16)
            else:
                sp.wait_ge(sems_layer["u"], at_turn(L, t) + 1)
                sp.dma_start(slots_view(x1slot)[:, bass.ds(t * C, C), :], ox[:, s, :, :]).then_inc(s_ust[s], 16)
                sp.wait_ge(sems_layer["o3"], t + 1)
                sp.dma_start(where, o3[:, s, :, :]).then_inc(s_ust[s], 16)

        def layer_sp(sp, L):
            if L > 0:
                for s in range(2):
                    sp.wait_ge(s_ust[s], dmas(L, 0, s))
            else:
                sp.wait_ge(sems_dense["x1"], 2 * ND)
            load_self(sp, L, 0, 0)
            load_self(sp, L, 0, 1)
            load_self(sp, L, 1, 0)
            with sp.Fori(0, NCH // 2 - 1) as i:
                load_self(sp, L, i + 1, 1)
                store_slots(sp, L, i, 0)
                load_self(sp, L, i + 2, 0)
                store_slots(sp, L, i, 1)
            store_slots(sp, L, NCH // 2 - 1, 0)
            store_slots(sp, L, NCH // 2 - 1, 1)
            store_slots(sp, L, NCH // 2, 0)
            if L == 2:
                for s in range(2):
                    sp.wait_ge(s_ust[s], dmas(2, NCH // 2 + 1 - s, s))

        def attention_sp(sp):
            def load(i, s):
                k = 2 * i + s
                t = (NCH - 1) - k
                if not (isinstance(k, int) and k < 2):
                    sp.wait_ge(sa["chain"], k - 1)
                    sp.sem_inc(s_turn_sp, 1)
                sp.dma_start(selfr[:, s, :, 0:D], slots_view(table[3])[:, bass.ds(t * C, C), :]).then_inc(s_loc[s], 16)

            def store(i, s):
                t = (NCH - 1) - (2 * i + s)
                sp.wait_ge(s_rows[s], (used(4, i, s) + 1) * (16 * C))
                sp.sem_inc(s_turn_sp, 1)
                sp.dma_start(slots_view(hsrc)[:, bass.ds(t * C, C), :], rows64[:, s, :, :]).then_inc(s_hst[s], 16)

            load(0, 0)
            load(0, 1)
            with sp.Fori(0, NCH // 2 - 1) as i:
                for s in range(2):
                    store(i, s)
                    load(i + 1, s)
            i = NCH // 2 - 1
            store(i, 0)
            load(i + 1, 0)
            store(i, 1)
            store(i + 1, 0)
            for s in range(2):
                sp.wait_ge(s_hst[s], 16 * (NCH // 2 + 1 - s))
            sp.wait_ge(sa["bulk_act"], 5)

            def load_sources(i, s):
                t = 2 * i + s
                if not (isinstance(t, int) and t < 2):
                    sp.wait_ge(sm["sources"], 2 * t - 2)
                    sp.sem_inc(s_turn_sp, 1)
                for half in range(2):
                    sp.dma_start(twice[:, s, :, D * half:D * half + D], slots_view(hsrc)[:, bass.ds(t * C, C), :]) \
                        .then_inc(s_src[s], 16)

            def load_x1(i, s):
                t = 2 * i + s
                if not (isinstance(t, int) and t < 2):
                    sp.wait_ge(sm["o"], t - 1)
                    sp.sem_inc(s_turn_sp, 1)
                sp.dma_start(selfr[:, s, :, 0:D], slots_view(x1slot)[:, bass.ds(t * C, C), :]).then_inc(s_x1[s], 16)

            load_sources(0, 0)
            load_sources(0, 1)
            load_x1(0, 0)
            load_x1(0, 1)
            load_sources(1, 0)
            load_sources(1, 1)
            with sp.Fori(1, NCH // 2 - 1) as i:
                for s in range(2):
                    load_x1(i, s)
                    load_sources(i + 1, s)
            load_x1(NCH // 2 - 1, 0)
            load_sources(NCH // 2, 0)
            load_x1(NCH // 2 - 1, 1)
            load_x1(NCH // 2, 0)

        def attention_pool(pool, gather_pass, stage):
            for s in range(2):
                pool.wait_ge(s_ust[s], dmas(2, NCH // 2 + 1 - s, s))

            def free(i, s):
                if isinstance(i, int) and i == 0:
                    return [(sems_layer["used"], 3 * NCH)]
                return [(sa["used"], 2 * i + s - 1), (s_hst[s], 16 * i)]

            gather_pass(4, row_of_src, table[3], D, ROWS - 1, free, reverse=True, ring=rows64)
            for s in range(2):
                pool.wait_ge(s_rows[s], used(5, 0, s) * (16 * C))

            def head_parts(t, s, m=C):
                if m == C:
                    pool.wait_ge(sm["agg"], t + 1)
                else:
                    pool.wait_ge(sm["chain_end"], 1)
                pool.sem_inc(s_turn, 1)
                for half in range(2):
                    n = min(C // 2, m - half * C // 2)
                    count = HEADSTEPS * t + half * HEADSTEPS // 2

                    def then(ins, k):
                        ins.then_inc(sm["headstep"], 1)
                        pool.wait_ge(sm["headstep"], count + k)
                        pool.sem_inc(s_turn, 1)

                    hb = headend[:, bass.ds(t * C + half * (C // 2), n)].rearrange("p (c k) -> p c k", k=1)
                    then(nc.gpsimd.tensor_tensor(headpart[:, 0:n, :], aggs[s][:, half * (C // 2):half * (C // 2) + n, :],
                                                 hb.broadcast_to([P, n, MW]), ALU.mult), 1)
                    then(nc.gpsimd.tensor_tensor(headpart[:, 0:n - 2, :], headpart[:, 0:n - 2, :], headpart[:, 2:n, :],
                                                 ALU.add), 2)
                    then(nc.gpsimd.tensor_tensor(headpart[:, 0, :], headpart[:, 0, :], headpart[:, 1, :], ALU.add), 3)
                    ins = nc.gpsimd.tensor_tensor(headsum[:], headsum[:], headpart[:, 0, :], ALU.add)
                    then(ins, 4)
                nc.gpsimd.sem_inc(sm["head"], 1)

            def scatter(i, s):
                k = 2 * i + s
                if not (isinstance(i, int) and i == 0):
                    pool.wait_ge(s_out[s], i * (16 * C))
                stage(idx_out, k, s)
                pool.wait_ge(sm["o"], k + 1)
                pool.wait_ge(s_idxr, 7 * NCH + k + 1)
                pool.sem_inc(s_turn, 1)
                for c in range(C):
                    pool.indirect_dma_start(out=out[:, :],
                                            out_offset=bass.IndirectOffsetOnAxis(ap=idxr[:, s, c:c + 1], axis=0),
                                            in_=o1[:, s, c, :], in_offset=None, bounds_check=N - 1,
                                            oob_is_err=False).then_inc(s_out[s], 16)

            head_parts(0, 0)
            head_parts(1, 1)
            head_parts(2, 0)
            scatter(0, 0)
            head_parts(3, 1)
            scatter(0, 1)
            with pool.Fori(2, NCH // 2) as i:
                for s in range(2):
                    head_parts(2 * i + s, s)
                    scatter(i - 1, s)
            head_parts(NCH - 1, 0, m=C - 1)
            scatter(NCH // 2 - 1, 0)
            scatter(NCH // 2 - 1, 1)
            scatter(NCH // 2, 0)
            for s in range(2):
                pool.wait_ge(s_out[s], (NCH // 2 + 1 - s) * 16 * C)

        def score_dve(dve):
            link = Steps(dve, sa["step"])
            PER = C + 5

            def turn(i, s, k):
                t = (NCH - 1) - k
                cols = bass.ds(t * C, C)
                first = isinstance(k, int) and k == 0
                g = rows64[:, s, :, :]
                own = selfr[:, s, :, 0:D]
                dve.wait_ge(s_loc[s], 16 * (i + 1))
                dve.sem_inc(s_turn_dve, 1)
                if first:
                    nc.vector.tensor_scalar(last[:], own[:, C - 1, :], owns[:, EC:SC], None, ALU.mult).then_inc(sa["seed"], 1)
                    dve.wait_ge(sa["seed_ps"], 1)
                    link(nc.vector.tensor_copy(hnext[:], bank[5][:, 0:D]))
                    link(nc.vector.tensor_scalar(edge[:, 0:1], owns[:, EC:SC], -1.0, 1.0, ALU.mult, ALU.add))
                    link(nc.vector.scalar_tensor_tensor(hclose[:], hnext[:], edge[:, 0:1], last[:], ALU.mult, ALU.add))
                ob = owns[:, cols].rearrange("p (c k) -> p c k", k=1)
                link(nc.vector.tensor_tensor(prod[:, :, 0:D], own, bc(ob, [P, C, D]), ALU.mult))
                for c in range(C):
                    ins = nc.vector.scalar_tensor_tensor(prod[:, c, 0:D], hclose[:], head[:, bass.ds(t * C + c, 1)],
                                                         prod[:, c, 0:D], ALU.mult, ALU.add)
                link(ins)
                if not first:
                    dve.wait_ge(sa["ps_t"], k)
                    dve.wait_ge(sa["sq"], k)
                columns = range(C - 2, -1, -1) if first else range(C - 1, -1, -1)
                for c in columns:
                    behind = hnext[:] if c == columns[0] else hdb[:, c + 1, :]
                    ins = nc.vector.scalar_tensor_tensor(hdb[:, c, :], behind, goes[:, bass.ds(t * C + c, 1)],
                                                         prod[:, c, 0:D], ALU.mult, ALU.add)
                    if c > 0:
                        link(ins)
                ins.then_inc(sa["chain"], 1)
                dve.wait_ge(sa["chain"], k + 1)
                dve.wait_ge(s_rows[s], (used(4, i, s) + 1) * (16 * C))
                nc.vector.tensor_copy(hnext[:], hdb[:, 0, :])
                link(nc.vector.tensor_tensor(prod[:, :, 0:D], g, hdb[:], ALU.mult))
                nc.vector.tensor_reduce(small[:, 2, cols], prod[:, :, 0:D], AX.X, ALU.add)
                dve.wait_ge(sa["sq"], k + 1)
                nc.vector.tensor_reduce(small[:, 0:2, cols], lnq[:, 0, :, :].rearrange("p (a c) f -> p a c f", a=2), AX.X,
                                        ALU.add)
                dve.wait_ge(sa["dots"], k + 1)
                oh = onehot[:, cols, :].rearrange("p c (r k) -> p (c r) k", k=1)
                for a in range(2):
                    ins = nc.vector.tensor_tensor(prod[:, :, 64 + 32 * a:96 + 32 * a].rearrange("p c (r h) -> p c r h", h=H),
                                                  bank[2][:, 256 * a:256 * a + 256].rearrange("p (c r h) -> p c r h", r=R, h=H),
                                                  bc(onehot[:, cols, :].rearrange("p c (r k) -> p c r k", k=1), [P, C, R, H]),
                                                  ALU.mult)
                link(ins)
                for a in range(2):
                    ins = nc.vector.tensor_reduce(dots[:, a, cols, :],
                                                  prod[:, :, 64 + 32 * a:96 + 32 * a].rearrange("p c (r h) -> p c h r", h=H),
                                                  AX.X, ALU.add)
                ins.then_inc(sa["used"], 1)
                dve.wait_ge(sa["used"], k + 1)

            link.restart(0)
            dve.wait_ge(sems_layer["o3"], NCH)
            turn(0, 0, 0)
            start = link.n
            link.restart(start)
            turn(0, 1, 1)
            per = link.n
            with dve.Fori(1, NCH // 2) as i:
                for s in range(2):
                    link.restart(start + (2 * i + s - 1) * per)
                    turn(i, s, 2 * i + s)
                    assert link.n == per
            link.restart(start + (NCH - 2) * per)
            turn(NCH // 2, 0, NCH - 1)
            assert link.n == per

            link = Steps(dve, sa["bulk"])
            acts = [0]
            ops = [0]

            def ready(ins):
                ops[0] += 1
                ins.then_inc(sa["bulk_op"], 1)

            def after_act():
                acts[0] += 1
                dve.wait_ge(sa["bulk_act"], acts[0])

            a2, b2, ab = small[:, 0, :], small[:, 1, :], small[:, 2, :]
            v = [small[:, n, :] for n in range(12)]

            def log_factor(norm2, into):
                ready(nc.vector.tensor_scalar(v[9], norm2, SQ_FLOOR, None, ALU.max))
                after_act()
                link(nc.vector.tensor_scalar(v[9], v[10], CURV ** 0.5, MIN_NORM, ALU.mult, ALU.max))
                ready(nc.vector.tensor_scalar(v[9], v[9], 1.0 - 1e-5, None, ALU.min))
                after_act()
                link(nc.vector.tensor_tensor(v[10], v[10], v[11], ALU.subtract))
                link(nc.vector.reciprocal(v[11], v[9]))
                link(nc.vector.scalar_tensor_tensor(into, v[10], 0.5, v[11], ALU.mult, ALU.mult))

            log_factor(a2, small[:, 3, :])
            link(nc.vector.tensor_scalar(v[4], ab, -2.0 * CURV, 1.0, ALU.mult, ALU.add))
            link(nc.vector.tensor_tensor(v[5], a2, b2, ALU.mult))
            link(nc.vector.scalar_tensor_tensor(v[5], v[5], CURV ** 2, v[4], ALU.mult, ALU.add))
            link(nc.vector.tensor_scalar(v[5], v[5], MIN_NORM, None, ALU.max))
            link(nc.vector.reciprocal(v[6], v[5]))
            link(nc.vector.scalar_tensor_tensor(v[4], b2, CURV, v[4], ALU.mult, ALU.add))
            link(nc.vector.tensor_tensor(v[4], v[4], v[6], ALU.mult))
            link(nc.vector.tensor_scalar(v[5], a2, -CURV, 1.0, ALU.mult, ALU.add))
            link(nc.vector.tensor_tensor(v[5], v[5], v[6], ALU.mult))
            link(nc.vector.tensor_tensor(v[6], v[4], a2, ALU.mult))
            link(nc.vector.tensor_tensor(v[7], v[5], ab, ALU.mult))
            link(nc.vector.scalar_tensor_tensor(v[6], v[7], -2.0, v[6], ALU.mult, ALU.add))
            link(nc.vector.tensor_tensor(v[6], v[6], v[4], ALU.mult))
            link(nc.vector.tensor_tensor(v[7], v[5], v[5], ALU.mult))
            link(nc.vector.tensor_tensor(v[7], v[7], b2, ALU.mult))
            link(nc.vector.tensor_tensor(v[6], v[6], v[7], ALU.add))
            log_factor(v[6], v[8])
            link(nc.vector.tensor_tensor(v[4], v[4], v[8], ALU.mult))
            link(nc.vector.tensor_tensor(v[5], v[5], v[8], ALU.mult))
            f4 = bc(v[4].rearrange("p (c k) -> p c k", k=1), [P, SC, H])
            f5 = bc(v[5].rearrange("p (c k) -> p c k", k=1), [P, SC, H])
            link(nc.vector.tensor_tensor(dots[:, 0, :, :], dots[:, 0, :, :], f4, ALU.mult))
            link(nc.vector.tensor_tensor(dots[:, 1, :, :], dots[:, 1, :, :], f5, ALU.mult))
            link(nc.vector.tensor_tensor(score[:], dots[:, 0, :, :], dots[:, 1, :, :], ALU.subtract))
            link(nc.vector.scalar_tensor_tensor(score[:], score[:], 0.2, score[:], ALU.mult, ALU.max))
            BIG = 1e30
            link(nc.vector.tensor_scalar(tmp[:], cont[:], BIG, -BIG, ALU.mult, ALU.add))
            link(nc.vector.tensor_scalar(tmp2[:, 0:EC], ends[:, 0:EC], -BIG, None, ALU.mult))
            for h in range(H):
                link(nc.vector.tensor_tensor_scan(smax[:, 0:EC, h], tmp[:, 0:EC], score[:, 0:EC, h], -BIG, ALU.add,
                                                  ALU.max))
            link(nc.vector.tensor_copy(edge[:], smax[:, EC - 1, :]))
            for h in range(H):
                nc.vector.tensor_tensor_scan(dots[:, 0, 0:EC, h][:, ::-1],
                                             tmp2[:, 0:EC][:, ::-1], smax[:, 0:EC, h][:, ::-1], -BIG, ALU.add, ALU.max)
            link(nc.vector.tensor_scalar(v[9], head[:], BIG, -BIG, ALU.mult, ALU.add))
            link(nc.vector.tensor_scalar(v[10], dstf[:], dstf[:, EC - 1:EC], None, ALU.is_equal))
            link(nc.vector.tensor_scalar(v[10], v[10], BIG, -BIG, ALU.mult, ALU.add))
            for h in range(H):
                for part, value, m, mask in ((0, edge[:, h:h + 1], carryt, v[9]), (1, dots[:, 0, 0, h:h + 1], carrym, v[10])):
                    ready(nc.vector.tensor_scalar(diag[:], ident[:], value, None, ALU.mult))
                    link(nc.vector.tensor_scalar(pen[:], m[:], BIG, -BIG, ALU.mult, ALU.add))
                    acts[0] += 0
                    dve.wait_ge(sa["bulk_pe"], 2 * h + part + 1)
                    link(nc.vector.tensor_tensor(pen[:], pen[:], bank[5][:, 0:P], ALU.add))
                    link(nc.vector.tensor_reduce(hpart[:, part:part + 1], pen[:], AX.X, ALU.max))
                for part, mask in ((0, v[9]), (1, v[10])):
                    link(nc.vector.scalar_tensor_tensor(dots[:, 0, :, h], mask, hpart[:, part:part + 1], dots[:, 0, :, h],
                                                        ALU.add, ALU.max))
            ready(nc.vector.tensor_tensor(score[:, 0:EC, :], score[:, 0:EC, :], dots[:, 0, 0:EC, :], ALU.subtract))
            after_act()

        def score_act(act):
            def turn(i, s, k):
                act.wait_ge(s_rows[s], (used(4, i, s) + 1) * (16 * C))
                nc.scalar.activation(lnq[:, 0, 0:C, :], rows64[:, s, :, :], ACT.Square)
                act.wait_ge(sa["chain"], k + 1)
                nc.scalar.activation(lnq[:, 0, C:2 * C, :], hdb[:], ACT.Square).then_inc(sa["sq"], 1)
                act.wait_ge(sa["ps_t"], k + 1)
                nc.scalar.copy(hT[:, 0, :], bank[0][:])
                nc.scalar.copy(hT[:, 1, :], bank[1][:]).then_inc(sa["t"], 1)

            def turn_at(i, s):
                k = 2 * i + s
                if not (isinstance(k, int) and k == 0):
                    act.wait_ge(sa["used"], k)
                turn(i, s, k)

            turn_at(0, 0)
            turn_at(0, 1)
            with act.Fori(1, NCH // 2) as i:
                turn_at(i, 0)
                turn_at(i, 1)
            turn_at(NCH // 2, 0)
            for n in range(2):
                act.wait_ge(sa["bulk_op"], 2 * n + 1)
                nc.scalar.activation(small[:, 10, :], small[:, 9, :], ACT.Sqrt).then_inc(sa["bulk_act"], 1)
                act.wait_ge(sa["bulk_op"], 2 * n + 2)
                nc.scalar.activation(small[:, 10, :], small[:, 9, :], ACT.Ln, bias=1.0, scale=1.0).then_inc(sa["bulk_ln"], 1)
                act.wait_ge(sa["bulk_ln"], n + 1)
                nc.scalar.activation(small[:, 11, :], small[:, 9, :], ACT.Ln, bias=1.0, scale=-1.0).then_inc(sa["bulk_act"], 1)
            act.wait_ge(sa["bulk_op"], 4 + 2 * H + 1)
            nc.scalar.activation(ex4[:, 0:EC, :], score[:, 0:EC, :], ACT.Exp).then_inc(sa["bulk_act"], 1)

        def score_pe(pe):
            def turn(i, s, k):
                pe.wait_ge(s_rows[s], (used(4, i, s) + 1) * (16 * C))
                if not (isinstance(k, int) and k == 0):
                    pe.wait_ge(sa["t"], k)
                for q in range(4):
                    nc.tensor.transpose(bank[0][:, q * P:(q + 1) * P], rows64[:, s, 2 * q:2 * q + 2, :].rearrange("p c f -> p (c f)"), ident[:])
                pe.wait_ge(sa["chain"], k + 1)
                for q in range(4):
                    ins = nc.tensor.transpose(bank[1][:, q * P:(q + 1) * P],
                                              hdb[:, 2 * q:2 * q + 2, :].rearrange("p c f -> p (c f)"), ident[:])
                ins.then_inc(sa["ps_t"], 1)
                pe.wait_ge(sa["t"], k + 1)
                if not (isinstance(k, int) and k == 0):
                    pe.wait_ge(sa["used"], k)
                for a in range(2):
                    for q in range(4):
                        ins = nc.tensor.matmul(bank[2][:, 256 * a + 64 * q:256 * a + 64 * q + 64],
                                               hT[:, a, q * P:(q + 1) * P], avblk[:], start=True, stop=True)
                ins.then_inc(sa["dots"], 1)

            pe.wait_ge(sa["seed"], 1)
            nc.tensor.matmul(bank[5][:, 0:D], carryt[:], last[:], start=True, stop=True).then_inc(sa["seed_ps"], 1)
            turn(0, 0, 0)
            turn(0, 1, 1)
            with pe.Fori(1, NCH // 2) as i:
                turn(i, 0, 2 * i)
                turn(i, 1, 2 * i + 1)
            turn(NCH // 2, 0, NCH - 1)
            for n in range(2 * H):
                pe.wait_ge(sa["bulk_op"], 4 + n + 1)
                nc.tensor.matmul(bank[5][:, 0:P], ones[:], diag[:], start=True, stop=True).then_inc(sa["bulk_pe"], 1)

        MASKS = 8

        def message_pe(pe):
            def one_hots(t):
                if not (isinstance(t, int) and t == 0):
                    pe.wait_ge(sm["mask"], MASKS * t)
                pe.wait_ge(sm["ohc"], t + 1)
                bk = bank[2][:].bitcast(BF16)
                for c in range(C):
                    ins = nc.tensor.transpose(bk[0:R, c * P:(c + 1) * P], ohc[:, c * R:(c + 1) * R], identb[:])
                ins.then_inc(sm["oh_ps"], 1)

            def mask(t, n):
                half, q = n // 4, n % 4
                if n == 0:
                    pe.wait_ge(sm["oh"], t + 1)
                if n >= 2:
                    pe.wait_ge(sm["mask"], MASKS * t + n - 1)
                nc.tensor.matmul(bank[2 + n % 2][:], pairsel[:, q, :], ohT[:, 512 * half:512 * half + 512],
                                 start=True, stop=True).then_inc(sm["mask_ps"], 1)

            def sources(i, s):
                t = 2 * i + s
                pe.wait_ge(s_src[s], 32 * (i + 1))
                if not (isinstance(t, int) and t == 0):
                    pe.wait_ge(sm["xm"], t * C)
                for c in range(C):
                    ins = nc.tensor.transpose(bank[c // 4][:, c % 4 * P:(c % 4 + 1) * P], twice[:, s, c, :], ident[:])
                    if c % 4 == 3:
                        ins.then_inc(sm["sources"], 1)

            def chunk(i, s, last_mask=False, last_chunk=False):
                t = 2 * i + s
                for c in range(C):
                    pe.wait_ge(sm["xm"], t * C + c + 1)
                    if c % 2 == 0 and not (isinstance(t, int) and t == 0):
                        pe.wait_ge(sm["rawsb"], (t - 1) * 4 + c // 2 + 1)
                    for q in range(4):
                        ins = nc.tensor.matmul(bank[4 + c // 2][:, 256 * (c % 2):256 * (c % 2) + 256],
                                               xm[:, c, q * P:(q + 1) * P], relw[:, q, :], start=(q == 0), stop=(q == 3))
                    if c % 2 == 1:
                        ins.then_inc(sm["raw"], 1)
                    if last_chunk:
                        continue
                    if c == 1:
                        one_hots(t + 1)
                    if c == 6:
                        sources(i + s, 1 - s)
                    for n in {2: (0, 1), 4: (2, 3), 5: (4, 5), 6: (6,), 7: (7,)}.get(c, ()):
                        mask(t + 1, n)

            pe.wait_ge(sa["bulk_act"], 5)
            pe.wait_ge(sa["used"], NCH)
            one_hots(0)
            for n in range(MASKS):
                mask(0, n)
            sources(0, 0)
            chunk(0, 0)
            chunk(0, 1)
            with pe.Fori(1, NCH // 2) as i:
                chunk(i, 0)
                chunk(i, 1)
            chunk(NCH // 2, 0, last_chunk=True)
            pe.wait_ge(sm["chain_end"], 1)
            nc.tensor.matmul(bank[0][:, 0:MW], carrym[:], aggs[0][:, C - 2, :], start=True, stop=True) \
                .then_inc(sm["carry"], 1)

        def message_act(act):
            def one_hots_in(t):
                nc.scalar.copy(ohc.rearrange("p (c r) -> p c r", r=R), onehot[:, bass.ds(t * C, C), :]).then_inc(sm["ohc"], 1)

            def one_hots_out(t):
                act.wait_ge(sm["oh_ps"], t + 1)
                nc.scalar.copy(ohT, bank[2][:].bitcast(BF16)[0:R, :]).then_inc(sm["oh"], 1)

            def mask_out(t, n):
                half, q = n // 4, n % 4
                if n == 0 and not (isinstance(t, int) and t == 0):
                    act.wait_ge(sm["xm"], t * C)
                act.wait_ge(sm["mask_ps"], MASKS * t + n + 1)
                nc.scalar.copy(masks[:, q, 512 * half:512 * half + 512], bank[2 + n % 2][:]).then_inc(sm["mask"], 1)

            def raw_out(t, m):
                act.wait_ge(sm["raw"], t * 4 + m + 1)
                if m == 0 and not (isinstance(t, int) and t == 0):
                    act.wait_ge(sm["scaled"], t)
                bk = bank[4 + m][:].rearrange("p (c f) -> p c f", f=H * D)
                nc.scalar.activation(sqb[:, 2 * m:2 * m + 2, :], bk, ACT.Square)
                nc.scalar.copy(rawsb[:, 2 * m:2 * m + 2, :], bk).then_inc(sm["rawsb"], 1)

            def turn(t, stages="AB", ahead=2):
                if ahead == 2:
                    one_hots_in(t + 2)
                act.wait_ge(sm["squares"], t + 1)
                nc.scalar.activation(norms, squares, ACT.Ln).then_inc(sm["log"], 1)
                act.wait_ge(sm["log"], t + 1)
                nc.scalar.activation(norms, norms, ACT.Exp, scale=0.5).then_inc(sm["norms"], 1)
                if ahead == 2:
                    one_hots_out(t + 2)
                act.wait_ge(sm["tanh_in"], t + 1)
                nc.scalar.activation(tanh_out, tanh_in, ACT.Tanh).then_inc(sm["tanh"], 1)
                nc.scalar.activation(logs[:, CH:2 * CH], logs[:, 0:CH], ACT.Ln, bias=1.0, scale=1.0)
                nc.scalar.activation(logs[:, 2 * CH:3 * CH], logs[:, 0:CH], ACT.Ln, bias=1.0, scale=-1.0) \
                    .then_inc(sm["ln"], 1)
                if ahead == 2:
                    for n in range(4):
                        mask_out(t + 2, n)
                if ahead >= 1:
                    raw_out(t + 1, 0)
                    raw_out(t + 1, 1)
                if ahead == 2:
                    mask_out(t + 2, 4)
                    mask_out(t + 2, 5)
                if "A" in stages:
                    act.wait_ge(sm["agg"], t + 1)
                    nc.scalar.activation(sqa, aggs_now(t)[:, :, 0:H * D], ACT.Square).then_inc(sm["aggsq"], 1)
                if ahead >= 1:
                    raw_out(t + 1, 2)
                if ahead == 2:
                    mask_out(t + 2, 6)
                if ahead >= 1:
                    raw_out(t + 1, 3)
                if ahead == 2:
                    mask_out(t + 2, 7)
                if "B" in stages:
                    act.wait_ge(sm["upd"], t)
                    nc.scalar.activation(updsq, upd, ACT.Square).then_inc(sm["updsq"], 1)

            slot = [0]

            def aggs_now(t):
                return aggs[slot[0]]

            def turn_in(s, t, **how):
                slot[0] = s
                turn(t, **how)

            for t in range(2):
                one_hots_in(t)
                one_hots_out(t)
                for n in range(6):
                    mask_out(t, n)
                    if t == 1 and n == 3:
                        raw_out(0, 0)
                        raw_out(0, 1)
                if t == 1:
                    raw_out(0, 2)
                mask_out(t, 6)
                if t == 1:
                    raw_out(0, 3)
                mask_out(t, 7)
            turn_in(0, 0, stages="A")
            turn_in(1, 1)
            with act.Fori(1, NCH // 2 - 1) as i:
                turn_in(0, 2 * i)
                turn_in(1, 2 * i + 1)
            turn_in(0, NCH - 3)
            turn_in(1, NCH - 2, ahead=1)
            turn_in(0, NCH - 1, ahead=0)
            turn_in(1, NCH, stages="B", ahead=0)
            turn_in(0, NCH + 1, stages="", ahead=0)

        def message_dve(dve):
            done = Marks(dve, sm["step"])

            def masked(t, c):
                if c % 4 == 0:
                    dve.wait_ge(sm["sources"], 2 * t + c // 4 + 1)
                    dve.wait_ge(sm["mask"], MASKS * t + c + 4)
                if c % 2 == 0 and not (isinstance(t, int) and t == 0):
                    dve.wait_ge(sm["raw"], (t - 1) * 4 + c // 2 + 1)
                nc.vector.tensor_tensor(xm[:, c, :].rearrange("p (q e) -> p q e", q=4),
                                        bc(bank[c // 4][:, c % 4 * P:(c % 4 + 1) * P].rearrange("p (k e) -> p k e", k=1), [P, 4, P]),
                                        masks[:, :, c * P:(c + 1) * P], ALU.mult).then_inc(sm["xm"], 1)

            def heads(v):
                return v.rearrange("p (c h) -> p c h", h=H)

            def over_features(v):
                return bc(v.rearrange("p (c h k) -> p c h k", h=H, k=1), [P, C, H, D])

            def by_head(buf):
                return buf[:, :, 0:H * D].rearrange("p c (h o) -> p c h o", o=D)

            def factor(t):
                return bc(small[:, 3, bass.ds(t * C, C)].rearrange("p (c k) -> p c k", k=1), [P, C, H])

            V = nc.vector
            sqA, sqC, sqB = squares[:, 0:CH], squares[:, CH:CH + C], squares[:, CH + C:]
            nA, nC, nB = norms[:, 0:CH], norms[:, CH:CH + C], norms[:, CH + C:]
            tA, tC = tanh_in[:, 0:CH], tanh_in[:, CH:CH + C]
            thA, thC = tanh_out[:, 0:CH], tanh_out[:, CH:CH + C]

            def turn(i, s, t, stages="ABC", ahead=True, first=False, last_chunk=False):
                A, B, Cc = ("A" in stages), ("B" in stages), ("C" in stages)
                mine, other = aggs[s], aggs[1 - s]
                if ahead:
                    for c in range(3):
                        masked(t + 1, c)
                if A:
                    dve.wait_ge(sm["rawsb"], t * 4 + 4)
                    m = done(V.tensor_reduce(ka[0], sqb.rearrange("p c (h o) -> p (c h) o", o=D), AX.X, ALU.add))
                    done.wait(m)
                    V.tensor_scalar(sqA, ka[0], SQ_FLOOR, None, ALU.max).then_inc(sm["squares"], 1)
                else:
                    dve.sem_inc(sm["squares"], 1)
                if B:
                    wsum, esum = other[:, :, H * D:H * D + H], other[:, :, H * D + H:MW]
                    b1 = done(V.scalar_tensor_tensor(heads(kb[0]), esum, EPS, wsum, ALU.mult, ALU.add))
                if ahead:
                    masked(t + 1, 3)
                if B:
                    done.wait(b1)
                    b1 = done(V.tensor_scalar(kb[0], kb[0], 1e-30, None, ALU.max))
                if ahead:
                    masked(t + 1, 4)
                if B:
                    done.wait(b1)
                    b1 = done(V.reciprocal(kb[1], kb[0]))
                if ahead:
                    masked(t + 1, 5)
                dve.wait_ge(sm["norms"], t + 1)
                if A:
                    a1 = done(V.tensor_tensor(heads(ka[0]), heads(nA), factor(t), ALU.mult))
                if B:
                    done.wait(b1)
                    b1 = done(V.tensor_tensor(kb[2], nB, kb[1], ALU.mult))
                if Cc:
                    ins = V.tensor_scalar(tC, nC, MIN_NORM, CURV ** 0.5, ALU.max, ALU.mult)
                if A:
                    done.wait(a1)
                    ins = V.tensor_scalar(tA, ka[0], MIN_NORM, CURV ** 0.5, ALU.max, ALU.mult)
                if B:
                    done.wait(b1)
                    b1 = done(V.tensor_scalar(kb[2], kb[2], MIN_NORM, None, ALU.max))
                    done.wait(b1)
                    b1 = done(V.reciprocal(kb[3], kb[2]))
                    done.wait(b1)
                    b1 = done(V.tensor_scalar(kb[3], kb[3], MAXNORM, 1.0, ALU.mult, ALU.min))
                    done.wait(b1)
                    b1 = done(V.tensor_tensor(kb[2], kb[2], kb[3], ALU.mult))
                    done.wait(b1)
                    b1 = done(V.tensor_scalar(kb[2], kb[2], CURV ** 0.5, MIN_NORM, ALU.mult, ALU.max))
                    done.wait(b1)
                    ins = V.tensor_scalar(logs[:, 0:CH], kb[2], 1.0 - 1e-5, None, ALU.min)
                ins.then_inc(sm["tanh_in"], 1)
                if ahead:
                    masked(t + 1, 6)
                dve.wait_ge(sm["tanh_in"], t + 1)
                if Cc:
                    c1 = done(V.reciprocal(kc[0], tC))
                if B:
                    b1 = done(V.reciprocal(kb[4], logs[:, 0:CH]))
                    b2 = done(V.tensor_tensor(kb[5], kb[1], kb[3], ALU.mult))
                if ahead:
                    masked(t + 1, 7)
                dve.wait_ge(sm["tanh"], t + 1)
                if A:
                    ext = ex4[:, bass.ds(t * C, C), :]
                    a1 = done(V.tensor_tensor(ka[0], thA, thA, ALU.mult))
                    a2 = done(V.tensor_tensor(heads(ka[3]), heads(thA), factor(t), ALU.mult))
                if Cc:
                    done.wait(c1)
                    c1 = done(V.tensor_tensor(kc[1], kc[0], thC, ALU.mult))
                if A:
                    done.wait(a1)
                    a1 = done(V.tensor_scalar(ka[0], ka[0], -1.0, 1.0, ALU.mult, ALU.add))
                    V.tensor_copy(prod[:, :, H * D + H:MW], ext)
                    done.wait(a1)
                    a1 = done(V.tensor_scalar(ka[0], ka[0], EPS, None, ALU.add))
                if B:
                    done.wait(b2)
                    b2 = done(V.tensor_tensor(kb[4], kb[4], kb[5], ALU.mult))
                if A:
                    done.wait(a1)
                    a1 = done(V.tensor_tensor(ka[0], ka[0], tA, ALU.mult))
                    done.wait(a1)
                    a1 = done(V.reciprocal(ka[1], ka[0]))
                if Cc:
                    done.wait(c1)
                    c1 = done(V.tensor_tensor(upd, upd, bc(kc[1].rearrange("p (c k) -> p c k", k=1), [P, C, D]), ALU.mult))
                if A:
                    done.wait(a1)
                    a1 = done(V.scalar_tensor_tensor(heads(ka[1]), heads(ka[1]), 2.0, ext, ALU.mult, ALU.mult))
                if Cc:
                    dve.wait_ge(s_x1[s], 16 * i)
                    if not (isinstance(i, int) and i <= 1):
                        dve.wait_ge(s_out[s], (i - 1) * (16 * C))
                    done.wait(c1)
                    V.tensor_tensor(o1[:, s, :, :], upd, selfr[:, s, :, 0:D], ALU.add).then_inc(sm["o"], 1)
                if A:
                    done.wait(a1)
                    a1 = done(V.tensor_tensor(ka[2], ka[1], ka[3], ALU.mult))
                    V.tensor_tensor(prod[:, :, H * D:H * D + H], heads(ka[1]), heads(tA), ALU.mult)
                    done.wait(a1)
                    V.tensor_tensor(by_head(prod), by_head(rawsb), over_features(ka[2]), ALU.mult).then_inc(sm["scaled"], 1)
                if B:
                    dve.wait_ge(sm["ln"], t + 1)
                    b1 = done(V.tensor_tensor(kb[6], logs[:, CH:2 * CH], logs[:, 2 * CH:3 * CH], ALU.subtract))
                    done.wait(b1)
                    b1 = done(V.scalar_tensor_tensor(kb[6], kb[6], 0.5 / H, kb[4], ALU.mult, ALU.mult))
                if A:
                    dve.wait_ge(sm["scaled"], t + 1)
                    n = C - 1 if last_chunk else C
                    for c in range(n):
                        if c == 0 and first:
                            ins = V.tensor_copy(mine[:, 0, :], prod[:, 0, :])
                        else:
                            before = other[:, C - 1, :] if c == 0 else mine[:, c - 1, :]
                            ins = V.scalar_tensor_tensor(mine[:, c, :], before, cont[:, bass.ds(t * C + c, 1)], prod[:, c, :],
                                                         ALU.mult, ALU.add)
                        if c < n - 1:
                            done.wait(done(ins))
                    if last_chunk:
                        ins.then_inc(sm["chain_end"], 1)
                        dve.wait_ge(sm["carry"], 1)
                        dve.wait_ge(sm["head"], NCH)
                        V.tensor_tensor(mine[:, C - 1, :], headsum[:], bank[0][:, 0:MW], ALU.add).then_inc(sm["agg"], 1)
                    else:
                        ins.then_inc(sm["agg"], 1)
                if B:
                    done.wait(b1)
                    dve.wait_ge(sm["head"], t)
                    b1 = done(V.tensor_tensor(by_head(other), by_head(other), over_features(kb[6]), ALU.mult))
                    done.wait(b1)
                    V.tensor_reduce(upd, other[:, :, 0:H * D].rearrange("p c (h o) -> p c o h", o=D), AX.X, ALU.add) \
                        .then_inc(sm["upd"], 1)
                if A:
                    dve.wait_ge(sm["aggsq"], t + 1)
                    a1 = done(V.tensor_reduce(ka[4], sqa.rearrange("p c (h o) -> p (c h) o", o=D), AX.X, ALU.add))
                if B:
                    dve.wait_ge(sm["updsq"], t)
                    b1 = done(V.tensor_reduce(kc[2], updsq, AX.X, ALU.add))
                if A:
                    done.wait(a1)
                    a1 = done(V.tensor_scalar(sqB, ka[4], SQ_FLOOR, None, ALU.max))
                if B:
                    done.wait(b1)
                    b1 = done(V.tensor_scalar(sqC, kc[2], SQ_FLOOR, None, ALU.max))
                if A or B:
                    done.wait(b1 if B else a1)

            V.memset(squares, 1.0)
            V.memset(tanh_in, 1.0)
            V.memset(logs, 0.5)
            done.wait(done(V.memset(headsum[:], 0.0)))
            for c in range(C):
                masked(0, c)
            turn(0, 0, 0, stages="A", first=True)
            turn(0, 1, 1, stages="AB")
            start = done.n
            turn(1, 0, 2)
            per = done.n - start
            turn(1, 1, 3)
            with dve.Fori(2, NCH // 2) as i:
                for s in range(2):
                    done.restart(start + (2 * i + s - 2) * per)
                    turn(i, s, 2 * i + s)
                    assert done.n == per
            done.restart(start + (NCH - 3) * per)
            turn(NCH // 2, 0, NCH - 1, ahead=False, last_chunk=True)
            turn(NCH // 2, 1, NCH, stages="BC", ahead=False)
            turn(NCH // 2 + 1, 0, NCH + 1, stages="C", ahead=False)

        @block.sync
        def _(sp):
            sp.dma_start(nodes.rearrange("(a n) f -> a (n f)", a=16), x.rearrange("(a n) f -> a (n f)", a=16)) \
                .then_inc(s_nodes, 16)
            sp.wait_ge(s_pad, 5)
            for a, t in ((src, srci), (dst, dsti), (etype, eti)):
                body, tail = edges_view(a)
                sp.dma_start(t[0:full_rows, 0:EC], body).then_inc(s_in, 16)
                sp.dma_start(t[full_rows:P, 0:rest], tail).then_inc(s_in, 16)
            sp.dma_start(dnext[0:full_rows, :], dst[EC:EC + (full_rows - 1) * EC + 1:EC].rearrange("(p k) -> p k", k=1),
                         allow_slow_non_contiguous=True).then_inc(s_in, 16)
            sp.wait_ge(s_padv, 1)
            for half in range(2):
                sp.dma_start(avblk[D * half:D * half + D, R * H * half:R * H * half + R * H],
                             attn_vec.rearrange("r h d -> d (r h)"), allow_slow_non_contiguous=True).then_inc(s_in, 16)
            for r in range(R):
                sp.dma_start(relw[D * (r % 2):D * (r % 2) + D, r // 2, :].rearrange("p (h o) -> p h o", o=D),
                             rel_weight[r].rearrange("h i o -> i h o")).then_inc(s_in, 16)
            for l in range(3):
                for half in range(2):
                    q = slice(D * half, D * half + D)
                    sp.dma_start(wblk[q, l, D * half:D * half + D], w[l][:, :]).then_inc(s_in, 16)
                    sp.dma_start(bcol[q, l:l + 1], b[l].rearrange("(f k) -> f k", k=1)).then_inc(s_in, 16)

            def store_c(i, s):
                sp.wait_ge(s_rows[s], (i + 1) * (16 * C))
                sp.dma_start(slots_view(xslot)[:, bass.ds((2 * i + s) * C, C), :], rows[:, s, :, :]).then_inc(s_xst[s], 16)

            with sp.Fori(0, NCH // 2) as i:
                store_c(i, 0)
                store_c(i, 1)
            store_c(NCH // 2, 0)
            for s in range(2):
                sp.wait_ge(s_xst[s], 16 * (NCH // 2 + 1 - s))

            for L in range(3):
                layer_sp(sp, L)
            attention_sp(sp)

        @block.gpsimd
        def _(pool):
            nc.gpsimd.memset(srci[:], 0).then_inc(s_pad, 1)
            nc.gpsimd.memset(eti[:], 0).then_inc(s_pad, 1)
            nc.gpsimd.memset(dsti[:], N).then_inc(s_pad, 1)
            nc.gpsimd.memset(dnext[:], 2 * N).then_inc(s_pad, 1)
            nc.gpsimd.memset(ident[:], 0.0)
            nc.gpsimd.memset(below[:], 0.0)
            nc.gpsimd.memset(pairsel[:], 0.0)
            nc.gpsimd.iota(slotno[:], pattern=[[1, SC]], base=1, channel_multiplier=SC).then_inc(s_const, 1)
            pool.wait_ge(s_const, 1)
            nc.gpsimd.affine_select(out=ident[:], in_=ident[:], compare_op=ALU.not_equal, fill=1.0, base=0,
                                    pattern=[[-1, P]], channel_multiplier=1).then_inc(s_const, 1)
            nc.gpsimd.affine_select(out=below[:], in_=below[:], compare_op=ALU.is_ge, fill=1.0, base=0,
                                    pattern=[[-1, P]], channel_multiplier=1).then_inc(s_const, 1)
            nc.gpsimd.affine_select(out=pairsel[:].rearrange("r q (a f) -> r (q a) f", a=2),
                                    in_=pairsel[:].rearrange("r q (a f) -> r (q a) f", a=2), compare_op=ALU.not_equal,
                                    fill=1.0, base=0, pattern=[[-1, R], [0, D]], channel_multiplier=1).then_inc(s_const, 1)


            def stage(array, t, s):
                nc.gpsimd.tensor_copy(idxr[:, s, :], array[:, bass.ds(t * C, C)]).then_inc(s_idxr, 1)

            def gather(q, i, s, array, table_, width, bound, free, reverse, ring):
                k = 2 * i + s
                t = (NCH - 1) - k if reverse else k
                if q > 0 or not isinstance(i, int) or i > 0:
                    pool.wait_ge(s_rows[s], used(q, i, s) * (16 * C))
                stage(array, t, s)
                for semaphore, value in free(i, s):
                    pool.wait_ge(semaphore, value)
                pool.wait_ge(s_idxr, (q if q == 0 else q + 2) * NCH + k + 1)
                pool.sem_inc(s_turn, 1)
                for c in range(C):
                    pool.indirect_dma_start(out=ring[:, s, c, 0:width], out_offset=None, in_=table_[:, :],
                                            in_offset=bass.IndirectOffsetOnAxis(ap=idxr[:, s, c:c + 1], axis=0),
                                            bounds_check=bound, oob_is_err=False).then_inc(s_rows[s], 16)

            def gather_pass(q, array, table_, width, bound, free, reverse=False, ring=rows):
                gather(q, 0, 0, array, table_, width, bound, free, reverse, ring)
                gather(q, 0, 1, array, table_, width, bound, free, reverse, ring)
                with pool.Fori(1, NCH // 2) as i:
                    for s in range(2):
                        gather(q, i, s, array, table_, width, bound, free, reverse, ring)
                gather(q, NCH // 2, 0, array, table_, width, bound, free, reverse, ring)

            pool.wait_ge(s_idx, 1)
            gather_pass(0, idx_dst, x, XW, N - 1, lambda i, s: [] if isinstance(i, int) and i == 0 else [(s_xst[s], i * 16)])

            pool.wait_ge(s_idx, 2)
            pool.wait_ge(s_nodes, 16)
            for s in range(2):
                pool.wait_ge(s_rows[s], used(1, 0, s) * (16 * C))

            def scatter_map(i, s):
                k = 2 * i + s
                if not (isinstance(i, int) and i == 0):
                    pool.wait_ge(s_map[s], i * (16 * C))
                stage(idx_map, k, s)
                nc.gpsimd.tensor_copy(datar[:, s, :, :], slotdata[:, bass.ds(k * C, C), :]).then_inc(s_idxr, 1)
                pool.wait_ge(s_idxr, NCH + 2 * k + 2)
                pool.sem_inc(s_turn, 1)
                for c in range(C):
                    pool.indirect_dma_start(out=nodes.rearrange("n (a b) -> (n a) b", b=4),
                                            out_offset=bass.IndirectOffsetOnAxis(ap=idxr[:, s, c:c + 1], axis=0),
                                            in_=datar[:, s, c, :], in_offset=None,
                                            bounds_check=N * (XW // 4) - 1, oob_is_err=False).then_inc(s_map[s], 16)

            scatter_map(0, 0)
            scatter_map(0, 1)
            with pool.Fori(1, NCH // 2) as i:
                scatter_map(i, 0)
                scatter_map(i, 1)
            scatter_map(NCH // 2, 0)
            for s in range(2):
                pool.wait_ge(s_map[s], (NCH // 2 + 1 - s) * 16 * C)

            for L in range(3):
                if L == 0:
                    for s in range(2):
                        pool.wait_ge(s_xst[s], 16 * (NCH // 2 + 1 - s))
                else:
                    if L == 1:
                        pool.wait_ge(s_map_used, NCH)
                        dense_stored(pool)
                    for s in range(2):
                        pool.wait_ge(s_ust[s], dmas(L, 0, s))

                def free(i, s, L=L):
                    k = 2 * i + s
                    if L == 0 and isinstance(i, int) and i == 0:
                        return []
                    return [(sems_layer["used"], at_turn(L, k) - 1)]

                if L == 0:
                    gather_pass(1, srci, nodes, XW, N - 1, free)
                else:
                    gather_pass(1 + L, row_of_src, table[L], D, ROWS - 1, free)
            attention_pool(pool, gather_pass, stage)

        layer_base = [0, 0, 0, 0]

        def layer_dve(dve, L):
            sl = sems_layer
            done = Marks(dve, sl["step"])
            V = nc.vector

            def norm_first(i, s):
                t = 2 * i + s
                g, own = rows[:, s, :, 0:D], selfr[:, s, :, 0:D]
                dve.wait_ge(s_rows[s], (used(1, i, s) + 1) * (16 * C))
                dve.wait_ge(s_self[s], dmas(0, i + 1, s))
                m1 = done(V.tensor_reduce(lns[:, 0, 0:C, 0], g, AX.X, ALU.add))
                m2 = done(V.tensor_reduce(lns[:, 0, C:2 * C, 0], own, AX.X, ALU.add))
                done.wait(m1)
                V.scalar_tensor_tensor(lnc[:, 0, 0:C, :], bc(lns[:, 0, 0:C, :], [P, C, D]), -1.0 / D, g, ALU.mult, ALU.add)
                done.wait(m2)
                V.scalar_tensor_tensor(lnc[:, 0, C:2 * C, :], bc(lns[:, 0, C:2 * C, :], [P, C, D]), -1.0 / D,
                                       own, ALU.mult, ALU.add).then_inc(sl["xc1"], 1)

            def norm_second(i, s):
                t = 2 * i + s
                cols = bass.ds(t * C, C)
                v = rows[:, s, :, D]
                m = done(V.scalar_tensor_tensor(tmp[:, 0:C], v, 0.0, srcf[:, cols], ALU.is_equal, ALU.mult))
                dve.wait_ge(sl["sq1"], t + 1)
                V.tensor_reduce(lnv[:, 0, :, 0], lnq[:, 0, :, :], AX.X, ALU.add).then_inc(sl["var1"], 1)
                done.wait(m)
                m = done(V.scalar_tensor_tensor(tmp[:, 0:C], tmp[:, 0:C], -1.0, v, ALU.add, ALU.add))
                done.wait(m)
                V.tensor_copy(row_of_src[:, cols], tmp[:, 0:C]).then_inc(s_map_used, 1)

            def norm_third(i, s):
                t = 2 * i + s
                dve.wait_ge(sl["std1"], t + 1)
                m = done(V.reciprocal(lnr[:, 0, :, 0], lnd[:, 0, :, 0]))
                done.wait(m)
                m1 = done(V.scalar_tensor_tensor(lnr[:, 0, 0:C, 0], rows[:, s, :, D + 1], 1.0, lnr[:, 0, 0:C, 0],
                                                 ALU.add, ALU.mult))
                m2 = done(V.tensor_tensor(lnr[:, 0, C:2 * C, 0], dis[:, bass.ds(t * C, C)], lnr[:, 0, C:2 * C, 0], ALU.mult))
                done.wait(m1)
                V.scalar_tensor_tensor(g_in[:, :, 1:].rearrange("p f c -> p c f"), lnc[:, 0, 0:C, :], 0.0,
                                       bc(lnr[:, 0, 0:C, :], [P, C, D]), ALU.max, ALU.mult).then_inc(sl["used"], 1)
                done.wait(m2)
                m = done(V.scalar_tensor_tensor(h0[:, C:2 * C, :], lnc[:, 0, C:2 * C, :], 0.0,
                                                bc(lnr[:, 0, C:2 * C, :], [P, C, D]), ALU.max, ALU.mult))
                done.wait(m)
                dve.wait_ge(sl["used"], t + 1)

            def running_sum(i, s, last_chunk=False):
                t = 2 * i + s
                n = at_turn(L, t)
                dve.wait_ge(sl["tiled"], n + 1)
                if not (isinstance(n, int) and n == 0):
                    dve.wait_ge(sl["head"], n)
                V.tensor_tensor_scan(scan_sum, scan_cont, scan_g, 0.0, ALU.mult, ALU.add).then_inc(sl["chain"], 1)
                dve.wait_ge(sl["chain"], n + 1)
                if last_chunk:
                    V.tensor_copy(last[:], sums[:, :, C - 1]).then_inc(sl["last"], 1)
                    dve.wait_ge(sl["carry"], L + 1)
                    m = done(V.tensor_copy(sums[:, :, C], bank[6][:, 0:D]))
                    done.wait(m)
                else:
                    done(V.tensor_copy(g_in[:, :, 0], sums[:, :, C]))

            def layer_input(i, s):
                t = 2 * i + s
                n = at_turn(L, t)
                own = h0[:, C:2 * C, :] if L == 0 else selfr[:, s, :, 0:D]
                if L > 0:
                    dve.wait_ge(s_self[s], dmas(L, i + 1, s))
                if L > 0 or not (isinstance(t, int) and t == 0):
                    dve.wait_ge(sl["t_ps"], n)
                m = done(V.tensor_tensor(zbuf[:], sums[:, :, 1:].rearrange("p f c -> p c f"), own, ALU.add))
                done.wait(m)
                if L > 0:
                    dve.sem_inc(sl["used"], 1)
                db = dis[:, bass.ds(t * C, C)].rearrange("p (c k) -> p c k", k=1)
                V.tensor_tensor(zbuf[:], zbuf[:], bc(db, [P, C, D]), ALU.mult).then_inc(sl["z"], 1)

            def rows_first(i, s):
                t = 2 * i + s
                n = at_turn(L, t)
                back = bank[4][:].rearrange("p (c f) -> p c f", f=D)
                dve.wait_ge(sl["back"], n + 1)
                if L > 0 or not (isinstance(i, int) and i == 0):
                    dve.wait_ge(s_ust[s], dmas(L, i, s))
                if L < 2:
                    db = dis[:, bass.ds(t * C, C)].rearrange("p (c k) -> p c k", k=1)
                    V.tensor_tensor(o1[:, s, :, :], back, bc(db, [P, C, D]), ALU.mult).then_inc(sl["u"], 1)
                    return
                V.tensor_tensor(ox[:, s, :, :], back, xd[:, s, :, 0:D], ALU.add).then_inc(sl["u"], 1)
                dve.wait_ge(sl["u"], n + 1)
                m = done(V.tensor_reduce(lns[:, 1, 0:C, 0], ox[:, s, :, :], AX.X, ALU.add))
                done.wait(m)
                V.scalar_tensor_tensor(lnc[:, 1, 0:C, :], bc(lns[:, 1, 0:C, :], [P, C, D]), -1.0 / D,
                                       ox[:, s, :, :], ALU.mult, ALU.add).then_inc(sl["xc2"], 1)
                dve.wait_ge(sl["sq2"], t + 1)
                V.tensor_reduce(lnv[:, 1, 0:C, 0], lnq[:, 1, 0:C, :], AX.X, ALU.add).then_inc(sl["var2"], 1)

            def rows_second(i, s):
                t = 2 * i + s
                dve.wait_ge(sl["std2"], t + 1)
                m = done(V.reciprocal(lnr[:, 1, 0:C, 0], lnd[:, 1, 0:C, 0]))
                done.wait(m)
                V.scalar_tensor_tensor(o3[:, s, :, :], lnc[:, 1, 0:C, :], 0.0, bc(lnr[:, 1, 0:C, :], [P, C, D]),
                                       ALU.max, ALU.mult).then_inc(sl["o3"], 1)

            def turn(i, s, before=True, after=True):
                behind, ahead = (i + s - 1, 1 - s), (i + s, 1 - s)
                if L == 0:
                    if after:
                        norm_first(*ahead)
                    running_sum(i, s, last_chunk=not after)
                    layer_input(i, s)
                    if after:
                        norm_second(*ahead)
                    if before:
                        rows_first(*behind)
                    if after:
                        norm_third(*ahead)
                else:
                    if before:
                        rows_first(*behind)
                    running_sum(i, s, last_chunk=not after)
                    layer_input(i, s)
                    if before and L == 2:
                        rows_second(*behind)

            base = layer_base[L]
            done.restart(base)
            if L == 0:
                V.memset(scan_cont, 0.0)
            m = done(V.memset(scan_g, 0.0))
            done.wait(m)
            dve.sem_inc(sl["ready"], 1)
            if L == 0:
                norm_first(0, 0)
                norm_second(0, 0)
                norm_third(0, 0)
            turn(0, 0, before=False)
            turn(0, 1)
            start = done.n
            done.restart(base + start)
            turn(1, 0)
            per = done.n
            turn(1, 1)
            with dve.Fori(2, NCH // 2) as i:
                for s in range(2):
                    done.restart(base + start + (2 * i + s - 2) * per)
                    turn(i, s)
                    assert done.n == per
            done.restart(base + start + (NCH - 3) * per)
            turn(NCH // 2, 0, after=False)
            rows_first(NCH // 2, 0)
            if L == 2:
                rows_second(NCH // 2, 0)
            layer_base[L + 1] = done.base + done.n

        prep_counts = {}

        def link_small(dve):
            return Steps(dve, s_prep)

        def prep_dve(dve):
            link = link_small(dve)
            nc.vector.memset(wblk[:], 0.0).then_inc(s_pad, 1)
            nc.vector.memset(avblk[:], 0.0).then_inc(s_padv, 1)
            nc.vector.memset(ones[:], 1.0)
            nc.vector.memset(ex4[:], 0.0)
            nc.vector.memset(hdb[:], 0.0)
            nc.vector.memset(score[:], 0.0)
            nc.vector.memset(epsln[:], 1e-5)
            nc.vector.memset(head[:], 0.0)
            nc.vector.memset(slotdata[:], 0.0)
            link(nc.vector.memset(cont[:], 0.0))
            dve.wait_ge(s_in, 16 * (6 + 1 + 2 + R + 12))
            dve.wait_ge(s_const, 4)
            nc.vector.tensor_copy(dstf[:], dsti[:])
            nc.vector.tensor_copy(srcf[:], srci[:])
            nc.vector.tensor_copy(etf[:], eti[:])
            nc.vector.tensor_copy(identb[:], ident[:])
            link(nc.vector.tensor_copy(dnextf[:], dnext[:]))
            link(nc.vector.tensor_copy(dstf[:, EC:SC], dstf[:, 0:1]))
            link(nc.vector.tensor_scalar(tmp[:], dstf[:], float(N - 1), None, ALU.min))
            nc.vector.tensor_copy(idx_dst[:], tmp[:]).then_inc(s_idx, 1)
            dve.wait_ge(s_idx, 1)
            nc.vector.tensor_tensor(cont[:, 1:EC], dstf[:, 1:EC], dstf[:, 0:EC - 1], ALU.is_equal)
            nc.vector.tensor_tensor(ends[:, 0:EC - 1], dstf[:, 1:EC], dstf[:, 0:EC - 1], ALU.not_equal)
            link(nc.vector.tensor_tensor(ends[:, EC - 1:EC], dstf[:, EC - 1:EC], dnextf[:], ALU.not_equal))
            link(nc.vector.tensor_scalar(head[:, 0:EC], dstf[:, 0:EC], dstf[:, 0:1], None, ALU.is_equal))
            link(nc.vector.tensor_tensor(headend[:, 0:EC], head[:, 0:EC], ends[:, 0:EC], ALU.mult))
            link(nc.vector.tensor_tensor(owns[:, 0:EC], ends[:, 0:EC], headend[:, 0:EC], ALU.subtract))
            link(nc.vector.tensor_reduce(owns[:, EC:SC], headend[:, 0:EC], AX.X, ALU.max))
            nc.vector.memset(headend[:, EC:SC], 0.0)
            link(nc.vector.tensor_scalar(tmp[:, 0:EC], ends[:, 0:EC], -1.0, 1.0, ALU.mult, ALU.add))
            link(nc.vector.tensor_scalar(tmp2[:, 0:EC], head[:, 0:EC], -1.0, 1.0, ALU.mult, ALU.add))
            link(nc.vector.memset(goes[:], 0.0))
            link(nc.vector.tensor_tensor(goes[:, 0:EC], tmp[:, 0:EC], tmp2[:, 0:EC], ALU.mult))
            link(nc.vector.tensor_scalar(diag[:], ident[:], dstf[:, 0:1], None, ALU.mult))
            nc.vector.tensor_scalar(tmp2[:, 0:1], dstf[:, EC - 1:EC], 1.0, None, ALU.mult).then_inc(s_prepdiag, 1)
            dve.wait_ge(s_prepdiag, 1)
            dve.wait_ge(s_preppe, 1)
            link(nc.vector.tensor_scalar(carrym[:], bank[0][:, 0:P], dstf[:, EC - 1:EC], None, ALU.is_equal))
            link(nc.vector.tensor_tensor(carrym[:], carrym[:], below[:], ALU.mult))
            nc.vector.memset(tmp[:], 1.0).then_inc(s_prepdiag, 1)
            dve.wait_ge(s_prepdiag, 2)
            dve.wait_ge(s_preppe, 2)
            link(nc.vector.tensor_copy(carryt[:], bank[1][:, 0:P]))
            link(nc.vector.tensor_tensor_scan(cnt[:, 0:EC], cont[:, 0:EC], tmp[:, 0:EC], 0.0, ALU.mult, ALU.add))
            link(nc.vector.tensor_tensor(tmp2[:, 0:EC], headend[:, 0:EC], cnt[:, 0:EC], ALU.mult))
            link(nc.vector.tensor_reduce(cnt[:, EC:SC], tmp2[:, 0:EC], AX.X, ALU.add))
            nc.vector.tensor_scalar(tmp2[:, 0:1], cnt[:, EC - 1:EC], 1.0, None, ALU.mult).then_inc(s_prepdiag, 1)
            dve.wait_ge(s_prepdiag, 3)
            dve.wait_ge(s_preppe, 3)
            link(nc.vector.tensor_tensor(cnt[:, EC:SC], cnt[:, EC:SC], bank[0][:, P:P + 1], ALU.add))
            nc.vector.tensor_scalar(tmp[:], cnt[:], 1.0, None, ALU.add).then_inc(s_prepdiag, 1)
            dve.wait_ge(s_prepact, 1)
            link(nc.vector.reciprocal(dis[:], tmp2[:]))
            nc.vector.tensor_copy(slotdata[:, :, 0], slotno[:])
            link(nc.vector.tensor_scalar(slotdata[:, :, 1], dis[:], -1.0, None, ALU.add))
            link(nc.vector.tensor_scalar(tmp[:], dstf[:], float(XW // 4), float(D // 4) - OUTSIDE, ALU.mult, ALU.add))
            link(nc.vector.tensor_tensor(tmp[:], tmp[:], owns[:], ALU.mult))
            link(nc.vector.tensor_scalar(idx_map[:], tmp[:], OUTSIDE, None, ALU.add))
            link(nc.vector.scalar_tensor_tensor(tmp[:], dstf[:], -OUTSIDE, owns[:], ALU.add, ALU.mult))
            nc.vector.tensor_scalar(idx_out[:], tmp[:], OUTSIDE, None, ALU.add).then_inc(s_idx, 1)
            for r in range(R):
                nc.vector.tensor_scalar(onehot[:, :, r], etf[:], float(r), None, ALU.is_equal)
            link(nc.vector.tensor_scalar(srcf[:], srcf[:], float(SLOTS + 1), None, ALU.add))

        @block.vector
        def _(dve):
            prep_dve(dve)
            link = Steps(dve, sems_dense["step"])
            sd = sems_dense

            def half(buf, a):
                return buf[:, C * a:C * a + C, :]

            def from_bank(n):
                return bank[n][:].rearrange("p (c f) -> p c f", f=D)

            def normalised_in(i, u):
                xk = dense_x[u][:, :, 0:D]
                dve.wait_ge(s_xd[u], (i // 3 + 1 if isinstance(i, int) else j_of(i, u)) * 16)
                link(nc.vector.tensor_reduce(lns[:, 0, :, 0], xk, AX.X, ALU.add))
                nc.vector.scalar_tensor_tensor(lnc[:, 0, :, :], bc(lns[:, 0, :, :], [P, DC, D]), -1.0 / D, xk,
                                               ALU.mult, ALU.add).then_inc(sd["xc1"], 1)

            def variance_in(i):
                dve.wait_ge(sd["sq1"], i + 1)
                nc.vector.tensor_reduce(lnv[:, 0, :, 0], lnq[:, 0, :, :], AX.X, ALU.add).then_inc(sd["var1"], 1)

            def hidden_in(i):
                dve.wait_ge(sd["std1"], i + 1)
                link(nc.vector.reciprocal(lnr[:, 0, :, 0], lnd[:, 0, :, 0]))
                if not (isinstance(i, int) and i == 0):
                    dve.wait_ge(sd["z"], 8 * i - 6)
                nc.vector.scalar_tensor_tensor(h0[:], lnc[:, 0, :, :], 0.0, bc(lnr[:, 0, :, :], [P, DC, D]),
                                               ALU.max, ALU.mult).then_inc(sd["h0"], 1)

            loads = [0]

            def j_of(i, u):
                return loads[0] + 1

            def turn(i, u, before=True, here=True, after=True):
                if before:
                    if not (isinstance(i, int) and i < 2):
                        dve.wait_ge(s_dst3, (i - 1) * 32)
                    for a in range(2):
                        dve.wait_ge(sd["b3"], 2 * i - 1 + a)
                        nc.vector.tensor_tensor(half(dx, a), from_bank(6 + a), half(dense_x[(u + 2) % 3], a)[:, :, 0:D],
                                                ALU.add).then_inc(sd["x1"], 1)
                    dve.wait_ge(sd["x1"], 2 * i)
                    link(nc.vector.tensor_reduce(lns[:, 1, :, 0], dx, AX.X, ALU.add))
                    nc.vector.scalar_tensor_tensor(lnc[:, 1, :, :], bc(lns[:, 1, :, :], [P, DC, D]), -1.0 / D, dx,
                                                   ALU.mult, ALU.add).then_inc(sd["xc2"], 1)
                if after:
                    normalised_in(i + 1, (u + 1) % 3)
                if before:
                    dve.wait_ge(sd["sq2"], i)
                    nc.vector.tensor_reduce(lnv[:, 1, :, 0], lnq[:, 1, :, :], AX.X, ALU.add).then_inc(sd["var2"], 1)
                if after:
                    variance_in(i + 1)
                if here:
                    if not (isinstance(i, int) and i == 0):
                        dve.wait_ge(s_dst1, i * 16)
                    for a in range(2):
                        dve.wait_ge(sd["b1"], 2 * i + a + 1)
                        nc.vector.tensor_copy(half(d1, a), from_bank(2 + a)).then_inc(sd["o1"], 1)
                if before:
                    dve.wait_ge(sd["std2"], i)
                    link(nc.vector.reciprocal(lnr[:, 1, :, 0], lnd[:, 1, :, 0]))
                    nc.vector.scalar_tensor_tensor(d3, lnc[:, 1, :, :], 0.0, bc(lnr[:, 1, :, :], [P, DC, D]),
                                                   ALU.max, ALU.mult).then_inc(sd["o3"], 1)
                if after:
                    hidden_in(i + 1)

            link.restart(0)
            normalised_in(0, 0)
            variance_in(0)
            hidden_in(0)
            turn(0, 0, before=False)
            start = link.n
            turn(1, 1)
            per = link.n - start
            turn(2, 2)
            with dve.Fori(1, ND // 3) as j:
                for u in range(3):
                    link.restart(start + (3 * j + u - 1) * per)
                    loads[0] = j + (u + 1) // 3
                    turn(3 * j + u, u)
                    assert link.n == per
            link.restart(start + (ND - 2) * per)
            turn(ND - 1, (ND - 1) % 3, after=False)
            turn(ND, ND % 3, here=False, after=False)
            dense_stored(dve)
            for L in range(3):
                layer_dve(dve, L)
            score_dve(dve)
            message_dve(dve)

        @block.scalar
        def _(act):
            act.wait_ge(s_prepdiag, 4)
            nc.scalar.activation(tmp2[:], tmp[:], ACT.Sqrt).then_inc(s_prepact, 1)
            sd = sems_dense

            def load(i, u):
                pp = LASTP if isinstance(i, int) and i == ND - 1 else P
                act.dma_start(dense_x[u][0:pp, :, :], dense_at(x, 0, i)).then_inc(s_xd[u], 16)

            def hidden(i, m):
                l, a = m // 2, m % 2
                act.wait_ge(sd["z"], 8 * i + m + 1)
                if l == 0:
                    nc.scalar.copy(hT[:, 2 * a, :], bank[a][:]).then_inc(sd["hT"], 1)
                else:
                    nc.scalar.activation(hT[:, 2 * a + l % 2, :], bank[a][:], ACT.Relu, bias=bcol[:, l - 1:l]) \
                        .then_inc(sd["hT"], 1)

            def squares_of(i, n):
                act.wait_ge(sd[f"xc{n + 1}"], i + 1)
                nc.scalar.activation(lnq[:, n, :, :], lnc[:, n, :, :], ACT.Square).then_inc(sd[f"sq{n + 1}"], 1)

            def deviation_of(i, n):
                act.wait_ge(sd[f"var{n + 1}"], i + 1)
                nc.scalar.activation(lnd[:, n, :, 0], lnv[:, n, :, 0], ACT.Sqrt, bias=epsln[:], scale=1.0 / D) \
                    .then_inc(sd[f"std{n + 1}"], 1)

            def rows2(i, a):
                act.wait_ge(sd["b2"], 2 * i + a + 1)
                if a == 0 and not (isinstance(i, int) and i == 0):
                    act.wait_ge(s_dst2, 16 * i)
                nc.scalar.copy(d2[:, C * a:C * a + C, :], bank[4 + a][:].rearrange("p (c f) -> p c f", f=D)) \
                    .then_inc(sd["o2"], 1)

            def store(i, rows_, tgt, base, done):
                pp = LASTP if isinstance(i, int) and i == ND - 1 else P
                act.dma_start(dense_at(tgt, base, i), rows_[0:pp, :, :]).then_inc(done, 16)

            def turn(i, u, before=True, here=True, after=True, loads=True):
                if here:
                    for m in range(4):
                        hidden(i, m)
                if before:
                    squares_of(i - 1, 1)
                    store(i - 1, dx, out, 0, s_dst3)
                if loads:
                    load(i + 2, (u + 2) % 3)
                if here:
                    hidden(i, 4)
                if after:
                    squares_of(i + 1, 0)
                if before:
                    deviation_of(i - 1, 1)
                if here:
                    hidden(i, 5)
                if after:
                    deviation_of(i + 1, 0)
                if here:
                    act.wait_ge(sd["o1"], 2 * i + 2)
                    store(i, d1, table[1], SLOTS, s_dst1)
                    hidden(i, 6)
                    rows2(i, 0)
                    hidden(i, 7)
                    rows2(i, 1)
                if before:
                    act.wait_ge(sd["o3"], i)
                    store(i - 1, d3, table[3], SLOTS, s_dst3)
                if here:
                    act.wait_ge(sd["o2"], 2 * i + 2)
                    store(i, d2, table[2], SLOTS, s_dst2)

            load(0, 0)
            load(1, 1)
            squares_of(0, 0)
            deviation_of(0, 0)
            turn(0, 0, before=False)
            turn(1, 1)
            turn(2, 2)
            with act.Fori(1, ND // 3 - 1) as j:
                for u in range(3):
                    turn(3 * j + u, u)
            for i in range(3 * (ND // 3 - 1), ND):
                turn(i, i % 3, after=i < ND - 1, loads=i + 2 < ND)
            turn(ND, ND % 3, here=False, after=False, loads=False)

            sl = sems_layer
            for L in range(3):
                def operands(i, s):
                    t = 2 * i + s
                    n = at_turn(L, t)
                    if isinstance(t, int) and t == 0:
                        act.wait_ge(sl["ready"], L + 1)
                    else:
                        act.wait_ge(sl["chain"], n)
                    flags = cont[:, bass.ds(t * C, C)].rearrange("p (k c) -> p k c", k=1).broadcast_to([P, D, C])
                    ins = nc.scalar.copy(cont_in[:, :, 1:], flags)
                    if L > 0:
                        act.wait_ge(s_rows[s], (used(1 + L, i, s) + 1) * (16 * C))
                        ins = nc.scalar.copy(g_in[:, :, 1:].rearrange("p f c -> p c f"), rows[:, s, :, 0:D])
                    ins.then_inc(sl["tiled"], 1)

                def head_part(t):
                    n = at_turn(L, t)
                    act.wait_ge(sl["chain"], n + 1)
                    if not (isinstance(n, int) and n == 0):
                        act.wait_ge(sl["head_added"], n)
                    for c in range(C):
                        ins = nc.scalar.activation(agghead[:, c, :], sums[:, :, 1 + c], ACT.Copy,
                                                   scale=headend[:, bass.ds(t * C + c, 1)])
                    ins.then_inc(sl["head"], 1)

                def through_layer(t, between=None):
                    n = at_turn(L, t)
                    act.wait_ge(sl["t_ps"], n + 1)
                    nc.scalar.copy(hT[:, 0, :], bank[0][:]).then_inc(sl["t"], 1)
                    if between:
                        between()
                    act.wait_ge(sl["mm"], n + 1)
                    nc.scalar.activation(hT[:, 1, :], bank[1][:], ACT.Relu, bias=bcol[:, L:L + 1]).then_inc(sl["relu"], 1)

                def squares_of(t, which):
                    act.wait_ge(sl[f"xc{which + 1}"], t + 1)
                    m = C if which else 2 * C
                    nc.scalar.activation(lnq[:, which, 0:m, :], lnc[:, which, 0:m, :], ACT.Square) \
                        .then_inc(sl[f"sq{which + 1}"], 1)

                def deviation_of(t, which):
                    act.wait_ge(sl[f"var{which + 1}"], t + 1)
                    m = C if which else 2 * C
                    nc.scalar.activation(lnd[:, which, 0:m, 0], lnv[:, which, 0:m, 0], ACT.Sqrt, bias=epsln[:],
                                         scale=1.0 / D).then_inc(sl[f"std{which + 1}"], 1)

                def layer_turn(i, s, before=True, after=True):
                    t = 2 * i + s
                    if L == 2 and before:
                        squares_of(t - 1, 1)
                        deviation_of(t - 1, 1)
                    operands(i, s)
                    if L == 0 and after:
                        squares_of(t + 1, 0)
                    head_part(t)
                    through_layer(t, (lambda: deviation_of(t + 1, 0)) if L == 0 and after else None)

                if L == 0:
                    squares_of(0, 0)
                    deviation_of(0, 0)
                layer_turn(0, 0, before=False)
                layer_turn(0, 1)
                with act.Fori(1, NCH // 2) as i:
                    layer_turn(i, 0)
                    layer_turn(i, 1)
                layer_turn(NCH // 2, 0, after=False)
                if L == 2:
                    squares_of(NCH - 1, 1)
                    deviation_of(NCH - 1, 1)

            score_act(act)
            message_act(act)

        @block.tensor
        def _(pe):
            pe.wait_ge(s_prepdiag, 1)
            nc.tensor.matmul(bank[0][:, 0:P], ones[:], diag[:], start=True, stop=True).then_inc(s_preppe, 1)
            pe.wait_ge(s_prepdiag, 2)
            nc.tensor.transpose(bank[1][:, 0:P], carrym[:], ident[:]).then_inc(s_preppe, 1)
            pe.wait_ge(s_prepdiag, 3)
            nc.tensor.matmul(bank[0][:, P:P + 1], carrym[:], tmp2[:, 0:1], start=True, stop=True).then_inc(s_preppe, 1)
            sd = sems_dense

            def transposes(bank_, source):
                for q in range(4):
                    ins = nc.tensor.transpose(bank_[:, q * P:(q + 1) * P], source(q), ident[:])
                return ins

            def dense_layers(i, first=False):
                pe.wait_ge(sd["h0"], i + 1)
                if first:
                    pe.wait_ge(s_prepdiag, 4)
                    pe.wait_ge(s_prepact, 1)
                for a in range(2):
                    transposes(bank[a], lambda q: h0[:, C * a + 2 * q:C * a + 2 * q + 2, :].rearrange("p c f -> p (c f)")) \
                        .then_inc(sd["z"], 1)
                for l in range(4):
                    for a in range(2):
                        now = hT[:, 2 * a + l % 2, :]
                        pe.wait_ge(sd["hT"], 8 * i + 2 * l + a + 1)
                        if l < 3:
                            nc.tensor.matmul(bank[a][:], wblk[:, l, :], now, start=True, stop=True).then_inc(sd["z"], 1)
                        if l > 0:
                            if not first:
                                pe.wait_ge(sd[("o1", "o2", "x1")[l - 1]], 2 * i - 1 + a)
                            transposes(bank[2 * l + a], lambda q: now[:, q * P:(q + 1) * P]).then_inc(sd[f"b{l}"], 1)

            dense_layers(0, first=True)
            with pe.Fori(1, ND) as i:
                dense_layers(i)

            sl = sems_layer
            for L in range(3):
                def layer_b(t, first_chunk=False, last_chunk=False):
                    n = at_turn(L, t)

                    def add_heads():
                        pe.wait_ge(sl["head"], n + 1)
                        for c in range(C):
                            ins = nc.tensor.matmul(bank[6][:, 0:D], ident[:], agghead[:, c, :],
                                                   start=first_chunk and c == 0, stop=False)
                        ins.then_inc(sl["head_added"], 1)

                    if last_chunk:
                        add_heads()
                        pe.wait_ge(sl["last"], L + 1)
                        nc.tensor.matmul(bank[6][:, 0:D], carrym[:], last[:], start=False, stop=True) \
                            .then_inc(sl["carry"], 1)
                    pe.wait_ge(sl["z"], n + 1)
                    transposes(bank[0], lambda q: zbuf[:, 2 * q:2 * q + 2, :].rearrange("p c f -> p (c f)")) \
                        .then_inc(sl["t_ps"], 1)
                    if not last_chunk:
                        add_heads()
                    pe.wait_ge(sl["t"], n + 1)
                    nc.tensor.matmul(bank[1][:], wblk[:, L, :], hT[:, 0, :], start=True, stop=True).then_inc(sl["mm"], 1)
                    pe.wait_ge(sl["relu"], n + 1)
                    if not (isinstance(n, int) and n == 0):
                        pe.wait_ge(sl["u"], n)
                    transposes(bank[4], lambda q: hT[:, 1, q * P:(q + 1) * P]).then_inc(sl["back"], 1)

                layer_b(0, first_chunk=True)
                with pe.Fori(1, NCH - 1) as t:
                    layer_b(t)
                layer_b(NCH - 1, last_chunk=True)
            score_pe(pe)
            message_pe(pe)


def kernel(x, src, dst, edge_type_8, L0_gnn_W0, L0_gnn_b0, L0_gnn_W1, L0_gnn_b1, L0_gnn_W2, L0_gnn_b2,
           L1_gnn_rel_weight, L1_gnn_attn_vec, L1_gnn_rel_emb):
    import concourse.bacc as bacc
    from concourse.bass_utils import run_bass_kernel_spmd

    nc = bacc.Bacc("TRN2", target_bir_lowering=False, num_devices=1)
    arrays, aps = {}, {}

    def given(name, a):
        a = np.ascontiguousarray(a)
        arrays[name] = a
        aps[name] = nc.dram_tensor(name, a.shape, mybir.dt.from_np(a.dtype), kind="ExternalInput").ap()
        return aps[name]

    padded = np.zeros((N, XW), np.float32)
    padded[:, :D] = x
    args = [given("x_in", padded), given("src_in", src), given("dst_in", dst), given("etype_in", edge_type_8),
            [given("w0", L0_gnn_W0), given("w1", L0_gnn_W1), given("w2", L0_gnn_W2)],
            [given("b0", L0_gnn_b0), given("b1", L0_gnn_b1), given("b2", L0_gnn_b2)],
            given("rel_weight", L1_gnn_rel_weight), given("attn_vec", L1_gnn_attn_vec)]
    out = nc.dram_tensor("out", (N, D), F32, kind="ExternalOutput").ap()
    build(nc, *args, out)
    got = run_bass_kernel_spmd(nc, [arrays], core_ids=[0])
    return got.results[0]["out"]
```

```python
from contextlib import ExitStack

import numpy as np
import concourse.bass as bass
from concourse import mybir

F32 = mybir.dt.float32
BF16 = mybir.dt.bfloat16
I32 = mybir.dt.int32
ALU = mybir.AluOpType
ACT = mybir.ActivationFunctionType
AX = mybir.AxisListType

P = 128
N, E, D, R, H = 100000, 50000, 64, 8, 4
C = 8
EC = -(-E // P)
SC = -(-(EC + 1) // C) * C
assert SC == EC + 1
NCH = SC // C
SLOTS = P * SC
ROWS = SLOTS + N
XW = D + 4
DC = 2 * C
NB = DC * P
ND = -(-N // NB)
PARTS = NCH // 2 + 1
assert N % (16 * PARTS) == 0
LASTP = (N - (ND - 1) * NB) // DC
assert (ND - 4) % 3 == 0 and LASTP * DC == N - (ND - 1) * NB
OUTSIDE = float(1 << 23)
MW = H * D + 2 * H
CURV, MIN_NORM, EPS = 0.01, 1e-10, 1e-6
MAXNORM = (1.0 - 1e-5) / 0.1
SQ_FLOOR = 1e-19


def build(nc, x, src, dst, etype, w, b, rel_weight, attn_vec, out):
    with ExitStack() as ctx:
        def sb(name, shape, dt=F32):
            return ctx.enter_context(nc.sbuf_tensor(name, shape, dt))

        def psum(name, shape, dt=F32):
            return ctx.enter_context(nc.psum_tensor(name, shape, dt))

        def sem(name):
            return ctx.enter_context(nc.semaphore(name))

        def dram(name, shape):
            return nc.dram_tensor(name, shape, F32).ap()

        nodes = dram("nodes", (N, XW))
        xslot = dram("xslot", (SLOTS, XW))
        table = [None, dram("table1", (ROWS, D)), dram("table2", (ROWS, D)), dram("table3", (ROWS, D))]
        x1slot = dram("x1slot", (SLOTS, D))
        hsrc = dram("hsrc", (SLOTS, D))
        msums = dram("msums", (SLOTS, MW))

        ident = sb("ident", [P, P])
        identb = sb("identb", [P, P], BF16)
        below = sb("below", [P, P])
        ones = sb("ones", [P, P])
        diag = sb("diag", [P, P])
        carrym = sb("carrym", [P, P])
        carryt = sb("carryt", [P, P])
        pen = sb("pen", [P, P])
        wblk = sb("wblk", [P, 3, P])
        bcol = sb("bcol", [P, 3])
        relw = sb("relw", [P, 4, H * D])
        avblk = sb("avblk", [P, 2 * R * H])
        epsln = sb("epsln", [P, 1])
        srci = sb("srci", [P, SC], I32)
        dsti = sb("dsti", [P, SC], I32)
        eti = sb("eti", [P, SC], I32)
        dnext = sb("dnext", [P, 1], I32)
        slotno = sb("slotno", [P, SC], I32)
        srcf = sb("srcf", [P, SC])
        dstf = sb("dstf", [P, SC])
        etf = sb("etf", [P, SC])
        dnextf = sb("dnextf", [P, 1])
        onehot = sb("onehot", [P, SC, R], BF16)
        cont = sb("cont", [P, SC])
        ends = sb("ends", [P, SC])
        head = sb("head", [P, SC])
        headend = sb("headend", [P, SC])
        owns = sb("owns", [P, SC])
        goes = sb("goes", [P, SC])
        cnt = sb("cnt", [P, SC])
        dis = sb("dis", [P, SC])
        tmp = sb("tmp", [P, SC])
        tmp2 = sb("tmp2", [P, SC])
        slotdata = sb("slotdata", [P, SC, 4])
        idx_dst = sb("idx_dst", [P, SC], I32)
        idx_map = sb("idx_map", [P, SC], I32)
        idx_out = sb("idx_out", [P, SC], I32)
        row_of_src = sb("row_of_src", [P, SC], I32)
        headsum = sb("headsum", [P, MW])
        idx_head = sb("idx_head", [P, 1], I32)
        hpart = sb("hpart", [P, 2])
        idxr = sb("idxr", [P, 2, C], I32)
        datar = sb("datar", [P, 2, C, 4])
        rows = sb("rows", [P, 2, C, XW])
        rows64 = rows[:].rearrange("p v c f -> p (v c f)")[:, 0:2 * C * D].rearrange("p (v c f) -> p v c f", v=2, f=D)
        xd = sb("xd", [P, 4, C, XW])
        lns = sb("lns", [P, 2, 2 * C, 1])
        lnc = sb("lnc", [P, 2, 2 * C, D])
        lnq = sb("lnq", [P, 2, 2 * C, D])
        lnv = sb("lnv", [P, 2, 2 * C, 1])
        lnd = sb("lnd", [P, 2, 2 * C, 1])
        lnr = sb("lnr", [P, 2, 2 * C, 1])
        h0 = sb("h0", [P, 2 * C, D])
        hT = sb("hT", [P, 4, P * 4])
        outs = sb("outs", [P, 4, 2, C, D])
        o1, o2, ox, o3 = (outs[:, n, :, :, :] for n in range(4))
        selfr = sb("selfr", [P, 2, C, XW])
        agghead = sb("agghead", [P, C, D])
        last = sb("last", [P, D])
        prod = sb("prod", [P, C, MW])
        small = sb("small", [P, 12, SC])

        dense_x = [xd[:].rearrange("p v c f -> p (v c) f")[:, DC * u:DC * u + DC, :] for u in range(2)]
        dense_x.append(prod[:].rearrange("p c f -> p (c f)")[:, 0:DC * XW].rearrange("p (c f) -> p c f", f=XW))
        d1, d2, dx, d3 = (outs[:, n, :, :, :].rearrange("p v c f -> p (v c) f") for n in range(4))
        zbuf = sb("zbuf", [P, C, D])
        scan_g, scan_cont, scan_sum = (prod[:].rearrange("p c f -> p (c f)")[:, n * D * (C + 1):(n + 1) * D * (C + 1)]
                                       for n in range(3))
        by_feature = [a.rearrange("p (f c) -> p f c", c=C + 1) for a in (scan_g, scan_cont, scan_sum)]
        g_in, cont_in, sums = by_feature
        hdb = sb("hdb", [P, C, D])
        hnext = sb("hnext", [P, D])
        hclose = sb("hclose", [P, D])
        score = sb("score", [P, SC, H])
        dots = sb("dots", [P, 2, SC, H])
        smax = sb("smax", [P, SC, H])
        ex4 = sb("ex4", [P, SC, H])
        edge = sb("edge", [P, H])
        masks = sb("masks", [P, 4, C * P], BF16)
        pairsel = sb("pairsel", [R, 4, P], BF16)
        xm = sb("xm", [P, C, 4 * P])
        twice = dots[:].rearrange("p a c h -> p (a c h)")[:, 0:4 * C * D].rearrange("p (v c f) -> p v c f", v=2, f=2 * D)
        ohT = smax[0:R, :, :].rearrange("p c h -> p (c h)")[:, 0:C * P // 2].bitcast(BF16)
        ohc = smax[:, :, :].rearrange("p c h -> p (c h)")[:, C * P // 2:C * P // 2 + C * R // 2].bitcast(BF16)
        rawsb = hT[:].rearrange("p a b -> p (a b)").rearrange("p (c f) -> p c f", f=H * D)
        sqb = outs[:, 2:4, :, :, :].rearrange("p n v c f -> p (n v c f)").rearrange("p (c f) -> p c f", f=H * D)
        sqa = lnq[:].rearrange("p v c f -> p (v c f)").rearrange("p (c f) -> p c f", f=H * D)
        aggs = [xd[:].rearrange("p v c f -> p (v c f)")[:, 0:C * MW].rearrange("p (c f) -> p c f", f=MW),
                small[:].rearrange("p n c -> p (n c)")[:, 4 * SC:4 * SC + C * MW].rearrange("p (c f) -> p c f", f=MW)]
        upd, updsq = lnc[:, 0, 0:C, :], lnc[:, 1, 0:C, :]
        scratch = score[:].rearrange("p c h -> p (c h)")
        CH = C * H

        def part(first, n):
            return scratch[:, first:first + n]

        squares, norms = part(0, 2 * CH + C), part(2 * CH + C, 2 * CH + C)
        tanh_in, tanh_out = part(4 * CH + 2 * C, CH + C), part(5 * CH + 3 * C, CH + C)
        logs = part(6 * CH + 4 * C, 3 * CH)
        ka = [part((9 + n) * CH + 4 * C, CH) for n in range(6)]
        kb = [part((15 + n) * CH + 4 * C, CH) for n in range(8)]
        kc = [part((23 + n) * CH + 4 * C, C) for n in range(4)]

        bank = [psum(f"bank{i}", [P, 512]) for i in range(8)]

        s_const = sem("constants_made")
        s_in = sem("edges_loaded")
        s_weights = sem("weights_loaded")
        s_pad = sem("pads_set")
        s_padv = sem("attention_pad_set")
        s_nodes = sem("nodes_copied")
        s_prep = sem("prep_step")
        s_prepdiag = sem("prep_operand_ready")
        s_prepact = sem("prep_sqrt")
        s_preppe = sem("prep_product")
        s_idx = sem("index_arrays_ready")
        s_turn, s_turn_sp, s_turn_dve = sem("pool_turn"), sem("sp_turn"), sem("dve_turn")
        s_idxr = sem("indices_staged")
        s_rows = [sem(f"rows_gathered{s}") for s in range(2)]
        s_xst = [sem(f"xslot_stored{s}") for s in range(2)]
        s_map = [sem(f"map_scattered{s}") for s in range(2)]

        sems_dense = {}
        for name in ("xc1", "sq1", "var1", "std1", "h0", "z", "hT", "b1", "b2", "b3", "o1", "o2", "x1", "xc2", "sq2",
                     "var2", "std2", "o3", "step"):
            sems_dense[name] = sem("dense_" + name)
        s_xd = [sem(f"dense_x_loaded{u}") for u in range(3)]
        s_dst1, s_dst2, s_dst3 = sem("dense_rows1_stored"), sem("dense_rows2_stored"), sem("dense_x1_rows3_stored")
        sems_layer = {}
        for name in ("xc1", "sq1", "var1", "std1", "used", "z", "t_ps", "t", "mm", "relu", "back", "u", "xc2", "sq2",
                     "var2", "std2", "o3", "step", "ready", "tiled", "chain", "head", "head_added", "last", "carry"):
            sems_layer[name] = sem("layer_" + name)
        s_self = [sem(f"self_rows_loaded{s}") for s in range(2)]
        s_ust = [sem(f"slots_stored{s}") for s in range(2)]
        s_map_used = sem("row_numbers_made")

        s_loc = [sem(f"attention_rows_loaded{s}") for s in range(2)]
        s_hst = [sem(f"hsrc_stored{s}") for s in range(2)]
        s_out = [sem(f"out_scattered{s}") for s in range(2)]
        sa = {}
        for name in ("step", "bulk", "chain", "ready", "tiled", "hd", "read", "sq", "ps_t", "t", "dots", "used", "seed",
                     "seed_ps", "bulk_pe", "bulk_op", "bulk_act", "bulk_ln"):
            sa[name] = sem("score_" + name)
        s_src = [sem(f"message_sources_loaded{s}") for s in range(2)]
        s_sums = [sem(f"message_sums_stored{s}") for s in range(2)]
        s_headsum = sem("head_sums_gathered")
        s_x1 = [sem(f"message_x1_loaded{s}") for s in range(2)]
        sm = {}
        for name in ("step", "ohc", "oh_ps", "oh", "mask_ps", "mask", "sources", "xm", "raw", "rawsb", "squares", "log",
                     "norms", "tanh_in", "tanh", "ln", "scaled", "agg", "aggsq", "upd", "updsq", "mid",
                     "factored", "weighed", "factor", "rescaled", "idx_head", "o", "chain_end", "carry"):
            sm[name] = sem("msg_" + name)

        def slots_view(t, width=None):
            v = t[0:SLOTS, :].rearrange("(p j) f -> p j f", j=SC)
            return v if width is None else v[:, :, 0:width]

        def dense_view(t, first):
            return t[first:first + (ND - 1) * NB, :].rearrange("(k p r) f -> k p r f", p=P, r=DC)

        def dense_last(t, first):
            return t[first + (ND - 1) * NB:first + N, :].rearrange("(p r) f -> p r f", r=DC)

        def dense_at(t, first, k):
            if isinstance(k, int) and k == ND - 1:
                return dense_last(t, first)
            return dense_view(t, first)[bass.ds(k, 1)].rearrange("k p r f -> (k p) r f")

        def dense_stored(eng):
            eng.wait_ge(s_dst1, 16 * ND)
            eng.wait_ge(s_dst2, 16 * ND)
            eng.wait_ge(s_dst3, 32 * ND)

        class Marks:

            def __init__(self, eng, semaphore):
                self.eng, self.semaphore, self.base, self.n = eng, semaphore, 0, 0

            def __call__(self, ins):
                self.n += 1
                ins.then_inc(self.semaphore, 1)
                return self.n

            def wait(self, mark):
                self.eng.wait_ge(self.semaphore, self.base + mark)

            def restart(self, base):
                self.base, self.n = base, 0

        class Steps:

            def __init__(self, eng, semaphore):
                self.eng, self.semaphore, self.base, self.n = eng, semaphore, 0, 0

            def __call__(self, ins):
                self.n += 1
                ins.then_inc(self.semaphore, 1)
                self.eng.wait_ge(self.semaphore, self.base + self.n)

            def restart(self, base):
                self.base, self.n = base, 0

        def bc(ap, shape):
            return ap.broadcast_to(shape)

        block = ctx.enter_context(nc.Block())
        full_rows, rest = P - 1, E - (P - 1) * EC

        def edges_view(a):
            return (a[0:full_rows * EC].rearrange("(p j) -> p j", j=EC),
                    a[full_rows * EC:E].rearrange("(p j) -> p j", p=1))

        def used(q, i, s):
            return q * (NCH // 2 + 1 - s) + i

        def dmas(L, i, s):
            return 16 * used(L, i, s) if L < 2 else 16 * used(2, 0, s) + 32 * i

        def at_turn(L, t):
            return L * NCH + t

        def load_self(sp, L, i, s):
            t = 2 * i + s
            if L > 0 or not (isinstance(t, int) and t < 2):
                sp.wait_ge(sems_layer["used"], at_turn(L, t) - 1)
                if L == 2:
                    sp.wait_ge(sems_layer["u"], at_turn(L, t) - 1)
            if L == 0:
                sp.dma_start(selfr[:, s, :, :], slots_view(xslot)[:, bass.ds(t * C, C), :]).then_inc(s_self[s], 16)
            else:
                sp.dma_start(selfr[:, s, :, 0:D], slots_view(table[L])[:, bass.ds(t * C, C), :]).then_inc(s_self[s], 16)
                if L == 2:
                    sp.dma_start(xd[:, s, :, :], slots_view(xslot)[:, bass.ds(t * C, C), :]).then_inc(s_self[s], 16)

        def store_slots(sp, L, i, s):
            t = 2 * i + s
            where = slots_view(table[L + 1])[:, bass.ds(t * C, C), :]
            if L < 2:
                sp.wait_ge(sems_layer["u"], at_turn(L, t) + 1)
                sp.dma_start(where, o1[:, s, :, :]).then_inc(s_ust[s], 16)
            else:
                sp.wait_ge(sems_layer["u"], at_turn(L, t) + 1)
                sp.dma_start(slots_view(x1slot)[:, bass.ds(t * C, C), :], ox[:, s, :, :]).then_inc(s_ust[s], 16)
                sp.wait_ge(sems_layer["o3"], t + 1)
                sp.dma_start(where, o3[:, s, :, :]).then_inc(s_ust[s], 16)

        def layer_sp(sp, L):
            if L > 0:
                for s in range(2):
                    sp.wait_ge(s_ust[s], dmas(L, 0, s))
            else:
                sp.wait_ge(sems_dense["x1"], 2 * ND)
            load_self(sp, L, 0, 0)
            load_self(sp, L, 0, 1)
            load_self(sp, L, 1, 0)
            with sp.Fori(0, NCH // 2 - 1) as i:
                load_self(sp, L, i + 1, 1)
                store_slots(sp, L, i, 0)
                load_self(sp, L, i + 2, 0)
                store_slots(sp, L, i, 1)
            store_slots(sp, L, NCH // 2 - 1, 0)
            store_slots(sp, L, NCH // 2 - 1, 1)
            store_slots(sp, L, NCH // 2, 0)
            if L == 2:
                for s in range(2):
                    sp.wait_ge(s_ust[s], dmas(2, NCH // 2 + 1 - s, s))

        def attention_sp(sp):
            def load(i, s):
                k = 2 * i + s
                t = (NCH - 1) - k
                if not (isinstance(k, int) and k < 2):
                    sp.wait_ge(sa["chain"], k - 1)
                    sp.sem_inc(s_turn_sp, 1)
                sp.dma_start(selfr[:, s, :, 0:D], slots_view(table[3])[:, bass.ds(t * C, C), :]).then_inc(s_loc[s], 16)

            def store(i, s):
                t = (NCH - 1) - (2 * i + s)
                sp.wait_ge(s_rows[s], (used(4, i, s) + 1) * (16 * C))
                sp.sem_inc(s_turn_sp, 1)
                sp.dma_start(slots_view(hsrc)[:, bass.ds(t * C, C), :], rows64[:, s, :, :]).then_inc(s_hst[s], 16)

            load(0, 0)
            load(0, 1)
            with sp.Fori(0, NCH // 2 - 1) as i:
                for s in range(2):
                    store(i, s)
                    load(i + 1, s)
            i = NCH // 2 - 1
            store(i, 0)
            load(i + 1, 0)
            store(i, 1)
            store(i + 1, 0)
            for s in range(2):
                sp.wait_ge(s_hst[s], 16 * (NCH // 2 + 1 - s))
            sp.wait_ge(sa["bulk_act"], 5)

            def load_sources(i, s):
                t = 2 * i + s
                if not (isinstance(t, int) and t < 2):
                    sp.wait_ge(sm["sources"], 2 * t - 2)
                    sp.sem_inc(s_turn_sp, 1)
                for half in range(2):
                    sp.dma_start(twice[:, s, :, D * half:D * half + D], slots_view(hsrc)[:, bass.ds(t * C, C), :]) \
                        .then_inc(s_src[s], 16)

            def load_x1(i, s):
                t = 2 * i + s
                if not (isinstance(t, int) and t < 2):
                    sp.wait_ge(sm["o"], t - 1)
                    sp.sem_inc(s_turn_sp, 1)
                sp.dma_start(selfr[:, s, :, 0:D], slots_view(x1slot)[:, bass.ds(t * C, C), :]).then_inc(s_x1[s], 16)

            load_sources(0, 0)
            load_sources(0, 1)
            load_x1(0, 0)
            load_x1(0, 1)
            load_sources(1, 0)
            load_sources(1, 1)
            def store_sums(i, s, last_chunk=False):
                t = 2 * i + s
                if not last_chunk:
                    sp.wait_ge(sm["agg"], t + 1)
                else:
                    sp.wait_ge(sm["chain_end"], 1)
                sp.sem_inc(s_turn_sp, 1)
                sp.dma_start(slots_view(msums)[:, bass.ds(t * C, C), :], aggs[s]).then_inc(s_sums[s], 16)

            store_sums(0, 0)
            load_sources(2, 0)
            store_sums(0, 1)
            with sp.Fori(1, NCH // 2 - 1) as i:
                for s in range(2):
                    load_sources(i + 1 + s, 1 - s)
                    load_x1(i, s)
                    store_sums(i, s)
            load_x1(NCH // 2 - 1, 0)
            store_sums(NCH // 2 - 1, 0)
            load_x1(NCH // 2 - 1, 1)
            store_sums(NCH // 2 - 1, 1)
            load_x1(NCH // 2, 0)
            store_sums(NCH // 2, 0, last_chunk=True)

        def attention_pool(pool, gather_pass, stage):
            for s in range(2):
                pool.wait_ge(s_ust[s], dmas(2, NCH // 2 + 1 - s, s))

            def free(i, s):
                if isinstance(i, int) and i == 0:
                    return [(sems_layer["used"], 3 * NCH)]
                return [(sa["used"], 2 * i + s - 1), (sa["ps_t"], 2 * i + s - 1), (s_hst[s], 16 * i)]

            gather_pass(4, row_of_src, table[3], D, ROWS - 1, free, reverse=True, ring=rows64)
            for s in range(2):
                pool.wait_ge(s_rows[s], used(5, 0, s) * (16 * C))

            def scatter(i, s):
                k = 2 * i + s
                if not (isinstance(i, int) and i == 0):
                    pool.wait_ge(s_out[s], i * (16 * C))
                stage(idx_out, k, s)
                pool.wait_ge(sm["o"], k + 1)
                pool.wait_ge(s_idxr, 7 * NCH + k + 1)
                pool.sem_inc(s_turn, 1)
                for c in range(C):
                    pool.indirect_dma_start(out=out[:, :],
                                            out_offset=bass.IndirectOffsetOnAxis(ap=idxr[:, s, c:c + 1], axis=0),
                                            in_=o1[:, s, c, :], in_offset=None, bounds_check=N - 1,
                                            oob_is_err=False).then_inc(s_out[s], 16)

            def update(i, s):
                t = 2 * i + s
                pool.wait_ge(sm["factor"], t + 1)
                pool.wait_ge(s_x1[s], 16 * (i + 1))
                if not (isinstance(i, int) and i == 0):
                    pool.wait_ge(s_out[s], i * (16 * C))
                pool.sem_inc(s_turn, 1)
                nc.gpsimd.tensor_tensor(upd, upd, bc(kc[1].rearrange("p (c k) -> p c k", k=1), [P, C, D]), ALU.mult) \
                    .then_inc(sm["rescaled"], 1)
                pool.wait_ge(sm["rescaled"], t + 1)
                pool.sem_inc(s_turn, 1)
                nc.gpsimd.tensor_tensor(o1[:, s, :, :], upd, selfr[:, s, :, 0:D], ALU.add).then_inc(sm["o"], 1)

            def weigh(i, s):
                t = 2 * i + s
                pool.wait_ge(sm["mid"], t + 1)
                pool.wait_ge(s_sums[s], 16 * (i + 1))
                pool.sem_inc(s_turn, 1)
                by_head = aggs[s][:, :, 0:H * D].rearrange("p c (h o) -> p c h o", o=D)
                nc.gpsimd.tensor_tensor(by_head, by_head, bc(kb[6].rearrange("p (c h k) -> p c h k", h=H, k=1), [P, C, H, D]),
                                        ALU.mult).then_inc(sm["factored"], 1)
                pool.wait_ge(sm["factored"], t + 1)
                pool.sem_inc(s_turn, 1)
                nc.gpsimd.tensor_tensor(aggs[s][:, :, 0:2 * D], aggs[s][:, :, 0:2 * D], aggs[s][:, :, 2 * D:4 * D], ALU.add) \
                    .then_inc(sm["weighed"], 1)

            weigh(0, 0)
            update(0, 0)
            weigh(0, 1)
            scatter(0, 0)
            update(0, 1)
            weigh(1, 0)
            scatter(0, 1)
            with pool.Fori(1, NCH // 2 - 1) as i:
                for s in range(2):
                    update(i, s)
                    weigh(i + s, 1 - s)
                    scatter(i, s)
            update(NCH // 2 - 1, 0)
            weigh(NCH // 2 - 1, 1)
            for s in range(2):
                pool.wait_ge(s_sums[s], 16 * (NCH // 2 + 1 - s))
            pool.wait_ge(sm["idx_head"], 1)
            pool.indirect_dma_start(out=headsum[:], out_offset=None, in_=msums[:, :],
                                    in_offset=bass.IndirectOffsetOnAxis(ap=idx_head[:, 0:1], axis=0),
                                    bounds_check=SLOTS - 1, oob_is_err=False).then_inc(s_headsum, 16)
            scatter(NCH // 2 - 1, 0)
            update(NCH // 2 - 1, 1)
            weigh(NCH // 2, 0)
            scatter(NCH // 2 - 1, 1)
            update(NCH // 2, 0)
            scatter(NCH // 2, 0)
            for s in range(2):
                pool.wait_ge(s_out[s], (NCH // 2 + 1 - s) * 16 * C)

        def score_dve(dve):
            done = Marks(dve, sa["step"])
            V = nc.vector
            g_in, _, sums = by_feature
            products = agghead[:]
            dot_parts = h0[:].rearrange("p c f -> p (c f)")[:, 0:2 * C * R * H].rearrange("p (a c r h) -> p a c r h", a=2, r=R, h=H)

            def destinations(i, s, first=False):
                k = 2 * i + s
                t = (NCH - 1) - k
                own = selfr[:, s, :, 0:D]
                dve.wait_ge(s_loc[s], 16 * (i + 1))
                dve.sem_inc(s_turn_dve, 1)
                if first:
                    V.tensor_scalar(last[:], own[:, C - 1, :], owns[:, EC:SC], None, ALU.mult).then_inc(sa["seed"], 1)
                    dve.wait_ge(sa["seed_ps"], 1)
                    m = done(V.tensor_copy(hnext[:], bank[5][:, 0:D]))
                    m = done(V.tensor_scalar(edge[:, 0:1], owns[:, EC:SC], -1.0, 1.0, ALU.mult, ALU.add))
                    done.wait(m)
                    V.scalar_tensor_tensor(hclose[:], hnext[:], edge[:, 0:1], last[:], ALU.mult, ALU.add) \
                        .then_inc(sa["ready"], 1)
                ob = owns[:, bass.ds(t * C, C)].rearrange("p (c k) -> p c k", k=1)
                m = done(V.tensor_tensor(g_in[:, :, 0:C].rearrange("p f c -> p c f"), own, bc(ob, [P, C, D]), ALU.mult))
                dve.wait_ge(sa["tiled"], k + 1)
                done.wait(m)
                m = done(V.tensor_tensor(g_in[:, :, 0:C], g_in[:, :, 0:C], zbuf[:].rearrange("p c f -> p f c"), ALU.add))
                done.wait(m)
                if first:
                    m = done(V.tensor_copy(g_in[:, :, C - 1], hnext[:]))
                    done.wait(m)
                if not first:
                    dve.wait_ge(sa["hd"], k)
                V.tensor_tensor_scan(scan_sum[:, ::-1], scan_cont[:, ::-1], scan_g[:, ::-1], 0.0, ALU.mult, ALU.add) \
                    .then_inc(sa["chain"], 1)
                dve.wait_ge(sa["chain"], k + 1)
                done(V.tensor_copy(g_in[:, :, C], sums[:, :, 0]))

            def edges(i, s, ahead=True):
                k = 2 * i + s
                cols = bass.ds(((NCH - 1) - k) * C, C)
                dve.wait_ge(s_rows[s], (used(4, i, s) + 1) * (16 * C))
                dve.wait_ge(sa["hd"], k + 1)
                dve.sem_inc(s_turn_dve, 1)
                m = done(V.tensor_tensor(products, rows64[:, s, :, :], hdb[:], ALU.mult))
                done.wait(m)
                dve.sem_inc(s_turn_dve, 1)
                done(V.tensor_reduce(small[:, 2, cols], products, AX.X, ALU.add))
                if ahead:
                    destinations(i + s, 1 - s)
                dve.wait_ge(sa["sq"], k + 1)
                dve.sem_inc(s_turn_dve, 1)
                V.tensor_reduce(small[:, 0:2, cols], lnq[:, 0, :, :].rearrange("p (a c) f -> p a c f", a=2), AX.X,
                                ALU.add).then_inc(sa["used"], 1)
                dve.wait_ge(sa["dots"], k + 1)
                for a in range(2):
                    m = done(V.tensor_tensor(dot_parts[:, a, :, :, :],
                                             bank[2][:, 256 * a:256 * a + 256].rearrange("p (c r h) -> p c r h", r=R, h=H),
                                             bc(onehot[:, cols, :].rearrange("p c (r k) -> p c r k", k=1), [P, C, R, H]),
                                             ALU.mult))
                done.wait(m)
                dve.sem_inc(sa["read"], 1)
                for a in range(2):
                    m = done(V.tensor_reduce(dots[:, a, cols, :], dot_parts[:, a, :, :, :].rearrange("p c r h -> p c h r"),
                                             AX.X, ALU.add))
                return m

            dve.wait_ge(sems_layer["o3"], NCH)
            m = done(V.memset(scan_g, 0.0))
            m = done(V.memset(scan_cont, 0.0))
            done.wait(m)
            dve.sem_inc(sa["ready"], 1)
            destinations(0, 0, first=True)
            edges(0, 0)
            edges(0, 1)
            start = done.n
            done.restart(start)
            edges(1, 0)
            per = done.n
            edges(1, 1)
            with dve.Fori(2, NCH // 2) as i:
                for s in range(2):
                    done.restart(start + (2 * i + s - 2) * per)
                    edges(i, s)
                    assert done.n == per
            done.restart(start + (NCH - 3) * per)
            done.wait(edges(NCH // 2, 0, ahead=False))
            dve.wait_ge(sa["used"], NCH)

            link = Steps(dve, sa["bulk"])
            acts = [0]
            ops = [0]

            def ready(ins):
                ops[0] += 1
                ins.then_inc(sa["bulk_op"], 1)

            def after_act():
                acts[0] += 1
                dve.wait_ge(sa["bulk_act"], acts[0])

            a2, b2, ab = small[:, 0, :], small[:, 1, :], small[:, 2, :]
            v = [small[:, n, :] for n in range(12)]

            def log_factor(norm2, into):
                ready(nc.vector.tensor_scalar(v[9], norm2, SQ_FLOOR, None, ALU.max))
                after_act()
                link(nc.vector.tensor_scalar(v[9], v[10], CURV ** 0.5, MIN_NORM, ALU.mult, ALU.max))
                ready(nc.vector.tensor_scalar(v[9], v[9], 1.0 - 1e-5, None, ALU.min))
                after_act()
                link(nc.vector.tensor_tensor(v[10], v[10], v[11], ALU.subtract))
                link(nc.vector.reciprocal(v[11], v[9]))
                link(nc.vector.scalar_tensor_tensor(into, v[10], 0.5, v[11], ALU.mult, ALU.mult))

            log_factor(a2, small[:, 3, :])
            link(nc.vector.tensor_scalar(v[4], ab, -2.0 * CURV, 1.0, ALU.mult, ALU.add))
            link(nc.vector.tensor_tensor(v[5], a2, b2, ALU.mult))
            link(nc.vector.scalar_tensor_tensor(v[5], v[5], CURV ** 2, v[4], ALU.mult, ALU.add))
            link(nc.vector.tensor_scalar(v[5], v[5], MIN_NORM, None, ALU.max))
            link(nc.vector.reciprocal(v[6], v[5]))
            link(nc.vector.scalar_tensor_tensor(v[4], b2, CURV, v[4], ALU.mult, ALU.add))
            link(nc.vector.tensor_tensor(v[4], v[4], v[6], ALU.mult))
            link(nc.vector.tensor_scalar(v[5], a2, -CURV, 1.0, ALU.mult, ALU.add))
            link(nc.vector.tensor_tensor(v[5], v[5], v[6], ALU.mult))
            link(nc.vector.tensor_tensor(v[6], v[4], a2, ALU.mult))
            link(nc.vector.tensor_tensor(v[7], v[5], ab, ALU.mult))
            link(nc.vector.scalar_tensor_tensor(v[6], v[7], -2.0, v[6], ALU.mult, ALU.add))
            link(nc.vector.tensor_tensor(v[6], v[6], v[4], ALU.mult))
            link(nc.vector.tensor_tensor(v[7], v[5], v[5], ALU.mult))
            link(nc.vector.tensor_tensor(v[7], v[7], b2, ALU.mult))
            link(nc.vector.tensor_tensor(v[6], v[6], v[7], ALU.add))
            log_factor(v[6], v[8])
            link(nc.vector.tensor_tensor(v[4], v[4], v[8], ALU.mult))
            link(nc.vector.tensor_tensor(v[5], v[5], v[8], ALU.mult))
            f4 = bc(v[4].rearrange("p (c k) -> p c k", k=1), [P, SC, H])
            f5 = bc(v[5].rearrange("p (c k) -> p c k", k=1), [P, SC, H])
            link(nc.vector.tensor_tensor(dots[:, 0, :, :], dots[:, 0, :, :], f4, ALU.mult))
            link(nc.vector.tensor_tensor(dots[:, 1, :, :], dots[:, 1, :, :], f5, ALU.mult))
            link(nc.vector.tensor_tensor(score[:], dots[:, 0, :, :], dots[:, 1, :, :], ALU.subtract))
            link(nc.vector.scalar_tensor_tensor(score[:], score[:], 0.2, score[:], ALU.mult, ALU.max))
            BIG = 1e30
            link(nc.vector.tensor_scalar(tmp[:], cont[:], BIG, -BIG, ALU.mult, ALU.add))
            link(nc.vector.tensor_scalar(tmp2[:, 0:EC], ends[:, 0:EC], -BIG, None, ALU.mult))
            for h in range(H):
                link(nc.vector.tensor_tensor_scan(smax[:, 0:EC, h], tmp[:, 0:EC], score[:, 0:EC, h], -BIG, ALU.add,
                                                  ALU.max))
            link(nc.vector.tensor_copy(edge[:], smax[:, EC - 1, :]))
            for h in range(H):
                nc.vector.tensor_tensor_scan(dots[:, 0, 0:EC, h][:, ::-1],
                                             tmp2[:, 0:EC][:, ::-1], smax[:, 0:EC, h][:, ::-1], -BIG, ALU.add, ALU.max)
            link(nc.vector.tensor_scalar(v[9], head[:], BIG, -BIG, ALU.mult, ALU.add))
            link(nc.vector.tensor_scalar(v[10], dstf[:], dstf[:, EC - 1:EC], None, ALU.is_equal))
            link(nc.vector.tensor_scalar(v[10], v[10], BIG, -BIG, ALU.mult, ALU.add))
            for h in range(H):
                for part, value, m, mask in ((0, edge[:, h:h + 1], carryt, v[9]), (1, dots[:, 0, 0, h:h + 1], carrym, v[10])):
                    ready(nc.vector.tensor_scalar(diag[:], ident[:], value, None, ALU.mult))
                    link(nc.vector.tensor_scalar(pen[:], m[:], BIG, -BIG, ALU.mult, ALU.add))
                    dve.wait_ge(sa["bulk_pe"], 2 * h + part + 1)
                    link(nc.vector.tensor_tensor(pen[:], pen[:], bank[5][:, 0:P], ALU.add))
                    link(nc.vector.tensor_reduce(hpart[:, part:part + 1], pen[:], AX.X, ALU.max))
                for part, mask in ((0, v[9]), (1, v[10])):
                    link(nc.vector.scalar_tensor_tensor(dots[:, 0, :, h], mask, hpart[:, part:part + 1], dots[:, 0, :, h],
                                                        ALU.add, ALU.max))
            ready(nc.vector.tensor_tensor(score[:, 0:EC, :], score[:, 0:EC, :], dots[:, 0, 0:EC, :], ALU.subtract))
            after_act()

        def score_act(act):
            _, cont_in, sums = by_feature

            def operands(k):
                t = (NCH - 1) - k
                if isinstance(k, int) and k == 0:
                    act.wait_ge(sa["ready"], 2)
                else:
                    act.wait_ge(sa["chain"], k)
                for c in range(C):
                    nc.scalar.activation(zbuf[:, c, :], hclose[:], ACT.Copy, scale=head[:, bass.ds(t * C + c, 1)])
                flags = goes[:, bass.ds(t * C, C)].rearrange("p (k c) -> p k c", k=1).broadcast_to([P, D, C])
                nc.scalar.copy(cont_in[:, :, 0:C], flags).then_inc(sa["tiled"], 1)

            def destinations_out(k):
                act.wait_ge(sa["chain"], k + 1)
                if not (isinstance(k, int) and k == 0):
                    act.wait_ge(sa["sq"], k)
                nc.scalar.copy(hdb[:], sums[:, :, 0:C].rearrange("p f c -> p c f")).then_inc(sa["hd"], 1)

            def turn(i, s, ahead=2):
                k = 2 * i + s
                act.wait_ge(s_rows[s], (used(4, i, s) + 1) * (16 * C))
                if not (isinstance(k, int) and k == 0):
                    act.wait_ge(sa["used"], k)
                nc.scalar.activation(lnq[:, 0, 0:C, :], rows64[:, s, :, :], ACT.Square)
                act.wait_ge(sa["hd"], k + 1)
                nc.scalar.activation(lnq[:, 0, C:2 * C, :], hdb[:], ACT.Square).then_inc(sa["sq"], 1)
                act.wait_ge(sa["ps_t"], k + 1)
                nc.scalar.copy(hT[:, 0, :], bank[0][:])
                nc.scalar.copy(hT[:, 1, :], bank[1][:]).then_inc(sa["t"], 1)
                if ahead >= 1:
                    destinations_out(k + 1)
                if ahead >= 2:
                    operands(k + 2)

            operands(0)
            destinations_out(0)
            operands(1)
            turn(0, 0)
            turn(0, 1)
            with act.Fori(1, NCH // 2 - 1) as i:
                turn(i, 0)
                turn(i, 1)
            turn(NCH // 2 - 1, 0)
            turn(NCH // 2 - 1, 1, ahead=1)
            turn(NCH // 2, 0, ahead=0)
            for n in range(2):
                act.wait_ge(sa["bulk_op"], 2 * n + 1)
                nc.scalar.activation(small[:, 10, :], small[:, 9, :], ACT.Sqrt).then_inc(sa["bulk_act"], 1)
                act.wait_ge(sa["bulk_op"], 2 * n + 2)
                nc.scalar.activation(small[:, 10, :], small[:, 9, :], ACT.Ln, bias=1.0, scale=1.0).then_inc(sa["bulk_ln"], 1)
                act.wait_ge(sa["bulk_ln"], n + 1)
                nc.scalar.activation(small[:, 11, :], small[:, 9, :], ACT.Ln, bias=1.0, scale=-1.0).then_inc(sa["bulk_act"], 1)
            act.wait_ge(sa["bulk_op"], 4 + 2 * H + 1)
            nc.scalar.activation(ex4[:, 0:EC, :], score[:, 0:EC, :], ACT.Exp).then_inc(sa["bulk_act"], 1)

        def score_pe(pe):
            def turn(i, s, k):
                pe.wait_ge(s_rows[s], (used(4, i, s) + 1) * (16 * C))
                if not (isinstance(k, int) and k == 0):
                    pe.wait_ge(sa["t"], k)
                for q in range(4):
                    nc.tensor.transpose(bank[0][:, q * P:(q + 1) * P], rows64[:, s, 2 * q:2 * q + 2, :].rearrange("p c f -> p (c f)"), ident[:])
                pe.wait_ge(sa["hd"], k + 1)
                for q in range(4):
                    ins = nc.tensor.transpose(bank[1][:, q * P:(q + 1) * P],
                                              hdb[:, 2 * q:2 * q + 2, :].rearrange("p c f -> p (c f)"), ident[:])
                ins.then_inc(sa["ps_t"], 1)
                pe.wait_ge(sa["t"], k + 1)
                if not (isinstance(k, int) and k == 0):
                    pe.wait_ge(sa["read"], k)
                for a in range(2):
                    for q in range(4):
                        ins = nc.tensor.matmul(bank[2][:, 256 * a + 64 * q:256 * a + 64 * q + 64],
                                               hT[:, a, q * P:(q + 1) * P], avblk[:], start=True, stop=True)
                ins.then_inc(sa["dots"], 1)

            pe.wait_ge(sa["seed"], 1)
            nc.tensor.matmul(bank[5][:, 0:D], carryt[:], last[:], start=True, stop=True).then_inc(sa["seed_ps"], 1)
            turn(0, 0, 0)
            turn(0, 1, 1)
            with pe.Fori(1, NCH // 2) as i:
                turn(i, 0, 2 * i)
                turn(i, 1, 2 * i + 1)
            turn(NCH // 2, 0, NCH - 1)
            for n in range(2 * H):
                pe.wait_ge(sa["bulk_op"], 4 + n + 1)
                nc.tensor.matmul(bank[5][:, 0:P], ones[:], diag[:], start=True, stop=True).then_inc(sa["bulk_pe"], 1)

        MASKS = 8

        def message_pe(pe):
            def one_hots(t):
                if not (isinstance(t, int) and t == 0):
                    pe.wait_ge(sm["mask"], MASKS * t)
                pe.wait_ge(sm["ohc"], t + 1)
                bk = bank[2][:].bitcast(BF16)
                for c in range(C):
                    ins = nc.tensor.transpose(bk[0:R, c * P:(c + 1) * P], ohc[:, c * R:(c + 1) * R], identb[:])
                ins.then_inc(sm["oh_ps"], 1)

            def mask(t, n):
                half, q = n // 4, n % 4
                if n == 0:
                    pe.wait_ge(sm["oh"], t + 1)
                if n >= 2:
                    pe.wait_ge(sm["mask"], MASKS * t + n - 1)
                nc.tensor.matmul(bank[2 + n % 2][:], pairsel[:, q, :], ohT[:, 512 * half:512 * half + 512],
                                 start=True, stop=True).then_inc(sm["mask_ps"], 1)

            def sources(i, s):
                t = 2 * i + s
                pe.wait_ge(s_src[s], 32 * (i + 1))
                if not (isinstance(t, int) and t == 0):
                    pe.wait_ge(sm["xm"], t * C)
                for c in range(C):
                    ins = nc.tensor.transpose(bank[c // 4][:, c % 4 * P:(c % 4 + 1) * P], twice[:, s, c, :], ident[:])
                    if c % 4 == 3:
                        ins.then_inc(sm["sources"], 1)

            def chunk(i, s, last_mask=False, last_chunk=False):
                t = 2 * i + s
                for c in range(C):
                    pe.wait_ge(sm["xm"], t * C + c + 1)
                    if c % 2 == 0 and not (isinstance(t, int) and t == 0):
                        pe.wait_ge(sm["rawsb"], (t - 1) * 4 + c // 2 + 1)
                    for q in range(4):
                        ins = nc.tensor.matmul(bank[4 + c // 2][:, 256 * (c % 2):256 * (c % 2) + 256],
                                               xm[:, c, q * P:(q + 1) * P], relw[:, q, :], start=(q == 0), stop=(q == 3))
                    if c % 2 == 1:
                        ins.then_inc(sm["raw"], 1)
                    if last_chunk:
                        continue
                    if c == 1:
                        one_hots(t + 1)
                    if c == 4:
                        sources(i + s, 1 - s)
                    for n in {2: (0, 1), 4: (2, 3), 5: (4, 5), 6: (6,), 7: (7,)}.get(c, ()):
                        mask(t + 1, n)

            pe.wait_ge(sa["bulk_act"], 5)
            pe.wait_ge(sa["read"], NCH)
            one_hots(0)
            for n in range(MASKS):
                mask(0, n)
            sources(0, 0)
            chunk(0, 0)
            chunk(0, 1)
            with pe.Fori(1, NCH // 2) as i:
                chunk(i, 0)
                chunk(i, 1)
            chunk(NCH // 2, 0, last_chunk=True)
            pe.wait_ge(sm["chain_end"], 1)
            nc.tensor.matmul(bank[0][:, 0:MW], carrym[:], aggs[0][:, C - 2, :], start=True, stop=True) \
                .then_inc(sm["carry"], 1)

        def message_act(act):
            def one_hots_in(t):
                nc.scalar.copy(ohc.rearrange("p (c r) -> p c r", r=R), onehot[:, bass.ds(t * C, C), :]).then_inc(sm["ohc"], 1)

            def one_hots_out(t):
                act.wait_ge(sm["oh_ps"], t + 1)
                nc.scalar.copy(ohT, bank[2][:].bitcast(BF16)[0:R, :]).then_inc(sm["oh"], 1)

            def mask_out(t, n):
                half, q = n // 4, n % 4
                if n == 0 and not (isinstance(t, int) and t == 0):
                    act.wait_ge(sm["xm"], t * C)
                act.wait_ge(sm["mask_ps"], MASKS * t + n + 1)
                nc.scalar.copy(masks[:, q, 512 * half:512 * half + 512], bank[2 + n % 2][:]).then_inc(sm["mask"], 1)

            def raw_out(t, m):
                act.wait_ge(sm["raw"], t * 4 + m + 1)
                if m == 0 and not (isinstance(t, int) and t == 0):
                    act.wait_ge(sm["scaled"], t)
                bk = bank[4 + m][:].rearrange("p (c f) -> p c f", f=H * D)
                nc.scalar.activation(sqb[:, 2 * m:2 * m + 2, :], bk, ACT.Square)
                nc.scalar.copy(rawsb[:, 2 * m:2 * m + 2, :], bk).then_inc(sm["rawsb"], 1)

            def turn(s, t, stages="AB", ahead=2):
                if ahead == 2:
                    one_hots_in(t + 2)
                    one_hots_out(t + 2)
                act.wait_ge(sm["squares"], t + 1)
                nc.scalar.activation(norms, squares, ACT.Ln).then_inc(sm["log"], 1)
                act.wait_ge(sm["log"], t + 1)
                nc.scalar.activation(norms, norms, ACT.Exp, scale=0.5).then_inc(sm["norms"], 1)
                act.wait_ge(sm["tanh_in"], t + 1)
                nc.scalar.activation(tanh_out, tanh_in, ACT.Tanh).then_inc(sm["tanh"], 1)
                nc.scalar.activation(logs[:, CH:2 * CH], logs[:, 0:CH], ACT.Ln, bias=1.0, scale=1.0)
                nc.scalar.activation(logs[:, 2 * CH:3 * CH], logs[:, 0:CH], ACT.Ln, bias=1.0, scale=-1.0) \
                    .then_inc(sm["ln"], 1)
                if ahead == 2:
                    for n in range(4):
                        mask_out(t + 2, n)
                if ahead >= 1:
                    raw_out(t + 1, 0)
                    raw_out(t + 1, 1)
                if ahead == 2:
                    mask_out(t + 2, 4)
                    mask_out(t + 2, 5)
                if ahead >= 1:
                    raw_out(t + 1, 2)
                if "A" in stages:
                    act.wait_ge(sm["agg"], t + 1)
                    nc.scalar.activation(sqa, aggs[s][:, :, 0:H * D], ACT.Square).then_inc(sm["aggsq"], 1)
                if ahead == 2:
                    mask_out(t + 2, 6)
                if ahead >= 1:
                    raw_out(t + 1, 3)
                if ahead == 2:
                    mask_out(t + 2, 7)
                if "B" in stages:
                    act.wait_ge(sm["upd"], t)
                    nc.scalar.activation(updsq, upd, ACT.Square).then_inc(sm["updsq"], 1)

            for t in range(2):
                one_hots_in(t)
                one_hots_out(t)
                for n in range(6):
                    mask_out(t, n)
                    if t == 1 and n == 3:
                        raw_out(0, 0)
                        raw_out(0, 1)
                if t == 1:
                    raw_out(0, 2)
                mask_out(t, 6)
                if t == 1:
                    raw_out(0, 3)
                mask_out(t, 7)
            turn(0, 0, stages="A")
            turn(1, 1)
            with act.Fori(1, NCH // 2 - 1) as i:
                turn(0, 2 * i)
                turn(1, 2 * i + 1)
            turn(0, NCH - 3)
            turn(1, NCH - 2, ahead=1)
            turn(0, NCH - 1, ahead=0)
            turn(1, NCH, stages="B", ahead=0)
            turn(0, NCH + 1, stages="", ahead=0)

        def message_dve(dve):
            done = Marks(dve, sm["step"])

            def masked(t, c):
                if c % 4 == 0:
                    dve.wait_ge(sm["sources"], 2 * t + c // 4 + 1)
                    dve.wait_ge(sm["mask"], MASKS * t + c + 4)
                if c % 2 == 0 and not (isinstance(t, int) and t == 0):
                    dve.wait_ge(sm["raw"], (t - 1) * 4 + c // 2 + 1)
                nc.vector.tensor_tensor(xm[:, c, :].rearrange("p (q e) -> p q e", q=4),
                                        bc(bank[c // 4][:, c % 4 * P:(c % 4 + 1) * P].rearrange("p (k e) -> p k e", k=1), [P, 4, P]),
                                        masks[:, :, c * P:(c + 1) * P], ALU.mult).then_inc(sm["xm"], 1)

            def heads(v):
                return v.rearrange("p (c h) -> p c h", h=H)

            def over_features(v):
                return bc(v.rearrange("p (c h k) -> p c h k", h=H, k=1), [P, C, H, D])

            def by_head(buf):
                return buf[:, :, 0:H * D].rearrange("p c (h o) -> p c h o", o=D)

            def factor(t):
                return bc(small[:, 3, bass.ds(t * C, C)].rearrange("p (c k) -> p c k", k=1), [P, C, H])

            V = nc.vector
            sqA, sqC, sqB = squares[:, 0:CH], squares[:, CH:CH + C], squares[:, CH + C:]
            nA, nC, nB = norms[:, 0:CH], norms[:, CH:CH + C], norms[:, CH + C:]
            tA, tC = tanh_in[:, 0:CH], tanh_in[:, CH:CH + C]
            thA, thC = tanh_out[:, 0:CH], tanh_out[:, CH:CH + C]

            def turn(i, s, t, stages="ABC", ahead=2, first=False, last_chunk=False):
                A, B, Cc = ("A" in stages), ("B" in stages), ("C" in stages)
                mine, other = aggs[s], aggs[1 - s]
                if A:
                    dve.wait_ge(sm["rawsb"], t * 4 + 4)
                    m = done(V.tensor_reduce(ka[0], sqb.rearrange("p c (h o) -> p (c h) o", o=D), AX.X, ALU.add))
                if Cc:
                    dve.wait_ge(sm["updsq"], t - 1)
                    c1 = done(V.tensor_reduce(kc[2], updsq, AX.X, ALU.add))
                if A:
                    done.wait(m)
                    ins = V.tensor_scalar(sqA, ka[0], SQ_FLOOR, None, ALU.max)
                if Cc:
                    done.wait(c1)
                    ins = V.tensor_scalar(sqC, kc[2], SQ_FLOOR, None, ALU.max)
                if A or Cc:
                    ins.then_inc(sm["squares"], 1)
                else:
                    dve.sem_inc(sm["squares"], 1)
                if B:
                    wsum, esum = other[:, :, H * D:H * D + H], other[:, :, H * D + H:MW]
                    b1 = done(V.scalar_tensor_tensor(heads(kb[0]), esum, EPS, wsum, ALU.mult, ALU.add))
                if ahead:
                    masked(t + 1, 3)
                if B:
                    done.wait(b1)
                    b1 = done(V.tensor_scalar(kb[0], kb[0], 1e-30, None, ALU.max))
                if ahead:
                    masked(t + 1, 4)
                if B:
                    done.wait(b1)
                    b1 = done(V.reciprocal(kb[1], kb[0]))
                if ahead:
                    masked(t + 1, 5)
                dve.wait_ge(sm["norms"], t + 1)
                if A:
                    a1 = done(V.tensor_tensor(heads(ka[0]), heads(nA), factor(t), ALU.mult))
                if B:
                    done.wait(b1)
                    b1 = done(V.tensor_tensor(kb[2], nB, kb[1], ALU.mult))
                if Cc:
                    ins = V.tensor_scalar(tC, nC, MIN_NORM, CURV ** 0.5, ALU.max, ALU.mult)
                if A:
                    done.wait(a1)
                    ins = V.tensor_scalar(tA, ka[0], MIN_NORM, CURV ** 0.5, ALU.max, ALU.mult)
                if B:
                    done.wait(b1)
                    b1 = done(V.tensor_scalar(kb[2], kb[2], MIN_NORM, None, ALU.max))
                    done.wait(b1)
                    b1 = done(V.reciprocal(kb[3], kb[2]))
                    done.wait(b1)
                    b1 = done(V.tensor_scalar(kb[3], kb[3], MAXNORM, 1.0, ALU.mult, ALU.min))
                    done.wait(b1)
                    b1 = done(V.tensor_tensor(kb[2], kb[2], kb[3], ALU.mult))
                    done.wait(b1)
                    b1 = done(V.tensor_scalar(kb[2], kb[2], CURV ** 0.5, MIN_NORM, ALU.mult, ALU.max))
                    done.wait(b1)
                    ins = V.tensor_scalar(logs[:, 0:CH], kb[2], 1.0 - 1e-5, None, ALU.min)
                ins.then_inc(sm["tanh_in"], 1)
                if ahead:
                    masked(t + 1, 6)
                dve.wait_ge(sm["tanh_in"], t + 1)
                if Cc:
                    c1 = done(V.reciprocal(kc[0], tC))
                if B:
                    b1 = done(V.reciprocal(kb[4], logs[:, 0:CH]))
                    b2 = done(V.tensor_tensor(kb[5], kb[1], kb[3], ALU.mult))
                if ahead:
                    masked(t + 1, 7)
                dve.wait_ge(sm["tanh"], t + 1)
                if A:
                    ext = ex4[:, bass.ds(t * C, C), :]
                    a1 = done(V.tensor_tensor(ka[0], thA, thA, ALU.mult))
                    a2 = done(V.tensor_tensor(heads(ka[3]), heads(thA), factor(t), ALU.mult))
                if Cc:
                    done.wait(c1)
                    V.tensor_tensor(kc[1], kc[0], thC, ALU.mult).then_inc(sm["factor"], 1)
                if A:
                    done.wait(a1)
                    a1 = done(V.tensor_scalar(ka[0], ka[0], -1.0, 1.0, ALU.mult, ALU.add))
                    V.tensor_copy(prod[:, :, H * D + H:MW], ext)
                    done.wait(a1)
                    a1 = done(V.tensor_scalar(ka[0], ka[0], EPS, None, ALU.add))
                if B:
                    done.wait(b2)
                    b2 = done(V.tensor_tensor(kb[4], kb[4], kb[5], ALU.mult))
                if A:
                    done.wait(a1)
                    a1 = done(V.tensor_tensor(ka[0], ka[0], tA, ALU.mult))
                    done.wait(a1)
                    a1 = done(V.reciprocal(ka[1], ka[0]))
                if A:
                    done.wait(a1)
                    a1 = done(V.scalar_tensor_tensor(heads(ka[1]), heads(ka[1]), 2.0, ext, ALU.mult, ALU.mult))
                if A:
                    done.wait(a1)
                    a1 = done(V.tensor_tensor(ka[2], ka[1], ka[3], ALU.mult))
                    V.tensor_tensor(prod[:, :, H * D:H * D + H], heads(ka[1]), heads(tA), ALU.mult)
                    done.wait(a1)
                    V.tensor_tensor(by_head(prod), by_head(rawsb), over_features(ka[2]), ALU.mult).then_inc(sm["scaled"], 1)
                if B:
                    dve.wait_ge(sm["ln"], t + 1)
                    b1 = done(V.tensor_tensor(kb[6], logs[:, CH:2 * CH], logs[:, 2 * CH:3 * CH], ALU.subtract))
                    done.wait(b1)
                    ins = V.scalar_tensor_tensor(kb[6], kb[6], 0.5 / H, kb[4], ALU.mult, ALU.mult)
                    if A:
                        done(ins)
                    else:
                        ins.then_inc(sm["mid"], 1)
                if A:
                    dve.wait_ge(sm["scaled"], t + 1)
                    if not (isinstance(i, int) and i == 0):
                        dve.wait_ge(s_sums[s], 16 * i)
                    n = C - 1 if last_chunk else C
                    parts = (slice(0, H * D // 2), slice(H * D // 2, MW))
                    marks = [None, None]
                    for c in range(n):
                        for half in range(2):
                            q = parts[half]
                            if marks[half]:
                                done.wait(marks[half])
                            if c == 0 and first:
                                ins = V.tensor_copy(mine[:, 0, q], prod[:, 0, q])
                            else:
                                before = other[:, C - 1, q] if c == 0 else mine[:, c - 1, q]
                                ins = V.scalar_tensor_tensor(mine[:, c, q], before, cont[:, bass.ds(t * C + c, 1)],
                                                             prod[:, c, q], ALU.mult, ALU.add)
                            if c == 0 and half == 1 and B:
                                done.wait(done(ins))
                                dve.sem_inc(sm["mid"], 1)
                            elif c < n - 1 or half == 0:
                                marks[half] = done(ins)
                    if last_chunk:
                        ins.then_inc(sm["chain_end"], 1)
                        dve.wait_ge(sm["carry"], 1)
                        dve.wait_ge(s_headsum, 16)
                        V.tensor_tensor(mine[:, C - 1, :], headsum[:], bank[0][:, 0:MW], ALU.add).then_inc(sm["agg"], 1)
                    else:
                        ins.then_inc(sm["agg"], 1)
                if ahead == 2:
                    for c in range(3):
                        masked(t + 2, c)
                if A:
                    dve.wait_ge(sm["aggsq"], t + 1)
                    a1 = done(V.tensor_reduce(ka[4], sqa.rearrange("p c (h o) -> p (c h) o", o=D), AX.X, ALU.add))
                if B:
                    dve.wait_ge(sm["weighed"], t)
                    V.tensor_tensor(upd, other[:, :, 0:D], other[:, :, D:2 * D], ALU.add).then_inc(sm["upd"], 1)
                if A:
                    done.wait(a1)
                    done.wait(done(V.tensor_scalar(sqB, ka[4], SQ_FLOOR, None, ALU.max)))

            V.memset(squares, 1.0)
            V.memset(tanh_in, 1.0)
            V.memset(logs, 0.5)
            m = done(V.tensor_tensor(tmp[:], headend[:], slotdata[:, :, 0], ALU.mult))
            done.wait(m)
            m = done(V.tensor_reduce(tmp2[:, 0:1], tmp[:], AX.X, ALU.add))
            done.wait(m)
            m = done(V.tensor_scalar(tmp2[:, 1:2], tmp2[:, 0:1], -1.0, 0.0, ALU.add, ALU.max))
            done.wait(m)
            V.tensor_copy(idx_head[:], tmp2[:, 1:2]).then_inc(sm["idx_head"], 1)
            for c in range(C):
                masked(0, c)
            for c in range(3):
                masked(1, c)
            turn(0, 0, 0, stages="A", first=True)
            turn(0, 1, 1, stages="AB")
            start = done.n
            turn(1, 0, 2)
            per = done.n - start
            turn(1, 1, 3)
            with dve.Fori(2, NCH // 2 - 1) as i:
                for s in range(2):
                    done.restart(start + (2 * i + s - 2) * per)
                    turn(i, s, 2 * i + s)
                    assert done.n == per
            done.restart(start + (NCH - 5) * per)
            turn(NCH // 2 - 1, 0, NCH - 3)
            turn(NCH // 2 - 1, 1, NCH - 2, ahead=1)
            done.restart(start + (NCH - 3) * per)
            turn(NCH // 2, 0, NCH - 1, ahead=0, last_chunk=True)
            turn(NCH // 2, 1, NCH, stages="BC", ahead=0)
            turn(NCH // 2 + 1, 0, NCH + 1, stages="C", ahead=0)

        @block.sync
        def _(sp):
            sp.wait_ge(s_pad, 5)
            for a, t in ((src, srci), (dst, dsti), (etype, eti)):
                body, tail = edges_view(a)
                sp.dma_start(t[0:full_rows, 0:EC], body).then_inc(s_in, 16)
                sp.dma_start(t[full_rows:P, 0:rest], tail).then_inc(s_in, 16)
            sp.dma_start(dnext[0:full_rows, :], dst[EC:EC + (full_rows - 1) * EC + 1:EC].rearrange("(p k) -> p k", k=1),
                         allow_slow_non_contiguous=True).then_inc(s_in, 16)
            sp.wait_ge(s_padv, 1)
            for half in range(2):
                sp.dma_start(avblk[D * half:D * half + D, R * H * half:R * H * half + R * H],
                             attn_vec.rearrange("r h d -> d (r h)"), allow_slow_non_contiguous=True).then_inc(s_weights, 16)
            for r in range(R):
                sp.dma_start(relw[D * (r % 2):D * (r % 2) + D, r // 2, :].rearrange("p (h o) -> p h o", o=D),
                             rel_weight[r].rearrange("h i o -> i h o")).then_inc(s_weights, 16)
            for l in range(3):
                for half in range(2):
                    q = slice(D * half, D * half + D)
                    sp.dma_start(wblk[q, l, D * half:D * half + D], w[l][:, :]).then_inc(s_weights, 16)
                    sp.dma_start(bcol[q, l:l + 1], b[l].rearrange("(f k) -> f k", k=1)).then_inc(s_weights, 16)
            def store_c(i, s):
                sp.wait_ge(s_rows[s], (i + 1) * (16 * C))
                sp.dma_start(slots_view(xslot)[:, bass.ds((2 * i + s) * C, C), :], rows[:, s, :, :]).then_inc(s_xst[s], 16)

            def copy_nodes(i):
                def part(t):
                    return t.rearrange("(k a n) f -> k a (n f)", k=PARTS, a=16)[bass.ds(i, 1)].rearrange("k a m -> (k a) m")

                sp.dma_start(part(nodes), part(x)).then_inc(s_nodes, 16)

            with sp.Fori(0, NCH // 2) as i:
                store_c(i, 0)
                copy_nodes(i)
                store_c(i, 1)
            store_c(NCH // 2, 0)
            copy_nodes(NCH // 2)
            for s in range(2):
                sp.wait_ge(s_xst[s], 16 * (NCH // 2 + 1 - s))

            for L in range(3):
                layer_sp(sp, L)
            attention_sp(sp)

        @block.gpsimd
        def _(pool):
            nc.gpsimd.memset(srci[:], 0).then_inc(s_pad, 1)
            nc.gpsimd.memset(eti[:], 0).then_inc(s_pad, 1)
            nc.gpsimd.memset(dsti[:], N).then_inc(s_pad, 1)
            nc.gpsimd.memset(dnext[:], 2 * N).then_inc(s_pad, 1)
            nc.gpsimd.memset(ident[:], 0.0)
            nc.gpsimd.memset(below[:], 0.0)
            nc.gpsimd.memset(pairsel[:], 0.0)
            nc.gpsimd.iota(slotno[:], pattern=[[1, SC]], base=1, channel_multiplier=SC).then_inc(s_const, 1)
            pool.wait_ge(s_const, 1)
            nc.gpsimd.affine_select(out=ident[:], in_=ident[:], compare_op=ALU.not_equal, fill=1.0, base=0,
                                    pattern=[[-1, P]], channel_multiplier=1).then_inc(s_const, 1)
            nc.gpsimd.affine_select(out=below[:], in_=below[:], compare_op=ALU.is_ge, fill=1.0, base=0,
                                    pattern=[[-1, P]], channel_multiplier=1).then_inc(s_const, 1)
            nc.gpsimd.affine_select(out=pairsel[:].rearrange("r q (a f) -> r (q a) f", a=2),
                                    in_=pairsel[:].rearrange("r q (a f) -> r (q a) f", a=2), compare_op=ALU.not_equal,
                                    fill=1.0, base=0, pattern=[[-1, R], [0, D]], channel_multiplier=1).then_inc(s_const, 1)


            def stage(array, t, s):
                nc.gpsimd.tensor_copy(idxr[:, s, :], array[:, bass.ds(t * C, C)]).then_inc(s_idxr, 1)

            def gather(q, i, s, array, table_, width, bound, free, reverse, ring):
                k = 2 * i + s
                t = (NCH - 1) - k if reverse else k
                if q > 0 or not isinstance(i, int) or i > 0:
                    pool.wait_ge(s_rows[s], used(q, i, s) * (16 * C))
                stage(array, t, s)
                for semaphore, value in free(i, s):
                    pool.wait_ge(semaphore, value)
                pool.wait_ge(s_idxr, (q if q == 0 else q + 2) * NCH + k + 1)
                pool.sem_inc(s_turn, 1)
                for c in range(C):
                    pool.indirect_dma_start(out=ring[:, s, c, 0:width], out_offset=None, in_=table_[:, :],
                                            in_offset=bass.IndirectOffsetOnAxis(ap=idxr[:, s, c:c + 1], axis=0),
                                            bounds_check=bound, oob_is_err=False).then_inc(s_rows[s], 16)

            def gather_pass(q, array, table_, width, bound, free, reverse=False, ring=rows):
                gather(q, 0, 0, array, table_, width, bound, free, reverse, ring)
                gather(q, 0, 1, array, table_, width, bound, free, reverse, ring)
                with pool.Fori(1, NCH // 2) as i:
                    for s in range(2):
                        gather(q, i, s, array, table_, width, bound, free, reverse, ring)
                gather(q, NCH // 2, 0, array, table_, width, bound, free, reverse, ring)

            pool.wait_ge(s_idx, 1)
            gather_pass(0, idx_dst, x, XW, N - 1, lambda i, s: [] if isinstance(i, int) and i == 0 else [(s_xst[s], i * 16)])

            pool.wait_ge(s_idx, 2)
            pool.wait_ge(s_nodes, 16 * PARTS)
            for s in range(2):
                pool.wait_ge(s_rows[s], used(1, 0, s) * (16 * C))

            def scatter_map(i, s):
                k = 2 * i + s
                if not (isinstance(i, int) and i == 0):
                    pool.wait_ge(s_map[s], i * (16 * C))
                stage(idx_map, k, s)
                nc.gpsimd.tensor_copy(datar[:, s, :, :], slotdata[:, bass.ds(k * C, C), :]).then_inc(s_idxr, 1)
                pool.wait_ge(s_idxr, NCH + 2 * k + 2)
                pool.sem_inc(s_turn, 1)
                for c in range(C):
                    pool.indirect_dma_start(out=nodes.rearrange("n (a b) -> (n a) b", b=4),
                                            out_offset=bass.IndirectOffsetOnAxis(ap=idxr[:, s, c:c + 1], axis=0),
                                            in_=datar[:, s, c, :], in_offset=None,
                                            bounds_check=N * (XW // 4) - 1, oob_is_err=False).then_inc(s_map[s], 16)

            scatter_map(0, 0)
            scatter_map(0, 1)
            with pool.Fori(1, NCH // 2) as i:
                scatter_map(i, 0)
                scatter_map(i, 1)
            scatter_map(NCH // 2, 0)
            for s in range(2):
                pool.wait_ge(s_map[s], (NCH // 2 + 1 - s) * 16 * C)

            for L in range(3):
                if L == 0:
                    for s in range(2):
                        pool.wait_ge(s_xst[s], 16 * (NCH // 2 + 1 - s))
                else:
                    if L == 1:
                        pool.wait_ge(s_map_used, NCH)
                        dense_stored(pool)
                    for s in range(2):
                        pool.wait_ge(s_ust[s], dmas(L, 0, s))

                def free(i, s, L=L):
                    k = 2 * i + s
                    if L == 0 and isinstance(i, int) and i == 0:
                        return []
                    return [(sems_layer["used"], at_turn(L, k) - 1)]

                if L == 0:
                    gather_pass(1, srci, nodes, XW, N - 1, free)
                else:
                    gather_pass(1 + L, row_of_src, table[L], D, ROWS - 1, free)
            attention_pool(pool, gather_pass, stage)

        layer_base = [0, 0, 0, 0]

        def layer_dve(dve, L):
            sl = sems_layer
            done = Marks(dve, sl["step"])
            V = nc.vector

            def norm_first(i, s):
                t = 2 * i + s
                g, own = rows[:, s, :, 0:D], selfr[:, s, :, 0:D]
                dve.wait_ge(s_rows[s], (used(1, i, s) + 1) * (16 * C))
                dve.wait_ge(s_self[s], dmas(0, i + 1, s))
                m1 = done(V.tensor_reduce(lns[:, 0, 0:C, 0], g, AX.X, ALU.add))
                m2 = done(V.tensor_reduce(lns[:, 0, C:2 * C, 0], own, AX.X, ALU.add))
                done.wait(m1)
                V.scalar_tensor_tensor(lnc[:, 0, 0:C, :], bc(lns[:, 0, 0:C, :], [P, C, D]), -1.0 / D, g, ALU.mult, ALU.add)
                done.wait(m2)
                V.scalar_tensor_tensor(lnc[:, 0, C:2 * C, :], bc(lns[:, 0, C:2 * C, :], [P, C, D]), -1.0 / D,
                                       own, ALU.mult, ALU.add).then_inc(sl["xc1"], 1)

            def norm_second(i, s):
                t = 2 * i + s
                cols = bass.ds(t * C, C)
                v = rows[:, s, :, D]
                m = done(V.scalar_tensor_tensor(tmp[:, 0:C], v, 0.0, srcf[:, cols], ALU.is_equal, ALU.mult))
                dve.wait_ge(sl["sq1"], t + 1)
                V.tensor_reduce(lnv[:, 0, :, 0], lnq[:, 0, :, :], AX.X, ALU.add).then_inc(sl["var1"], 1)
                done.wait(m)
                m = done(V.scalar_tensor_tensor(tmp[:, 0:C], tmp[:, 0:C], -1.0, v, ALU.add, ALU.add))
                done.wait(m)
                V.tensor_copy(row_of_src[:, cols], tmp[:, 0:C]).then_inc(s_map_used, 1)

            def norm_third(i, s):
                t = 2 * i + s
                dve.wait_ge(sl["std1"], t + 1)
                m = done(V.reciprocal(lnr[:, 0, :, 0], lnd[:, 0, :, 0]))
                done.wait(m)
                m1 = done(V.scalar_tensor_tensor(lnr[:, 0, 0:C, 0], rows[:, s, :, D + 1], 1.0, lnr[:, 0, 0:C, 0],
                                                 ALU.add, ALU.mult))
                m2 = done(V.tensor_tensor(lnr[:, 0, C:2 * C, 0], dis[:, bass.ds(t * C, C)], lnr[:, 0, C:2 * C, 0], ALU.mult))
                done.wait(m1)
                V.scalar_tensor_tensor(g_in[:, :, 1:].rearrange("p f c -> p c f"), lnc[:, 0, 0:C, :], 0.0,
                                       bc(lnr[:, 0, 0:C, :], [P, C, D]), ALU.max, ALU.mult).then_inc(sl["used"], 1)
                done.wait(m2)
                m = done(V.scalar_tensor_tensor(h0[:, C:2 * C, :], lnc[:, 0, C:2 * C, :], 0.0,
                                                bc(lnr[:, 0, C:2 * C, :], [P, C, D]), ALU.max, ALU.mult))
                done.wait(m)
                dve.wait_ge(sl["used"], t + 1)

            def running_sum(i, s, last_chunk=False):
                t = 2 * i + s
                n = at_turn(L, t)
                dve.wait_ge(sl["tiled"], n + 1)
                if not (isinstance(n, int) and n == 0):
                    dve.wait_ge(sl["head"], n)
                V.tensor_tensor_scan(scan_sum, scan_cont, scan_g, 0.0, ALU.mult, ALU.add).then_inc(sl["chain"], 1)
                dve.wait_ge(sl["chain"], n + 1)
                if last_chunk:
                    V.tensor_copy(last[:], sums[:, :, C - 1]).then_inc(sl["last"], 1)
                    dve.wait_ge(sl["carry"], L + 1)
                    m = done(V.tensor_copy(sums[:, :, C], bank[6][:, 0:D]))
                    done.wait(m)
                else:
                    done(V.tensor_copy(g_in[:, :, 0], sums[:, :, C]))

            def layer_input(i, s):
                t = 2 * i + s
                n = at_turn(L, t)
                own = h0[:, C:2 * C, :] if L == 0 else selfr[:, s, :, 0:D]
                if L > 0:
                    dve.wait_ge(s_self[s], dmas(L, i + 1, s))
                if L > 0 or not (isinstance(t, int) and t == 0):
                    dve.wait_ge(sl["t_ps"], n)
                m = done(V.tensor_tensor(zbuf[:], sums[:, :, 1:].rearrange("p f c -> p c f"), own, ALU.add))
                done.wait(m)
                if L > 0:
                    dve.sem_inc(sl["used"], 1)
                db = dis[:, bass.ds(t * C, C)].rearrange("p (c k) -> p c k", k=1)
                V.tensor_tensor(zbuf[:], zbuf[:], bc(db, [P, C, D]), ALU.mult).then_inc(sl["z"], 1)

            def rows_first(i, s):
                t = 2 * i + s
                n = at_turn(L, t)
                back = bank[4][:].rearrange("p (c f) -> p c f", f=D)
                dve.wait_ge(sl["back"], n + 1)
                if L > 0 or not (isinstance(i, int) and i == 0):
                    dve.wait_ge(s_ust[s], dmas(L, i, s))
                if L < 2:
                    db = dis[:, bass.ds(t * C, C)].rearrange("p (c k) -> p c k", k=1)
                    V.tensor_tensor(o1[:, s, :, :], back, bc(db, [P, C, D]), ALU.mult).then_inc(sl["u"], 1)
                    return
                V.tensor_tensor(ox[:, s, :, :], back, xd[:, s, :, 0:D], ALU.add).then_inc(sl["u"], 1)
                dve.wait_ge(sl["u"], n + 1)
                m = done(V.tensor_reduce(lns[:, 1, 0:C, 0], ox[:, s, :, :], AX.X, ALU.add))
                done.wait(m)
                V.scalar_tensor_tensor(lnc[:, 1, 0:C, :], bc(lns[:, 1, 0:C, :], [P, C, D]), -1.0 / D,
                                       ox[:, s, :, :], ALU.mult, ALU.add).then_inc(sl["xc2"], 1)
                dve.wait_ge(sl["sq2"], t + 1)
                V.tensor_reduce(lnv[:, 1, 0:C, 0], lnq[:, 1, 0:C, :], AX.X, ALU.add).then_inc(sl["var2"], 1)

            def rows_second(i, s):
                t = 2 * i + s
                dve.wait_ge(sl["std2"], t + 1)
                m = done(V.reciprocal(lnr[:, 1, 0:C, 0], lnd[:, 1, 0:C, 0]))
                done.wait(m)
                V.scalar_tensor_tensor(o3[:, s, :, :], lnc[:, 1, 0:C, :], 0.0, bc(lnr[:, 1, 0:C, :], [P, C, D]),
                                       ALU.max, ALU.mult).then_inc(sl["o3"], 1)

            def turn(i, s, before=True, after=True):
                behind, ahead = (i + s - 1, 1 - s), (i + s, 1 - s)
                if L == 0:
                    if after:
                        norm_first(*ahead)
                    running_sum(i, s, last_chunk=not after)
                    layer_input(i, s)
                    if after:
                        norm_second(*ahead)
                    if before:
                        rows_first(*behind)
                    if after:
                        norm_third(*ahead)
                else:
                    running_sum(i, s, last_chunk=not after)
                    layer_input(i, s)
                    if L == 2 and not (isinstance(i, int) and i == 0):
                        rows_second(i - 1, s)
                    if before:
                        rows_first(*behind)

            base = layer_base[L]
            done.restart(base)
            if L == 0:
                V.memset(scan_cont, 0.0)
            m = done(V.memset(scan_g, 0.0))
            done.wait(m)
            dve.sem_inc(sl["ready"], 1)
            if L == 0:
                norm_first(0, 0)
                norm_second(0, 0)
                norm_third(0, 0)
            turn(0, 0, before=False)
            turn(0, 1)
            start = done.n
            done.restart(base + start)
            turn(1, 0)
            per = done.n
            turn(1, 1)
            with dve.Fori(2, NCH // 2) as i:
                for s in range(2):
                    done.restart(base + start + (2 * i + s - 2) * per)
                    turn(i, s)
                    assert done.n == per
            done.restart(base + start + (NCH - 3) * per)
            turn(NCH // 2, 0, after=False)
            if L == 2:
                rows_second(NCH // 2 - 1, 1)
            rows_first(NCH // 2, 0)
            if L == 2:
                rows_second(NCH // 2, 0)
            layer_base[L + 1] = done.base + done.n

        def prep_dve(dve):
            link = Steps(dve, s_prep)
            nc.vector.memset(wblk[:], 0.0).then_inc(s_pad, 1)
            nc.vector.memset(avblk[:], 0.0).then_inc(s_padv, 1)
            nc.vector.memset(ones[:], 1.0)
            nc.vector.memset(ex4[:], 0.0)
            nc.vector.memset(hdb[:], 0.0)
            nc.vector.memset(score[:], 0.0)
            nc.vector.memset(epsln[:], 1e-5)
            nc.vector.memset(head[:], 0.0)
            nc.vector.memset(slotdata[:], 0.0)
            link(nc.vector.memset(cont[:], 0.0))
            dve.wait_ge(s_in, 16 * (6 + 1))
            dve.wait_ge(s_const, 4)
            nc.vector.tensor_copy(dstf[:], dsti[:])
            nc.vector.tensor_copy(srcf[:], srci[:])
            nc.vector.tensor_copy(etf[:], eti[:])
            nc.vector.tensor_copy(identb[:], ident[:])
            link(nc.vector.tensor_copy(dnextf[:], dnext[:]))
            link(nc.vector.tensor_copy(dstf[:, EC:SC], dstf[:, 0:1]))
            link(nc.vector.tensor_scalar(tmp[:], dstf[:], float(N - 1), None, ALU.min))
            nc.vector.tensor_copy(idx_dst[:], tmp[:]).then_inc(s_idx, 1)
            dve.wait_ge(s_idx, 1)
            nc.vector.tensor_tensor(cont[:, 1:EC], dstf[:, 1:EC], dstf[:, 0:EC - 1], ALU.is_equal)
            nc.vector.tensor_tensor(ends[:, 0:EC - 1], dstf[:, 1:EC], dstf[:, 0:EC - 1], ALU.not_equal)
            link(nc.vector.tensor_tensor(ends[:, EC - 1:EC], dstf[:, EC - 1:EC], dnextf[:], ALU.not_equal))
            link(nc.vector.tensor_scalar(head[:, 0:EC], dstf[:, 0:EC], dstf[:, 0:1], None, ALU.is_equal))
            link(nc.vector.tensor_tensor(headend[:, 0:EC], head[:, 0:EC], ends[:, 0:EC], ALU.mult))
            link(nc.vector.tensor_tensor(owns[:, 0:EC], ends[:, 0:EC], headend[:, 0:EC], ALU.subtract))
            link(nc.vector.tensor_reduce(owns[:, EC:SC], headend[:, 0:EC], AX.X, ALU.max))
            nc.vector.memset(headend[:, EC:SC], 0.0)
            link(nc.vector.tensor_scalar(tmp[:, 0:EC], ends[:, 0:EC], -1.0, 1.0, ALU.mult, ALU.add))
            link(nc.vector.tensor_scalar(tmp2[:, 0:EC], head[:, 0:EC], -1.0, 1.0, ALU.mult, ALU.add))
            link(nc.vector.memset(goes[:], 0.0))
            link(nc.vector.tensor_tensor(goes[:, 0:EC], tmp[:, 0:EC], tmp2[:, 0:EC], ALU.mult))
            link(nc.vector.tensor_scalar(diag[:], ident[:], dstf[:, 0:1], None, ALU.mult))
            nc.vector.tensor_scalar(tmp2[:, 0:1], dstf[:, EC - 1:EC], 1.0, None, ALU.mult).then_inc(s_prepdiag, 1)
            dve.wait_ge(s_prepdiag, 1)
            dve.wait_ge(s_preppe, 1)
            link(nc.vector.tensor_scalar(carrym[:], bank[0][:, 0:P], dstf[:, EC - 1:EC], None, ALU.is_equal))
            link(nc.vector.tensor_tensor(carrym[:], carrym[:], below[:], ALU.mult))
            nc.vector.memset(tmp[:], 1.0).then_inc(s_prepdiag, 1)
            dve.wait_ge(s_prepdiag, 2)
            dve.wait_ge(s_preppe, 2)
            link(nc.vector.tensor_copy(carryt[:], bank[1][:, 0:P]))
            link(nc.vector.tensor_tensor_scan(cnt[:, 0:EC], cont[:, 0:EC], tmp[:, 0:EC], 0.0, ALU.mult, ALU.add))
            link(nc.vector.tensor_tensor(tmp2[:, 0:EC], headend[:, 0:EC], cnt[:, 0:EC], ALU.mult))
            link(nc.vector.tensor_reduce(cnt[:, EC:SC], tmp2[:, 0:EC], AX.X, ALU.add))
            nc.vector.tensor_scalar(tmp2[:, 0:1], cnt[:, EC - 1:EC], 1.0, None, ALU.mult).then_inc(s_prepdiag, 1)
            dve.wait_ge(s_prepdiag, 3)
            dve.wait_ge(s_preppe, 3)
            link(nc.vector.tensor_tensor(cnt[:, EC:SC], cnt[:, EC:SC], bank[0][:, P:P + 1], ALU.add))
            nc.vector.tensor_scalar(tmp[:], cnt[:], 1.0, None, ALU.add).then_inc(s_prepdiag, 1)
            dve.wait_ge(s_prepact, 1)
            link(nc.vector.reciprocal(dis[:], tmp2[:]))
            nc.vector.tensor_copy(slotdata[:, :, 0], slotno[:])
            link(nc.vector.tensor_scalar(slotdata[:, :, 1], dis[:], -1.0, None, ALU.add))
            link(nc.vector.tensor_scalar(tmp[:], dstf[:], float(XW // 4), float(D // 4) - OUTSIDE, ALU.mult, ALU.add))
            link(nc.vector.tensor_tensor(tmp[:], tmp[:], owns[:], ALU.mult))
            link(nc.vector.tensor_scalar(idx_map[:], tmp[:], OUTSIDE, None, ALU.add))
            link(nc.vector.scalar_tensor_tensor(tmp[:], dstf[:], -OUTSIDE, owns[:], ALU.add, ALU.mult))
            nc.vector.tensor_scalar(idx_out[:], tmp[:], OUTSIDE, None, ALU.add).then_inc(s_idx, 1)
            for r in range(R):
                nc.vector.tensor_scalar(onehot[:, :, r], etf[:], float(r), None, ALU.is_equal)
            link(nc.vector.tensor_scalar(srcf[:], srcf[:], float(SLOTS + 1), None, ALU.add))

        @block.vector
        def _(dve):
            prep_dve(dve)
            link = Steps(dve, sems_dense["step"])
            sd = sems_dense

            def half(buf, a):
                return buf[:, C * a:C * a + C, :]

            def from_bank(n):
                return bank[n][:].rearrange("p (c f) -> p c f", f=D)

            def normalised_in(i, u):
                xk = dense_x[u][:, :, 0:D]
                dve.wait_ge(s_xd[u], (i // 3 + 1 if isinstance(i, int) else j_of(i, u)) * 16)
                link(nc.vector.tensor_reduce(lns[:, 0, :, 0], xk, AX.X, ALU.add))
                nc.vector.scalar_tensor_tensor(lnc[:, 0, :, :], bc(lns[:, 0, :, :], [P, DC, D]), -1.0 / D, xk,
                                               ALU.mult, ALU.add).then_inc(sd["xc1"], 1)

            def variance_in(i):
                dve.wait_ge(sd["sq1"], i + 1)
                nc.vector.tensor_reduce(lnv[:, 0, :, 0], lnq[:, 0, :, :], AX.X, ALU.add).then_inc(sd["var1"], 1)

            def hidden_in(i):
                dve.wait_ge(sd["std1"], i + 1)
                link(nc.vector.reciprocal(lnr[:, 0, :, 0], lnd[:, 0, :, 0]))
                if not (isinstance(i, int) and i == 0):
                    dve.wait_ge(sd["z"], 8 * i - 6)
                nc.vector.scalar_tensor_tensor(h0[:], lnc[:, 0, :, :], 0.0, bc(lnr[:, 0, :, :], [P, DC, D]),
                                               ALU.max, ALU.mult).then_inc(sd["h0"], 1)

            loads = [0]

            def j_of(i, u):
                return loads[0] + 1

            def turn(i, u, before=True, here=True, after=True):
                if before:
                    if not (isinstance(i, int) and i < 2):
                        dve.wait_ge(s_dst3, (i - 1) * 32)
                    for a in range(2):
                        dve.wait_ge(sd["b3"], 2 * i - 1 + a)
                        nc.vector.tensor_tensor(half(dx, a), from_bank(6 + a), half(dense_x[(u + 2) % 3], a)[:, :, 0:D],
                                                ALU.add).then_inc(sd["x1"], 1)
                    dve.wait_ge(sd["x1"], 2 * i)
                    link(nc.vector.tensor_reduce(lns[:, 1, :, 0], dx, AX.X, ALU.add))
                    nc.vector.scalar_tensor_tensor(lnc[:, 1, :, :], bc(lns[:, 1, :, :], [P, DC, D]), -1.0 / D, dx,
                                                   ALU.mult, ALU.add).then_inc(sd["xc2"], 1)
                if after:
                    normalised_in(i + 1, (u + 1) % 3)
                if before:
                    dve.wait_ge(sd["sq2"], i)
                    nc.vector.tensor_reduce(lnv[:, 1, :, 0], lnq[:, 1, :, :], AX.X, ALU.add).then_inc(sd["var2"], 1)
                if after:
                    variance_in(i + 1)
                if here:
                    if not (isinstance(i, int) and i == 0):
                        dve.wait_ge(s_dst1, i * 16)
                    for a in range(2):
                        dve.wait_ge(sd["b1"], 2 * i + a + 1)
                        nc.vector.tensor_copy(half(d1, a), from_bank(2 + a)).then_inc(sd["o1"], 1)
                if before:
                    dve.wait_ge(sd["std2"], i)
                    link(nc.vector.reciprocal(lnr[:, 1, :, 0], lnd[:, 1, :, 0]))
                    nc.vector.scalar_tensor_tensor(d3, lnc[:, 1, :, :], 0.0, bc(lnr[:, 1, :, :], [P, DC, D]),
                                                   ALU.max, ALU.mult).then_inc(sd["o3"], 1)
                if after:
                    hidden_in(i + 1)

            dve.wait_ge(s_weights, 16 * (2 + R + 12))
            link.restart(0)
            normalised_in(0, 0)
            variance_in(0)
            hidden_in(0)
            turn(0, 0, before=False)
            start = link.n
            turn(1, 1)
            per = link.n - start
            turn(2, 2)
            with dve.Fori(1, ND // 3) as j:
                for u in range(3):
                    link.restart(start + (3 * j + u - 1) * per)
                    loads[0] = j + (u + 1) // 3
                    turn(3 * j + u, u)
                    assert link.n == per
            link.restart(start + (ND - 2) * per)
            turn(ND - 1, (ND - 1) % 3, after=False)
            turn(ND, ND % 3, here=False, after=False)
            dense_stored(dve)
            for L in range(3):
                layer_dve(dve, L)
            score_dve(dve)
            message_dve(dve)

        @block.scalar
        def _(act):
            act.wait_ge(s_prepdiag, 4)
            nc.scalar.activation(tmp2[:], tmp[:], ACT.Sqrt).then_inc(s_prepact, 1)
            sd = sems_dense

            def load(i, u):
                pp = LASTP if isinstance(i, int) and i == ND - 1 else P
                act.dma_start(dense_x[u][0:pp, :, :], dense_at(x, 0, i)).then_inc(s_xd[u], 16)

            def hidden(i, m):
                l, a = m // 2, m % 2
                act.wait_ge(sd["z"], 8 * i + m + 1)
                if l == 0:
                    nc.scalar.copy(hT[:, 2 * a, :], bank[a][:]).then_inc(sd["hT"], 1)
                else:
                    nc.scalar.activation(hT[:, 2 * a + l % 2, :], bank[a][:], ACT.Relu, bias=bcol[:, l - 1:l]) \
                        .then_inc(sd["hT"], 1)

            def squares_of(i, n):
                act.wait_ge(sd[f"xc{n + 1}"], i + 1)
                nc.scalar.activation(lnq[:, n, :, :], lnc[:, n, :, :], ACT.Square).then_inc(sd[f"sq{n + 1}"], 1)

            def deviation_of(i, n):
                act.wait_ge(sd[f"var{n + 1}"], i + 1)
                nc.scalar.activation(lnd[:, n, :, 0], lnv[:, n, :, 0], ACT.Sqrt, bias=epsln[:], scale=1.0 / D) \
                    .then_inc(sd[f"std{n + 1}"], 1)

            def rows2(i, a):
                act.wait_ge(sd["b2"], 2 * i + a + 1)
                if a == 0 and not (isinstance(i, int) and i == 0):
                    act.wait_ge(s_dst2, 16 * i)
                nc.scalar.copy(d2[:, C * a:C * a + C, :], bank[4 + a][:].rearrange("p (c f) -> p c f", f=D)) \
                    .then_inc(sd["o2"], 1)

            def store(i, rows_, tgt, base, done):
                pp = LASTP if isinstance(i, int) and i == ND - 1 else P
                act.dma_start(dense_at(tgt, base, i), rows_[0:pp, :, :]).then_inc(done, 16)

            def turn(i, u, before=True, here=True, after=True, loads=True):
                if here:
                    for m in range(4):
                        hidden(i, m)
                if before:
                    squares_of(i - 1, 1)
                    store(i - 1, dx, out, 0, s_dst3)
                if loads:
                    load(i + 2, (u + 2) % 3)
                if here:
                    hidden(i, 4)
                if after:
                    squares_of(i + 1, 0)
                if before:
                    deviation_of(i - 1, 1)
                if here:
                    hidden(i, 5)
                if after:
                    deviation_of(i + 1, 0)
                if here:
                    act.wait_ge(sd["o1"], 2 * i + 2)
                    store(i, d1, table[1], SLOTS, s_dst1)
                    hidden(i, 6)
                    rows2(i, 0)
                    hidden(i, 7)
                    rows2(i, 1)
                if before:
                    act.wait_ge(sd["o3"], i)
                    store(i - 1, d3, table[3], SLOTS, s_dst3)
                if here:
                    act.wait_ge(sd["o2"], 2 * i + 2)
                    store(i, d2, table[2], SLOTS, s_dst2)

            load(0, 0)
            load(1, 1)
            squares_of(0, 0)
            deviation_of(0, 0)
            turn(0, 0, before=False)
            turn(1, 1)
            turn(2, 2)
            with act.Fori(1, ND // 3 - 1) as j:
                for u in range(3):
                    turn(3 * j + u, u)
            for i in range(3 * (ND // 3 - 1), ND):
                turn(i, i % 3, after=i < ND - 1, loads=i + 2 < ND)
            turn(ND, ND % 3, here=False, after=False, loads=False)

            sl = sems_layer
            for L in range(3):
                def operands(i, s):
                    t = 2 * i + s
                    n = at_turn(L, t)
                    if isinstance(t, int) and t == 0:
                        act.wait_ge(sl["ready"], L + 1)
                    else:
                        act.wait_ge(sl["chain"], n)
                    flags = cont[:, bass.ds(t * C, C)].rearrange("p (k c) -> p k c", k=1).broadcast_to([P, D, C])
                    ins = nc.scalar.copy(cont_in[:, :, 1:], flags)
                    if L > 0:
                        act.wait_ge(s_rows[s], (used(1 + L, i, s) + 1) * (16 * C))
                        ins = nc.scalar.copy(g_in[:, :, 1:].rearrange("p f c -> p c f"), rows[:, s, :, 0:D])
                    ins.then_inc(sl["tiled"], 1)

                def head_part(t):
                    n = at_turn(L, t)
                    act.wait_ge(sl["chain"], n + 1)
                    if not (isinstance(n, int) and n == 0):
                        act.wait_ge(sl["head_added"], n)
                    for c in range(C):
                        ins = nc.scalar.activation(agghead[:, c, :], sums[:, :, 1 + c], ACT.Copy,
                                                   scale=headend[:, bass.ds(t * C + c, 1)])
                    ins.then_inc(sl["head"], 1)

                def through_layer(t, between=None):
                    n = at_turn(L, t)
                    act.wait_ge(sl["t_ps"], n + 1)
                    nc.scalar.copy(hT[:, 0, :], bank[0][:]).then_inc(sl["t"], 1)
                    if between:
                        between()
                    act.wait_ge(sl["mm"], n + 1)
                    nc.scalar.activation(hT[:, 1, :], bank[1][:], ACT.Relu, bias=bcol[:, L:L + 1]).then_inc(sl["relu"], 1)

                def squares_of(t, which):
                    act.wait_ge(sl[f"xc{which + 1}"], t + 1)
                    m = C if which else 2 * C
                    nc.scalar.activation(lnq[:, which, 0:m, :], lnc[:, which, 0:m, :], ACT.Square) \
                        .then_inc(sl[f"sq{which + 1}"], 1)

                def deviation_of(t, which):
                    act.wait_ge(sl[f"var{which + 1}"], t + 1)
                    m = C if which else 2 * C
                    nc.scalar.activation(lnd[:, which, 0:m, 0], lnv[:, which, 0:m, 0], ACT.Sqrt, bias=epsln[:],
                                         scale=1.0 / D).then_inc(sl[f"std{which + 1}"], 1)

                def layer_turn(i, s, before=True, after=True):
                    t = 2 * i + s
                    operands(i, s)
                    if L == 0 and after:
                        squares_of(t + 1, 0)
                    head_part(t)
                    between = None
                    if L == 0 and after:
                        between = lambda: deviation_of(t + 1, 0)
                    if L == 2 and before:
                        between = lambda: squares_of(t - 1, 1)
                    through_layer(t, between)
                    if L == 2 and before:
                        deviation_of(t - 1, 1)

                if L == 0:
                    squares_of(0, 0)
                    deviation_of(0, 0)
                layer_turn(0, 0, before=False)
                layer_turn(0, 1)
                with act.Fori(1, NCH // 2) as i:
                    layer_turn(i, 0)
                    layer_turn(i, 1)
                layer_turn(NCH // 2, 0, after=False)
                if L == 2:
                    squares_of(NCH - 1, 1)
                    deviation_of(NCH - 1, 1)

            score_act(act)
            message_act(act)

        @block.tensor
        def _(pe):
            pe.wait_ge(s_prepdiag, 1)
            nc.tensor.matmul(bank[0][:, 0:P], ones[:], diag[:], start=True, stop=True).then_inc(s_preppe, 1)
            pe.wait_ge(s_prepdiag, 2)
            nc.tensor.transpose(bank[1][:, 0:P], carrym[:], ident[:]).then_inc(s_preppe, 1)
            pe.wait_ge(s_prepdiag, 3)
            nc.tensor.matmul(bank[0][:, P:P + 1], carrym[:], tmp2[:, 0:1], start=True, stop=True).then_inc(s_preppe, 1)
            sd = sems_dense

            def transposes(bank_, source):
                for q in range(4):
                    ins = nc.tensor.transpose(bank_[:, q * P:(q + 1) * P], source(q), ident[:])
                return ins

            def dense_layers(i, first=False):
                pe.wait_ge(sd["h0"], i + 1)
                if first:
                    pe.wait_ge(s_prepdiag, 4)
                    pe.wait_ge(s_prepact, 1)
                for a in range(2):
                    transposes(bank[a], lambda q: h0[:, C * a + 2 * q:C * a + 2 * q + 2, :].rearrange("p c f -> p (c f)")) \
                        .then_inc(sd["z"], 1)
                for l in range(4):
                    for a in range(2):
                        now = hT[:, 2 * a + l % 2, :]
                        pe.wait_ge(sd["hT"], 8 * i + 2 * l + a + 1)
                        if l < 3:
                            nc.tensor.matmul(bank[a][:], wblk[:, l, :], now, start=True, stop=True).then_inc(sd["z"], 1)
                        if l > 0:
                            if not first:
                                pe.wait_ge(sd[("o1", "o2", "x1")[l - 1]], 2 * i - 1 + a)
                            transposes(bank[2 * l + a], lambda q: now[:, q * P:(q + 1) * P]).then_inc(sd[f"b{l}"], 1)

            dense_layers(0, first=True)
            with pe.Fori(1, ND) as i:
                dense_layers(i)

            sl = sems_layer
            for L in range(3):
                def layer_b(t, first_chunk=False, last_chunk=False):
                    n = at_turn(L, t)

                    def add_heads():
                        pe.wait_ge(sl["head"], n + 1)
                        for c in range(C):
                            ins = nc.tensor.matmul(bank[6][:, 0:D], ident[:], agghead[:, c, :],
                                                   start=first_chunk and c == 0, stop=False)
                        ins.then_inc(sl["head_added"], 1)

                    if last_chunk:
                        add_heads()
                        pe.wait_ge(sl["last"], L + 1)
                        nc.tensor.matmul(bank[6][:, 0:D], carrym[:], last[:], start=False, stop=True) \
                            .then_inc(sl["carry"], 1)
                    pe.wait_ge(sl["z"], n + 1)
                    transposes(bank[0], lambda q: zbuf[:, 2 * q:2 * q + 2, :].rearrange("p c f -> p (c f)")) \
                        .then_inc(sl["t_ps"], 1)
                    pe.wait_ge(sl["t"], n + 1)
                    nc.tensor.matmul(bank[1][:], wblk[:, L, :], hT[:, 0, :], start=True, stop=True).then_inc(sl["mm"], 1)
                    if not last_chunk:
                        add_heads()
                    pe.wait_ge(sl["relu"], n + 1)
                    if not (isinstance(n, int) and n == 0):
                        pe.wait_ge(sl["u"], n)
                    transposes(bank[4], lambda q: hT[:, 1, q * P:(q + 1) * P]).then_inc(sl["back"], 1)

                layer_b(0, first_chunk=True)
                with pe.Fori(1, NCH - 1) as t:
                    layer_b(t)
                layer_b(NCH - 1, last_chunk=True)
            score_pe(pe)
            message_pe(pe)


def kernel(x, src, dst, edge_type_8, L0_gnn_W0, L0_gnn_b0, L0_gnn_W1, L0_gnn_b1, L0_gnn_W2, L0_gnn_b2,
           L1_gnn_rel_weight, L1_gnn_attn_vec, L1_gnn_rel_emb):
    import concourse.bacc as bacc
    from concourse.bass_utils import run_bass_kernel_spmd

    nc = bacc.Bacc("TRN2", target_bir_lowering=False, num_devices=1)
    arrays, aps = {}, {}

    def given(name, a):
        a = np.ascontiguousarray(a)
        arrays[name] = a
        aps[name] = nc.dram_tensor(name, a.shape, mybir.dt.from_np(a.dtype), kind="ExternalInput").ap()
        return aps[name]

    padded = np.zeros((N, XW), np.float32)
    padded[:, :D] = x
    args = [given("x_in", padded), given("src_in", src), given("dst_in", dst), given("etype_in", edge_type_8),
            [given("w0", L0_gnn_W0), given("w1", L0_gnn_W1), given("w2", L0_gnn_W2)],
            [given("b0", L0_gnn_b0), given("b1", L0_gnn_b1), given("b2", L0_gnn_b2)],
            given("rel_weight", L1_gnn_rel_weight), given("attn_vec", L1_gnn_attn_vec)]
    out = nc.dram_tensor("out", (N, D), F32, kind="ExternalOutput").ap()
    build(nc, *args, out)
    got = run_bass_kernel_spmd(nc, [arrays], core_ids=[0])
    return got.results[0]["out"]
```
